# Optimizing a Trainium2 kernel written in Bass

```python
import numpy as np
import jax
import jax.numpy as jnp

def _softmax(x, axis=-1):
    return jax.nn.softmax(x, axis=axis)

def _gelu(x):
    return jax.nn.gelu(x, approximate=True)

def _silu(x):
    return jax.nn.silu(x)

def _sigmoid(x):
    return jax.nn.sigmoid(x)

def _layernorm(x, axis=-1, eps=1e-05):
    m = jnp.mean(x, axis=axis, keepdims=True)
    v = jnp.var(x, axis=axis, keepdims=True)
    return (x - m) / jnp.sqrt(v + eps)

def _scatter_add(tgt, idx, src, axis=0):
    return tgt.at[idx].add(src)

def _segment_sum(src, seg, n):
    return jax.ops.segment_sum(src, seg, n)
kernel_name = 'mk_vit_tower_postln_d1_tok_img256_r4_e53fb5'

def setup_inputs(seed: int=0):
    np.random.seed(seed)
    _w = jnp.asarray

    def _rec_inputs():
        import jax
        import jax.numpy as jnp
        _rk = jax.random.key(seed)
        x = -0.000202321 + 1.00025 * jax.random.normal(jax.random.fold_in(_rk, 1), (4, 64, 56, 56), jnp.float32)
        return x
    x = _rec_inputs()

    def _L0_tok_setup():
        import jax, jax.numpy as jnp
        import numpy as np
        B, C, H, W = (8, 64, 56, 56)
        K = 3

        def _unfold3x3(x):
            b, c, h, w = x.shape
            xp = jnp.pad(x, ((0, 0), (0, 0), (1, 1), (1, 1)))
            patches = jnp.stack([xp[:, :, i:i + h, j:j + w] for i in range(K) for j in range(K)], axis=2)
            return patches.reshape(b, c * K * K, h * w).transpose(0, 2, 1)
        key = jax.random.key(seed)
        ks = jax.random.split(key, 8)
        d = C * K * K
        s1 = 1.0 / np.sqrt(d)
        s2 = 1.0 / np.sqrt(C)
        return {'x': jax.random.normal(ks[0], (B, C, H, W), jnp.float32), 'W1': jax.random.uniform(ks[1], (d, C), jnp.float32, -s1, s1), 'b1': jax.random.uniform(ks[2], (C,), jnp.float32, -s1, s1), 'W2': jax.random.uniform(ks[3], (C, d), jnp.float32, -s2, s2), 'b2': jax.random.uniform(ks[4], (d,), jnp.float32, -s2, s2), 'W3': jax.random.uniform(ks[5], (d, C), jnp.float32, -s1, s1), 'b3': jax.random.uniform(ks[6], (C,), jnp.float32, -s1, s1)}
    _L0_tok_all = _L0_tok_setup()
    _L0_tok_in = {k: v for k, v in _L0_tok_all.items() if k in ('W1', 'b1', 'W2', 'b2', 'W3', 'b3')}
    del _L0_tok_all

    def _L0_attn_setup():
        import jax, jax.numpy as jnp
        import numpy as np
        H = 8
        key = jax.random.key(seed)
        ks = jax.random.split(key, 10)
        B, N, D, E = (1, 1024, 64, 16384)
        s = 0.02
        return {'x': jax.random.normal(ks[0], (B, N, D), jnp.float32), 'edge_index': jax.random.randint(ks[1], (2, E), 0, N, jnp.int32), 'edge_attr': jax.random.normal(ks[2], (E, 3), jnp.float32), 'Wq': jax.random.normal(ks[3], (D, D), jnp.float32) * s, 'bq': jnp.zeros((D,), jnp.float32), 'Wk': jax.random.normal(ks[4], (D, D), jnp.float32) * s, 'bk': jnp.zeros((D,), jnp.float32), 'Wv': jax.random.normal(ks[5], (D, D), jnp.float32) * s, 'bv': jnp.zeros((D,), jnp.float32), 'Wo': jax.random.normal(ks[6], (D, D), jnp.float32) * s, 'bo': jnp.zeros((D,), jnp.float32), 'We': jax.random.normal(ks[7], (3, H), jnp.float32) * s, 'be': jnp.zeros((H,), jnp.float32)}
    _L0_attn_all = _L0_attn_setup()
    _L0_attn_in = {k: v for k, v in _L0_attn_all.items() if k in ('edge_index', 'edge_attr', 'Wq', 'bq', 'Wk', 'bk', 'Wv', 'bv', 'Wo', 'bo', 'We', 'be')}
    del _L0_attn_all

    def _L0_ffn_setup():
        import jax, jax.numpy as jnp
        import numpy as np
        B, S, H, F, E, K = (8, 1024, 64, 128, 16, 2)
        EPS = 1e-05
        key = jax.random.key(seed)
        ks = jax.random.split(key, 9)
        sc = 0.02
        return {'x': jax.random.normal(ks[0], (B, S, H), dtype=jnp.float32), 'gate_w': jax.random.normal(ks[1], (H, E), dtype=jnp.float32) * sc, 'gate_b': jnp.zeros((E,), dtype=jnp.float32), 'w1': jax.random.normal(ks[2], (E, H, F), dtype=jnp.float32) * sc, 'b1': jnp.zeros((E, F), dtype=jnp.float32), 'w2': jax.random.normal(ks[3], (E, F, H), dtype=jnp.float32) * sc, 'b2': jnp.zeros((E, H), dtype=jnp.float32), 'gamma': jnp.ones((H,), dtype=jnp.float32), 'beta': jnp.zeros((H,), dtype=jnp.float32)}
    _L0_ffn_all = _L0_ffn_setup()
    _L0_ffn_in = {k: v for k, v in _L0_ffn_all.items() if k in ('gate_w', 'gate_b', 'w1', 'b1', 'w2', 'b2', 'gamma', 'beta')}
    del _L0_ffn_all
    return {'x': x, 'L0_tok_W1': _L0_tok_in['W1'], 'L0_tok_b1': _L0_tok_in['b1'], 'L0_tok_W2': _L0_tok_in['W2'], 'L0_tok_b2': _L0_tok_in['b2'], 'L0_tok_W3': _L0_tok_in['W3'], 'L0_tok_b3': _L0_tok_in['b3'], 'L0_attn_edge_index': _L0_attn_in['edge_index'], 'L0_attn_edge_attr': _L0_attn_in['edge_attr'], 'L0_attn_Wq': _L0_attn_in['Wq'], 'L0_attn_bq': _L0_attn_in['bq'], 'L0_attn_Wk': _L0_attn_in['Wk'], 'L0_attn_bk': _L0_attn_in['bk'], 'L0_attn_Wv': _L0_attn_in['Wv'], 'L0_attn_bv': _L0_attn_in['bv'], 'L0_attn_Wo': _L0_attn_in['Wo'], 'L0_attn_bo': _L0_attn_in['bo'], 'L0_attn_We': _L0_attn_in['We'], 'L0_attn_be': _L0_attn_in['be'], 'L0_ffn_gate_w': _L0_ffn_in['gate_w'], 'L0_ffn_gate_b': _L0_ffn_in['gate_b'], 'L0_ffn_w1': _L0_ffn_in['w1'], 'L0_ffn_b1': _L0_ffn_in['b1'], 'L0_ffn_w2': _L0_ffn_in['w2'], 'L0_ffn_b2': _L0_ffn_in['b2'], 'L0_ffn_gamma': _L0_ffn_in['gamma'], 'L0_ffn_beta': _L0_ffn_in['beta']}

def reference(x, L0_tok_W1, L0_tok_b1, L0_tok_W2, L0_tok_b2, L0_tok_W3, L0_tok_b3, L0_attn_edge_index, L0_attn_edge_attr, L0_attn_Wq, L0_attn_bq, L0_attn_Wk, L0_attn_bk, L0_attn_Wv, L0_attn_bv, L0_attn_Wo, L0_attn_bo, L0_attn_We, L0_attn_be, L0_ffn_gate_w, L0_ffn_gate_b, L0_ffn_w1, L0_ffn_b1, L0_ffn_w2, L0_ffn_b2, L0_ffn_gamma, L0_ffn_beta):
    import jax
    import jax.numpy as jnp

    def _L0_tok_ref(x, W1, b1, W2, b2, W3, b3):
        import jax, jax.numpy as jnp
        import numpy as np
        B, C, H, W = (8, 64, 56, 56)
        K = 3

        def _unfold3x3(x):
            b, c, h, w = x.shape
            xp = jnp.pad(x, ((0, 0), (0, 0), (1, 1), (1, 1)))
            patches = jnp.stack([xp[:, :, i:i + h, j:j + w] for i in range(K) for j in range(K)], axis=2)
            return patches.reshape(b, c * K * K, h * w).transpose(0, 2, 1)
        t = _unfold3x3(x)
        h1 = jax.nn.relu(jnp.einsum('bld,dc->blc', t, W1) + b1)
        s = jax.nn.sigmoid(jnp.einsum('blc,cd->bld', h1, W2) + b2)
        out = jnp.einsum('bld,dc->blc', t * s, W3) + b3
        return out

    def _L0_attn_ref(x, edge_index, edge_attr, Wq, bq, Wk, bk, Wv, bv, Wo, bo, We, be):
        import jax, jax.numpy as jnp
        import numpy as np
        H = 8
        B, N, D = x.shape
        hd = D // H
        q = (x @ Wq + bq).reshape(B, N, H, hd)
        k = (x @ Wk + bk).reshape(B, N, H, hd)
        v = (x @ Wv + bv).reshape(B, N, H, hd)
        scores = jnp.einsum('bihd,bjhd->bhij', q, k) / jnp.sqrt(jnp.asarray(hd, x.dtype))
        eb = edge_attr @ We + be
        edge_tgt = edge_index[1]
        col_bias = jnp.zeros((H, N), x.dtype).at[:, edge_tgt].set(eb.T)
        scores = scores + col_bias[None, :, None, :]
        attn = jax.nn.softmax(scores, axis=-1)
        out = jnp.einsum('bhij,bjhd->bihd', attn, v).reshape(B, N, D)
        return out @ Wo + bo

    def _L0_ffn_ref(x, gate_w, gate_b, w1, b1, w2, b2, gamma, beta):
        import jax, jax.numpy as jnp
        import numpy as np
        B, S, H, F, E, K = (8, 1024, 64, 128, 16, 2)
        EPS = 1e-05
        gate_logits = x @ gate_w + gate_b
        topk_vals, topk_idx = jax.lax.top_k(gate_logits, K)
        topk_w = jax.nn.softmax(topk_vals, axis=-1)
        h = jax.nn.relu(jnp.einsum('bsh,ehf->bsef', x, w1) + b1)
        expert_out = jnp.einsum('bsef,efh->bseh', h, w2) + b2
        sel = jnp.take_along_axis(expert_out, topk_idx[:, :, :, None], axis=2)
        moe = jnp.sum(topk_w[..., None] * sel, axis=2)
        y = x + moe
        mu = jnp.mean(y, axis=-1, keepdims=True)
        var = jnp.var(y, axis=-1, keepdims=True)
        return (y - mu) / jnp.sqrt(var + EPS) * gamma + beta
    h = _L0_tok_ref(x, L0_tok_W1, L0_tok_b1, L0_tok_W2, L0_tok_b2, L0_tok_W3, L0_tok_b3)
    h = _layernorm(h + _L0_attn_ref(h, L0_attn_edge_index, L0_attn_edge_attr, L0_attn_Wq, L0_attn_bq, L0_attn_Wk, L0_attn_bk, L0_attn_Wv, L0_attn_bv, L0_attn_Wo, L0_attn_bo, L0_attn_We, L0_attn_be), axis=-1)
    h = _layernorm(h + _L0_ffn_ref(h, L0_ffn_gate_w, L0_ffn_gate_b, L0_ffn_w1, L0_ffn_b1, L0_ffn_w2, L0_ffn_b2, L0_ffn_gamma, L0_ffn_beta), axis=-1)
    return h

_drawn_inputs = setup_inputs


def setup_inputs(seed=0):
    import zlib

    import numpy as np

    out = dict(_drawn_inputs(seed))
    spreads = {'L0_attn_bq': (0.0, 0.8),
     'L0_attn_bk': (0.0, 2.0),
     'L0_attn_bv': (0.0, 0.1),
     'L0_attn_bo': (0.0, 0.1),
     'L0_attn_be': (0.0, 2.0),
     'L0_ffn_gate_b': (0.0, 0.1),
     'L0_ffn_b1': (0.0, 0.8),
     'L0_ffn_b2': (0.0, 0.28),
     'L0_ffn_gamma': (1.0, 0.2),
     'L0_ffn_beta': (0.0, 0.1)}
    factors = {'L0_tok_b1': 8.0,
     'L0_attn_edge_attr': 8.0,
     'L0_attn_Wq': 21.641,
     'L0_attn_Wk': 8.0,
     'L0_attn_Wv': 8.0,
     'L0_attn_We': 8.0,
     'L0_ffn_w1': 7.246,
     'L0_ffn_w2': 5.371}
    for name, (base, spread) in spreads.items():
        noise = np.random.default_rng([zlib.crc32(name.encode()), seed]).standard_normal(out[name].shape)
        drawn = base * np.exp(spread * noise) if base else spread * noise
        out[name] = jnp.asarray(drawn.astype(out[name].dtype))
    for name, factor in factors.items():
        out[name] = (out[name] * factor).astype(out[name].dtype)
    return out
```

```python
from contextlib import ExitStack

import numpy as np

import concourse.bass as bass
from concourse import mybir

ALU = mybir.AluOpType
ACT = mybir.ActivationFunctionType
AX = mybir.AxisListType
F32 = mybir.dt.float32
BF16 = mybir.dt.bfloat16
I32 = mybir.dt.int32
U32 = mybir.dt.uint32

B, C, HW, K = 4, 64, 56, 3
N = HW * HW
PADW = HW + 2
H, HD = 8, 8
E_EDGES = 16384
EXP, FF = 16, 128
P = 128

CH = 8 * HW
NCH = N // CH
TM = CH // 4
NT = N // TM
KT = -(-N // P)
NP = KT * P
TAIL = N - (KT - 1) * P
TPC = N - TAIL

TAPS_LO = [0, 1, 2, 6, 8]
TAPS_HI = [3, 4, 5, 7]
NSLOT = len(TAPS_LO)

BIAS_ROW = 9 * HD
SHIFT_ROW = BIAS_ROW + 3
GROUPS = 4
SCORE_LIMIT = 56.0
EPS = 1e-5
KEY_BASE = 63 * P


class Steps:

    def __init__(self, eng, sem):
        self.eng, self.sem, self.base, self.n = eng, sem, 0, 0

    def loop(self, base):
        self.base, self.n = base, 0

    def __call__(self, ins):
        self.n += 1
        ins.then_inc(self.sem, 1)
        self.eng.wait_ge(self.sem, self.base + self.n)


class Core:

    def __init__(self, nc, io, out, ctx):
        self.nc, self.io, self.out, self.ctx = nc, io, out, ctx

        def keep(name, shape, dt):
            return ctx.enter_context(nc.sbuf_tensor(name, shape, dt))

        def scratch(name, shape, dt):
            return nc.dram_tensor(name, shape, dt, kind="Internal").ap()

        self.w1 = keep("tok_w1", [P, NSLOT, C], F32)
        self.w2 = keep("tok_w2", [C, NSLOT, P], F32)
        self.w3 = keep("tok_w3", [P, NSLOT, C], F32)
        self.b1 = keep("tok_b1", [C, 1], F32)
        self.b2 = keep("tok_b2_half", [P, NSLOT], F32)
        self.b3 = keep("tok_b3", [C, 1], F32)
        self.wqk = keep("attn_wqk", [C, 2 * C], F32)
        self.bqk = keep("attn_bqk", [2 * C, 1], F32)
        self.wv = keep("attn_wv_bv", [C + 1, C], F32)
        self.eye_bo = keep("eye_bo", [C + 1, C], F32)
        self.wo = keep("attn_wo", [P, C], F32)
        self.ident = keep("ident", [P, P], F32)
        self.ident_bf = keep("ident_bf", [P, P], BF16)
        self.x_tm = keep("x_token_major", [TM, B * NT, C], F32)
        self.values = keep("values", [P, B * H, KT, HD + 1], F32)
        self.flag = keep("need_maximum", [1, 1], I32)
        self.d_qk = scratch("qk_parts", [3, 2, B * C, N], BF16)
        self.d_bias = scratch("bias_parts", [B * H, 3, NP], BF16)
        self.d_shift = scratch("shift_parts", [B * H, 3, NP], BF16)
        self.d_recip = scratch("denominator_recips", [B * H, N], F32)
        self.d_mix = scratch("mixed", [B * H, GROUPS, HD + 1, N], F32)


def setup_phase(k):
    nc, io = k.nc, k.io
    with ExitStack() as ctx:
        def sb(name, shape, dt):
            return ctx.enter_context(nc.sbuf_tensor(name, shape, dt))

        def sem(name):
            return ctx.enter_context(nc.semaphore(name))

        EC = E_EDGES // P
        PER = 10
        NB = -(-EC // PER)
        W = KT * 2
        w2raw = sb("w2_raw", [C, K * K * C], F32)
        b2raw = sb("b2_raw", [P, K * K], F32)
        tgt = sb("edge_target", [P, EC], I32)
        tlo = sb("target_lo", [P, EC], I32)
        thi = sb("target_hi", [P, EC], I32)
        tlof = sb("target_lo_f", [P, EC], F32)
        thif = sb("target_hi_f", [P, EC], F32)
        index = sb("index_row", [P, P], F32)
        weight = sb("edge_weight", [P, 2], F32)
        onelo = sb("one_hot_lo", [P, EC, P], BF16)
        onehi = sb("one_hot_hi", [P, EC, KT], BF16)
        rhs = sb("weighted_hi", [P, EC, KT, 2], BF16)
        keyi = sb("key_bits", [P, EC, W], I32)
        keyf = onelo[:, :, 0:2 * W].bitcast(F32)
        best = sb("best_key", [P, KT], F32)
        has = sb("has_edge", [P, KT], F32)
        edge = sb("edge_index", [P, KT], U32)
        attr = sb("edge_attr", [P, KT, 3], F32)
        we = sb("edge_w", [P, 3 * H], F32)
        be = sb("edge_b", [P, H], F32)
        term = sb("bias_term", [P, KT, H], F32)
        bias = sb("key_bias", [P, KT, H], F32)
        masked = sb("bias_masked", [P, KT, H], F32)
        bmax = sb("bias_max", [P, H], F32)
        gmax = sb("bias_max_all", [P, H], F32)
        parts = sb("bias_parts_tm", [P, KT, H, 3], BF16)
        rows = sb("bias_rows", [3 * H, NP], BF16)
        zero = sb("zero_rows", [3, NP], BF16)
        ps = [ctx.enter_context(nc.psum_tensor(f"edge_ps{i}", [P, 512], F32)) for i in range(2)]
        pt = [ctx.enter_context(nc.psum_tensor(f"bias_ps{i}", [P, 1024], BF16)) for i in range(4)]

        loaded = sem("setup_loaded")
        edges_in = sem("edges_loaded")
        onehot = sem("one_hots_ready")
        counted = sem("edges_counted")
        taken = sem("counts_taken")
        indexed = sem("edge_index_ready")
        gathered = sem("attrs_gathered")
        bmax_own = sem("bias_max_ready")
        bmax_all = sem("bias_max_shared")
        split = sem("bias_split")
        turned = sem("bias_turned")
        rowed = sem("bias_rows_ready")
        written = sem("setup_written")
        zeroed = sem("zero_rows_ready")
        dve_step = sem("setup_dve_step")
        n_load = [0]

        with nc.Block() as block:
            @block.sync
            def _(sp):
                ei = io["L0_attn_edge_index"]
                sp.dma_start(tgt[:], ei[1].rearrange("(p c) -> p c", p=P)).then_inc(edges_in, 16)
                sp.dma_start(index[:], io["c_index"]).then_inc(edges_in, 16)
                sp.dma_start(weight[:], io["c_weight"]).then_inc(edges_in, 16)
                sp.dma_start(we[:], io["L0_attn_We"].rearrange("a h -> (a h)").partition_broadcast(P)).then_inc(edges_in, 16)
                sp.dma_start(be[:], io["L0_attn_be"].partition_broadcast(P)).then_inc(edges_in, 16)

                def load(dst, src):
                    n_load[0] += 16
                    sp.dma_start(dst, src).then_inc(loaded, 16)

                for w, name in ((k.w1, "L0_tok_W1"), (k.w3, "L0_tok_W3")):
                    by_tap = io[name].rearrange("(c t) m -> t c m", t=K * K)
                    for s, t in enumerate(TAPS_LO):
                        load(w[0:C, s, :], by_tap[t])
                    for s, t in enumerate(TAPS_HI):
                        load(w[C:P, s, :], by_tap[t])
                load(w2raw[:], io["L0_tok_W2"])
                for half in range(2):
                    load(b2raw[half * C:half * C + C, :], io["L0_tok_b2"].rearrange("(c t) -> c t", t=K * K))
                load(k.b1[:], io["L0_tok_b1"].unsqueeze(1))
                load(k.b3[:], io["L0_tok_b3"].unsqueeze(1))
                for i, s in enumerate("qk"):
                    load(k.wqk[:, i * C:i * C + C], io["L0_attn_W" + s])
                    load(k.bqk[i * C:i * C + C, :], io["L0_attn_b" + s].unsqueeze(1))
                load(k.wv[0:C, :], io["L0_attn_Wv"])
                load(k.wv[C:C + 1, :], io["L0_attn_bv"].unsqueeze(0))
                load(k.eye_bo[0:C, :], io["c_ident"][0:C, 0:C])
                load(k.eye_bo[C:C + 1, :], io["L0_attn_bo"].unsqueeze(0))
                for half in range(2):
                    load(k.wo[half * C:half * C + C, :], io["L0_attn_Wo"])
                load(k.ident[:], io["c_ident"])
                sp.wait_ge(zeroed, 1)
                for bh in range(B * H):
                    sp.dma_start(k.d_shift[bh], zero[:]).then_inc(written, 16)
                sp.wait_ge(rowed, 1)
                for b in range(B):
                    sp.dma_start(k.d_bias[b * H:b * H + H].rearrange("h a n -> (h a) n"), rows[:]).then_inc(written, 16)
                sp.wait_ge(written, 16 * (B * H + B))

            @block.gpsimd
            def _(pool):
                nc.gpsimd.memset(zero[:], 0.0).then_inc(zeroed, 1)
                pool.wait_ge(indexed, 1)
                for t in range(KT):
                    nc.gpsimd.indirect_dma_start(
                        attr[:, t, :], None, io["L0_attn_edge_attr"],
                        bass.IndirectOffsetOnAxis(ap=edge[:, t:t + 1], axis=0)).then_inc(gathered, 16)
                pool.wait_ge(bmax_own, 1)
                nc.gpsimd.partition_all_reduce(gmax[:], bmax[:], P, bass.bass_isa.ReduceOp.max).then_inc(bmax_all, 1)

            @block.tensor
            def _(pe):
                pe.wait_ge(onehot, 1)
                for c in range(EC):
                    g = c // PER
                    if c % PER == 0 and g >= 2:
                        pe.wait_ge(taken, g - 1)
                    o = (c % PER) * W
                    mm = nc.tensor.matmul(ps[g % 2][:, o:o + W], onelo[:, c, :],
                                          rhs[:, c, :, :].rearrange("p h r -> p (h r)"), start=True, stop=True)
                    if c % PER == PER - 1 or c == EC - 1:
                        mm.then_inc(counted, 1)
                pe.wait_ge(split, 1)
                for t in range(KT):
                    tr = nc.tensor.transpose(pt[t // 8][0:3 * H, (t % 8) * P:(t % 8 + 1) * P],
                                             parts[:, t, :, :].rearrange("p h a -> p (h a)"), k.ident_bf[:])
                tr.then_inc(turned, 1)

            @block.vector
            def _(dve):
                v = nc.vector
                step = Steps(dve, dve_step)
                dve.wait_ge(edges_in, 16 * 5)
                step(v.tensor_scalar(tlo[:], tgt[:], P - 1, None, ALU.bitwise_and))
                step(v.tensor_scalar(thi[:], tgt[:], 7, None, ALU.logical_shift_right))
                step(v.tensor_copy(tlof[:], tlo[:]))
                step(v.tensor_copy(thif[:], thi[:]))
                step(v.tensor_tensor(onehi[:], index[:, 0:KT].unsqueeze(1).to_broadcast([P, EC, KT]),
                                     thif[:].unsqueeze(2).to_broadcast([P, EC, KT]), ALU.is_equal))
                for r in range(2):
                    step(v.tensor_scalar(rhs[:, :, :, r], onehi[:], weight[:, r:r + 1], None, ALU.mult))
                v.tensor_tensor(onelo[:], index[:].unsqueeze(1).to_broadcast([P, EC, P]),
                                tlof[:].unsqueeze(2).to_broadcast([P, EC, P]), ALU.is_equal).then_inc(onehot, 1)
                for g in range(NB):
                    n = min(PER, EC - g * PER)
                    dve.wait_ge(counted, g + 1)
                    v.tensor_scalar(keyi[:, g * PER:g * PER + n, :].rearrange("p c w -> p (c w)"),
                                    ps[g % 2][:, 0:n * W].bitcast(I32), 16, 0xFF80,
                                    ALU.logical_shift_right, ALU.bitwise_and).then_inc(taken, 1)
                dve.wait_ge(taken, NB)
                step(v.tensor_tensor(keyf, keyi[:], index[:].unsqueeze(2).to_broadcast([P, EC, W]), ALU.add))
                step(v.tensor_reduce(best[:], keyf.rearrange("p c (h r) -> p h c r", r=2), AX.XY, ALU.max))
                step(v.tensor_scalar(has[:], best[:], float(KEY_BASE), None, ALU.is_ge))
                v.tensor_scalar(edge[:], best[:], float(-KEY_BASE), 0.0, ALU.add, ALU.max).then_inc(indexed, 1)
                dve.wait_ge(loaded, n_load[0])
                for s, t in enumerate(TAPS_LO):
                    step(v.tensor_copy(k.w2[:, s, 0:C], w2raw[:, t::K * K]))
                    step(v.tensor_scalar(k.b2[0:C, s:s + 1], b2raw[0:C, t:t + 1], 0.5, None, ALU.mult))
                for s, t in enumerate(TAPS_HI):
                    step(v.tensor_copy(k.w2[:, s, C:P], w2raw[:, t::K * K]))
                    step(v.tensor_scalar(k.b2[C:P, s:s + 1], b2raw[C:P, t:t + 1], 0.5, None, ALU.mult))
                step(v.memset(k.w1[C:P, NSLOT - 1, :], 0.0))
                step(v.memset(k.w2[:, NSLOT - 1, C:P], 0.0))
                step(v.memset(k.w3[C:P, NSLOT - 1, :], 0.0))
                step(v.memset(k.b2[C:P, NSLOT - 1:NSLOT], 0.0))
                step(v.tensor_scalar(k.w3[:], k.w3[:], 0.5, None, ALU.mult))
                step(v.tensor_scalar(k.wqk[:, 0:C], k.wqk[:, 0:C], float(HD) ** -0.5, None, ALU.mult))
                step(v.tensor_scalar(k.bqk[0:C, :], k.bqk[0:C, :], float(HD) ** -0.5, None, ALU.mult))
                step(v.tensor_copy(k.ident_bf[:], k.ident[:]))
                dve.wait_ge(gathered, 16 * KT)
                for a in range(3):
                    w = we[:, a * H:a * H + H].unsqueeze(1).to_broadcast([P, KT, H])
                    x = attr[:, :, a:a + 1].to_broadcast([P, KT, H])
                    step(v.tensor_tensor((term if a else bias)[:], x, w, ALU.mult))
                    if a:
                        step(v.tensor_tensor(bias[:], bias[:], term[:], ALU.add))
                step(v.tensor_tensor(bias[:], bias[:], be[:].unsqueeze(1).to_broadcast([P, KT, H]), ALU.add))
                step(v.tensor_tensor(bias[:], bias[:], has[:].unsqueeze(2).to_broadcast([P, KT, H]), ALU.mult))
                step(v.tensor_copy(masked[:], bias[:]))
                step(v.memset(masked[TAIL:P, KT - 1, :], -3.0e38))
                v.tensor_reduce(bmax[:], masked[:].rearrange("p t h -> p h t"), AX.X, ALU.max).then_inc(bmax_own, 1)
                dve.wait_ge(bmax_all, 1)
                step(v.tensor_tensor(bias[:], bias[:], gmax[:].unsqueeze(1).to_broadcast([P, KT, H]), ALU.subtract))
                step(v.tensor_copy(parts[:, :, :, 0], bias[:]))
                step(v.tensor_tensor(bias[:], bias[:], parts[:, :, :, 0], ALU.subtract))
                step(v.tensor_copy(parts[:, :, :, 1], bias[:]))
                step(v.tensor_tensor(bias[:], bias[:], parts[:, :, :, 1], ALU.subtract))
                v.tensor_copy(parts[:, :, :, 2], bias[:]).then_inc(split, 1)
                dve.wait_ge(turned, 1)
                for g in range(4):
                    n = min(1024, NP - 1024 * g)
                    step(v.tensor_copy(rows[:, 1024 * g:1024 * g + n], pt[g][0:3 * H, 0:n]))
                v.memset(k.values[:], 0.0).then_inc(rowed, 1)


def tok_phase(k):
    nc, io = k.nc, k.io
    with ExitStack() as ctx:
        def sb(name, shape, dt):
            return ctx.enter_context(nc.sbuf_tensor(name, shape, dt))

        def bank(name):
            return ctx.enter_context(nc.psum_tensor(name, [P, 512], F32))

        def sem(name):
            return ctx.enter_context(nc.semaphore(name))

        raw = sb("image", [P, N], F32)
        pad_row = sb("padded_and_a_row_on", [P, PADW, PADW], F32)
        pad_col = sb("padded_and_a_column_on", [P, PADW, PADW], F32)
        h1 = sb("hidden", [C, CH], F32)
        th = sb("gate_tanh", [P, 2, CH], F32)
        ts = sb("gated_taps", [P, NSLOT, CH], F32)
        hT = sb("h_chunk", [C + 1, CH], F32)
        hTb = sb("h_image", [C + 1, NP], F32)
        part = sb("qk_parts_chunk", [P, 3, CH], BF16)
        rest = sb("qk_rest", [P, CH], F32)
        amax = sb("qk_abs_max", [P, B * NCH], F32)
        amax_b = sb("qk_abs_max_image", [P, B], F32)
        kmax = sb("k_abs_max", [C, B], F32)
        bound = sb("score_bound", [C, B], F32)
        head_sum = sb("head_sum", [C, C], F32)
        bmx = sb("bound_max", [C, 1], F32)
        bmx_all = sb("bound_max_all", [C, 1], F32)
        p_h1 = bank("p_h1")
        p_s = [bank("p_s0"), bank("p_s1")]
        p_h = bank("p_h")
        p_qk = bank("p_qk")
        p_tm = bank("p_tm")
        p_v = [bank("p_v0"), bank("p_v1")]

        img_in = sem("image_loaded")
        pad_zero = sem("padding_zeroed")
        padded = sem("image_padded")
        dve_pad = sem("image_padded_dve")
        h1_sum = sem("hidden_summed")
        h1_rdy = sem("hidden_ready")
        s_sum = sem("gate_summed")
        th_rdy = sem("tanh_ready")
        ts_rdy = sem("gated_ready")
        h_sum = sem("h_summed")
        h_rdy = sem("h_ready")
        hc_rdy = sem("h_chunk_ready")
        qk_sum = sem("qk_summed")
        hi_rdy = sem("hi_ready")
        r1_rdy = sem("rest_ready")
        mid_rdy = sem("mid_ready")
        lo_rdy = sem("lo_ready")
        stored = sem("qk_stored")
        tm_sum = sem("token_major_summed")
        tm_rdy = sem("token_major_ready")
        v_sum = sem("values_summed")
        v_rdy = sem("values_ready")
        step_s = sem("ones_set")
        am_rdy = sem("abs_max_of_chunk_ready")
        kmv = sem("k_max_moved")
        bsum = sem("bounds_summed")
        ball = sem("bound_shared")
        bown = sem("abs_max_ready")
        bmul = sem("bound_products_ready")
        bone = sem("bound_of_heads_ready")
        const_in = sem("head_sum_loaded")
        flagged = sem("flag_ready")

        NV = -(-KT // 8)

        def window(buf, c, tap):
            ki, kj = tap // K, tap % K
            return buf[:, bass.ds(c * 8 + ki, 8), kj:kj + HW]

        SLOT_BUF = [pad_row] * 3 + [pad_col, pad_row]

        with nc.Block() as block:
            @block.sync
            def _(sp):
                sp.dma_start(head_sum[:], io["c_head_sum"]).then_inc(const_in, 16)
                with sp.Fori(0, B) as b:
                    sp.wait_ge(padded, b * 2 + 2)
                    sp.wait_ge(dve_pad, b * 2 + 2)
                    for half in range(2):
                        sp.dma_start(raw[half * C:half * C + C, :],
                                     io["x"][b].rearrange("c h w -> c (h w)")).then_inc(img_in, 16)
                    with sp.Fori(0, NCH) as c:
                        it = b * NCH + c
                        sp.wait_ge(hi_rdy, it + 1)
                        sp.wait_ge(mid_rdy, it + 1)
                        sp.wait_ge(lo_rdy, it + 1)
                        for j in range(3):
                            for i in range(2):
                                sp.dma_start(k.d_qk[j, i, bass.ds(b * C, C), bass.ds(c * CH, CH)],
                                             part[i * C:i * C + C, j, :]).then_inc(stored, 16)
                sp.wait_ge(bown, 1)
                sp.dma_start(kmax[:], amax_b[C:P, :]).then_inc(kmv, 16)
                sp.wait_ge(stored, 16 * 6 * B * NCH)

            @block.gpsimd
            def _(pool):
                step = Steps(pool, padded)
                step(nc.gpsimd.memset(pad_row[:], 0.0))
                step(nc.gpsimd.memset(hTb[C:C + 1, :], 1.0))
                with pool.Fori(0, B * NCH) as it:
                    pool.wait_ge(stored, it * 96)
                    pool.wait_ge(mid_rdy, it + 1)
                    nc.gpsimd.tensor_tensor(part[:, 2, :], rest[:], part[:, 1, :], ALU.subtract).then_inc(lo_rdy, 1)
                pool.wait_ge(bone, 1)
                nc.gpsimd.partition_all_reduce(bmx_all[:], bmx[:], C, bass.bass_isa.ReduceOp.max).then_inc(ball, 1)

            @block.tensor
            def _(pe):
                mm = nc.tensor.matmul
                pe.wait_ge(step_s, 1)
                with pe.Fori(0, B) as b:
                    with pe.Fori(0, NCH) as c:
                        it = b * NCH + c
                        pe.wait_ge(padded, b * 2 + 4)
                        pe.wait_ge(dve_pad, b * 2 + 4)
                        pe.wait_ge(h1_rdy, it)
                        for s in range(NSLOT):
                            i = mm(p_h1[0:C, 0:CH], k.w1[:, s, :], window(SLOT_BUF[s], c, TAPS_LO[s]),
                                   start=(s == 0), stop=(s == NSLOT - 1))
                        i.then_inc(h1_sum, 1)
                        pe.wait_ge(h1_rdy, it + 1)

                        def gate(s):
                            pe.wait_ge(th_rdy, it * NSLOT + max(0, s - 1))
                            mm(p_s[s % 2][:, 0:CH], k.w2[:, s, :], h1[:], start=True, stop=True).then_inc(s_sum, 1)

                        def mix(s):
                            if s == 0:
                                pe.wait_ge(h_rdy, it)
                            pe.wait_ge(ts_rdy, it * NSLOT + s + 1)
                            i = mm(p_h[0:C, 0:CH], k.w3[:, s, :], ts[:, s, :],
                                   start=(s == 0), stop=(s == NSLOT - 1))
                            if s == NSLOT - 1:
                                i.then_inc(h_sum, 1)

                        gate(0)
                        gate(1)
                        for s in range(2, NSLOT):
                            gate(s)
                            mix(s - 2)
                        mix(NSLOT - 2)
                        mix(NSLOT - 1)
                        pe.wait_ge(hc_rdy, it + 1)
                        pe.wait_ge(r1_rdy, it)
                        mm(p_qk[:, 0:CH], k.wqk[:], hT[0:C, :], start=True, stop=True).then_inc(qk_sum, 1)
                        pe.wait_ge(tm_rdy, it)
                        for j in range(4):
                            i = mm(p_tm[0:TM, j * C:j * C + C], hT[:, j * TM:j * TM + TM], k.eye_bo[:],
                                   start=True, stop=True)
                        i.then_inc(tm_sum, 1)
                    pe.wait_ge(h_rdy, b * NCH + NCH)
                    for t in range(KT):
                        g = t // 8
                        if t % 8 == 0:
                            pe.wait_ge(v_rdy, b * NV + max(0, g - 1))
                        m = min(P, N - t * P)
                        i = mm(p_v[g % 2][0:m, (t % 8) * C:(t % 8) * C + C], hTb[:, t * P:t * P + m], k.wv[:],
                               start=True, stop=True)
                        if t % 8 == 7 or t == KT - 1:
                            i.then_inc(v_sum, 1)
                pe.wait_ge(bmul, 1)
                pe.wait_ge(const_in, 16)
                mm(p_h1[0:C, 0:B], head_sum[:], bound[:], start=True, stop=True).then_inc(bsum, 1)

            @block.scalar
            def _(act):
                a = nc.scalar.activation
                with act.Fori(0, B) as b:
                    act.wait_ge(img_in, b * 32 + 32)
                    act.wait_ge(h_sum, b * NCH)
                    act.wait_ge(padded, 2)
                    x = raw[:].rearrange("p (r c) -> p r c", r=HW)
                    a(pad_row[0:C, 1:HW + 1, 1:HW + 1], x[0:C], ACT.Copy).then_inc(padded, 1)
                    a(pad_row[C:P, 0:HW, 1:HW + 1], x[C:P], ACT.Copy).then_inc(padded, 1)
                    with act.Fori(0, NCH) as c:
                        it = b * NCH + c
                        act.wait_ge(h1_sum, it + 1)
                        act.wait_ge(s_sum, it * NSLOT)
                        a(h1[:], p_h1[0:C, 0:CH], ACT.Relu, bias=k.b1[:]).then_inc(h1_rdy, 1)
                        for s in range(NSLOT):
                            act.wait_ge(s_sum, it * NSLOT + s + 1)
                            act.wait_ge(ts_rdy, it * NSLOT + max(0, s - 1))
                            a(th[:, s % 2, :], p_s[s % 2][:, 0:CH], ACT.Tanh, bias=k.b2[:, s:s + 1],
                              scale=0.5).then_inc(th_rdy, 1)
                        act.wait_ge(h_sum, it + 1)
                        act.wait_ge(qk_sum, it)
                        act.wait_ge(tm_sum, it)
                        act.wait_ge(v_sum, b * NV)
                        a(hT[0:C, :], p_h[0:C, 0:CH], ACT.Identity, bias=k.b3[:]).then_inc(hc_rdy, 1)
                        a(hTb[0:C, bass.ds(c * CH, CH)], p_h[0:C, 0:CH], ACT.Identity, bias=k.b3[:]).then_inc(h_rdy, 1)
                        act.wait_ge(qk_sum, it + 1)
                        act.wait_ge(stored, it * 96)
                        act.wait_ge(am_rdy, it)
                        a(part[:, 0, :], p_qk[:, 0:CH], ACT.Identity, bias=k.bqk[:]).then_inc(hi_rdy, 1)

            @block.vector
            def _(dve):
                v = nc.vector
                v.memset(hT[C:C + 1, :], 1.0).then_inc(step_s, 1)
                v.memset(k.values[:, :, 0:KT - 1, HD], 1.0).then_inc(step_s, 1)
                v.memset(k.values[0:TAIL, :, KT - 1, HD], 1.0).then_inc(step_s, 1)
                v.memset(pad_col[:], 0.0).then_inc(dve_pad, 2)
                dve.wait_ge(dve_pad, 2)
                with dve.Fori(0, B) as b:
                    dve.wait_ge(img_in, b * 32 + 32)
                    dve.wait_ge(h_sum, b * NCH)
                    x = raw[:].rearrange("p (r c) -> p r c", r=HW)
                    v.tensor_copy(pad_col[0:C, 1:HW + 1, 1:HW + 1], x[0:C]).then_inc(dve_pad, 1)
                    v.tensor_copy(pad_col[C:P, 1:HW + 1, 0:HW], x[C:P]).then_inc(dve_pad, 1)
                    with dve.Fori(0, NCH) as c:
                        it = b * NCH + c
                        dve.wait_ge(dve_pad, b * 2 + 4)
                        dve.wait_ge(padded, b * 2 + 4)
                        for s in range(NSLOT):
                            dve.wait_ge(th_rdy, it * NSLOT + s + 1)
                            if s == 0:
                                dve.wait_ge(h_sum, it)
                            v.scalar_tensor_tensor(
                                out=ts[:, s, :].rearrange("p (r c) -> p r c", r=8),
                                in0=th[:, s % 2, :].rearrange("p (r c) -> p r c", r=8), scalar=1.0,
                                in1=window(SLOT_BUF[s], c, TAPS_LO[s]), op0=ALU.add,
                                op1=ALU.mult).then_inc(ts_rdy, 1)
                        dve.wait_ge(tm_sum, it + 1)
                        v.tensor_copy(k.x_tm[:, bass.ds(it * 4, 4), :].rearrange("p t c -> p (t c)"),
                                      p_tm[0:TM, 0:4 * C]).then_inc(tm_rdy, 1)
                        dve.wait_ge(hi_rdy, it + 1)
                        dve.wait_ge(lo_rdy, it)
                        v.scalar_tensor_tensor(out=rest[:], in0=p_qk[:, 0:CH], scalar=k.bqk[:], in1=part[:, 0, :],
                                               op0=ALU.add, op1=ALU.subtract).then_inc(r1_rdy, 1)
                        dve.wait_ge(stored, it * 96)
                        dve.wait_ge(r1_rdy, it + 1)
                        v.tensor_copy(part[:, 1, :], rest[:]).then_inc(mid_rdy, 1)
                        v.tensor_reduce(amax[:, bass.ds(it, 1)], part[:, 0, :], AX.X, ALU.max,
                                        apply_absolute_value=True).then_inc(am_rdy, 1)
                    for g in range(NV):
                        dve.wait_ge(v_sum, b * NV + g + 1)
                        n = min(8, KT - 8 * g)
                        m = P if n == 8 else TAIL
                        v.tensor_copy(
                            k.values[0:m, bass.ds(b * H, H), 8 * g:8 * g + n, 0:HD],
                            p_v[g % 2][0:m, 0:n * C].rearrange("p (t h d) -> p h t d", h=H, d=HD)).then_inc(v_rdy, 1)
                dve.wait_ge(am_rdy, B * NCH)
                v.tensor_reduce(amax_b[:], amax[:].rearrange("p (b c) -> p b c", c=NCH), AX.X,
                                ALU.max).then_inc(bown, 1)
                dve.wait_ge(bown, 1)
                dve.wait_ge(kmv, 16)
                v.tensor_tensor(bound[:], amax_b[0:C, :], kmax[:], ALU.mult).then_inc(bmul, 1)
                dve.wait_ge(bsum, 1)
                v.tensor_reduce(bmx[:], p_h1[0:C, 0:B], AX.X, ALU.max).then_inc(bone, 1)
                dve.wait_ge(ball, 1)
                v.tensor_scalar(k.flag[:], bmx_all[0:1, :], SCORE_LIMIT, None, ALU.is_gt).then_inc(flagged, 1)
                dve.wait_ge(flagged, 1)


class Stage:

    LOADS = 8

    def __init__(self, k, ctx, name, n):
        nc = k.nc
        self.k = k
        self.q = [ctx.enter_context(nc.sbuf_tensor(f"{name}_q{i}", [P, NP], BF16)) for i in range(n)]
        self.kk = [ctx.enter_context(nc.sbuf_tensor(f"{name}_k{i}", [P, NP], BF16)) for i in range(n)]
        self.const_in = ctx.enter_context(nc.semaphore(f"{name}_constants"))
        self.cleared = ctx.enter_context(nc.semaphore(f"{name}_cleared"))

    def clear(self):
        for t in self.q + self.kk:
            self.k.nc.gpsimd.memset(t[:], 0.0).then_inc(self.cleared, 1)

    def constants(self, sp):
        sp.wait_ge(self.cleared, 2 * len(self.q))
        for q, kk in zip(self.q, self.kk):
            sp.dma_start(q[BIAS_ROW:SHIFT_ROW, :], self.k.io["c_ones"]).then_inc(self.const_in, 16)
            sp.dma_start(kk[SHIFT_ROW:SHIFT_ROW + 3, :], self.k.io["c_ones"]).then_inc(self.const_in, 16)

    def load(self, sp, i, bh, sem):
        k = self.k
        r = 3 * HD
        for a in range(3):
            src = k.d_qk[a, 0, bass.ds(bh * HD, HD), :].unsqueeze(0).to_broadcast([3, HD, N])
            sp.dma_start(self.q[i][a * r:a * r + r, 0:N], src).then_inc(sem, 16)
            src = k.d_qk[:, 1, bass.ds(bh * HD, HD), :]
            sp.dma_start(self.kk[i][a * r:a * r + r, 0:N], src).then_inc(sem, 16)
        sp.dma_start(self.kk[i][BIAS_ROW:SHIFT_ROW, 0:N],
                     k.d_bias[bass.ds(bh, 1), :, 0:N].rearrange("o a n -> (o a) n")).then_inc(sem, 16)
        sp.dma_start(self.q[i][SHIFT_ROW:SHIFT_ROW + 3, :],
                     k.d_shift[bass.ds(bh, 1)].rearrange("o a n -> (o a) n")).then_inc(sem, 16)


def maximum_phase(k):
    nc = k.nc
    with ExitStack() as ctx:
        def sem(name):
            return ctx.enter_context(nc.semaphore(name))

        def sb(name, shape, dt):
            return ctx.enter_context(nc.sbuf_tensor(name, shape, dt))

        stage = Stage(k, ctx, "max", 1)
        rowmax = sb("row_max", [P, KT], F32)
        parts = sb("shift_parts_tm", [P, 3, KT], BF16)
        rows = sb("shift_rows", [3 * KT, P], BF16)
        scores = ctx.enter_context(nc.psum_tensor("max_scores", [P, NCH, 512], F32))
        turned = ctx.enter_context(nc.psum_tensor("max_turned", [P, 1024], BF16))
        staged = sem("max_staged")
        scored = sem("max_scored")
        reduced = sem("max_reduced")
        split = sem("max_split")
        flipped = sem("max_flipped")
        rowed = sem("max_rowed")
        stored = sem("max_stored")
        one = sem("max_step")
        with nc.Block() as block:
            @block.gpsimd
            def _(pool):
                stage.clear()

            @block.sync
            def _(sp):
                stage.constants(sp)
                sp.wait_ge(stage.const_in, 32)
                need = sp.value_load(k.flag[0:1, 0:1], min_val=0, max_val=1)
                with sp.If(need > 0):
                    with sp.Fori(0, B * H) as bh:
                        sp.wait_ge(split, bh)
                        stage.load(sp, 0, bh, staged)
                        sp.wait_ge(rowed, bh + 1)
                        sp.dma_start(k.d_shift[bass.ds(bh, 1)].rearrange("o a (t p) -> (o a t) p", p=P),
                                     rows[:]).then_inc(stored, 16)
                    sp.wait_ge(stored, 16 * B * H)

            @block.tensor
            def _(pe):
                pe.wait_ge(stage.const_in, 32)
                need = pe.value_load(k.flag[0:1, 0:1], min_val=0, max_val=1)
                with pe.If(need > 0):
                    with pe.Fori(0, B * H) as bh:
                        with pe.Fori(0, KT) as t:
                            pe.wait_ge(staged, bh * (16 * Stage.LOADS) + 16 * Stage.LOADS)
                            pe.wait_ge(reduced, bh * KT + t)
                            for c in range(NCH):
                                mm = nc.tensor.matmul(scores[:, c, 0:CH], stage.q[0][:, bass.ds(t * P, P)],
                                                      stage.kk[0][:, c * CH:c * CH + CH], start=True, stop=True)
                            mm.then_inc(scored, 1)
                        pe.wait_ge(split, bh + 1)
                        pe.wait_ge(stage.const_in, 32)
                        nc.tensor.transpose(turned[0:3 * KT, 0:P], parts[:].rearrange("p a t -> p (a t)"),
                                            k.ident_bf[:]).then_inc(flipped, 1)

            @block.vector
            def _(dve):
                v = nc.vector
                step = Steps(dve, one)
                dve.wait_ge(stage.const_in, 32)
                need = dve.value_load(k.flag[0:1, 0:1], min_val=0, max_val=1)
                with dve.If(need > 0):
                    with dve.Fori(0, B * H) as bh:
                        with dve.Fori(0, KT) as t:
                            dve.wait_ge(scored, bh * KT + t + 1)
                            v.tensor_reduce(rowmax[:, bass.ds(t, 1)], scores[:, :, 0:CH], AX.XY,
                                            ALU.max).then_inc(reduced, 1)
                        dve.wait_ge(reduced, bh * KT + KT)
                        step.loop(bh * 5)
                        step(v.tensor_scalar(rowmax[:], rowmax[:], -1.0, None, ALU.mult))
                        step(v.tensor_copy(parts[:, 0, :], rowmax[:]))
                        step(v.tensor_tensor(rowmax[:], rowmax[:], parts[:, 0, :], ALU.subtract))
                        step(v.tensor_copy(parts[:, 1, :], rowmax[:]))
                        step(v.tensor_tensor(rowmax[:], rowmax[:], parts[:, 1, :], ALU.subtract))
                        v.tensor_copy(parts[:, 2, :], rowmax[:]).then_inc(split, 1)
                        dve.wait_ge(stored, bh * 16)
                        dve.wait_ge(flipped, bh + 1)
                        v.tensor_copy(rows[:], turned[0:3 * KT, 0:P]).then_inc(rowed, 1)


def attention_phase(k):
    nc = k.nc
    UNIT = 3
    UNITS = (KT - 1) // UNIT
    RING = 4
    PAIRS = B * H // 2
    HEAD = UNITS * NCH
    with ExitStack() as ctx:
        def sem(name):
            return ctx.enter_context(nc.semaphore(name))

        def sb(name, shape, dt):
            return ctx.enter_context(nc.sbuf_tensor(name, shape, dt))

        def psum(name, shape):
            return ctx.enter_context(nc.psum_tensor(name, shape, F32))

        stage = Stage(k, ctx, "stage", 2)
        vst = [sb(f"stage_v{i}", [P, KT, HD + 1], F32) for i in range(2)]
        probs = sb("probs", [P, RING, UNIT, CH], F32)
        ptail = sb("probs_tail", [P, CH], F32)
        mixed = [sb(f"mixed{i}", [P, N], F32) for i in range(2)]
        p_sc = [psum(f"p_scores{i}", [P, UNIT, 512]) for i in range(2)]
        p_tl = psum("p_tail", [P, 512])
        p_mx = psum("p_mixed", [P, 512])

        staged = [sem(f"staged{i}") for i in range(2)]
        v_staged = [sem(f"values_staged{i}") for i in range(2)]
        s_rdy = sem("scores_ready")
        e_rdy = sem("exps_ready")
        used = sem("exps_used")
        t_rdy = sem("tail_ready")
        te_rdy = sem("tail_exp_ready")
        t_used = sem("tail_exp_used")
        mx_out = sem("mixed_taken")
        stored = [sem(f"mixed_stored{i}") for i in range(2)]
        tail_clean = sem("tail_slot_zeroed")
        sums_clean = sem("sums_bank_zeroed")

        with nc.Block() as block:
            @block.gpsimd
            def _(pool):
                stage.clear()
                nc.gpsimd.memset(ptail[:], 0.0).then_inc(tail_clean, 1)
                for i in range(2):
                    nc.gpsimd.tensor_copy(vst[i][:], k.values[:, i]).then_inc(v_staged[i], 1)
                with pool.Fori(0, PAIRS - 1) as pair:
                    for i in range(2):
                        pool.wait_ge(used, (pair * 2 + i + 1) * HEAD + RING)
                        nc.gpsimd.tensor_copy(vst[i][:], k.values[:, bass.ds(pair * 2 + 2 + i, 1)].rearrange(
                            "p o t d -> p (o t) d")).then_inc(v_staged[i], 1)

            @block.sync
            def _(sp):
                def store(i, pair):
                    sp.wait_ge(mx_out, (pair * 2 + i) * NCH + NCH)
                    for g in range(GROUPS):
                        sp.dma_start(k.d_mix[bass.ds(pair * 2 + i, 1), g].rearrange("o r n -> (o r) n"),
                                     mixed[i][32 * g:32 * g + HD + 1, :]).then_inc(stored[i], 16)

                stage.constants(sp)
                for i in range(2):
                    stage.load(sp, i, i, staged[i])
                with sp.Fori(0, PAIRS - 1) as pair:
                    for i in range(2):
                        store(i, pair)
                        sp.wait_ge(s_rdy, (pair * 2 + i + 1) * HEAD)
                        stage.load(sp, i, pair * 2 + 2 + i, staged[i])
                for i in range(2):
                    store(i, PAIRS - 1)
                for i in range(2):
                    sp.wait_ge(stored[i], 16 * GROUPS * PAIRS)

            @block.tensor
            def _(pe):
                mm = nc.tensor.matmul

                def scores(i, c, it, u):
                    pe.wait_ge(e_rdy, it * UNITS + u + 1)
                    for j in range(UNIT):
                        t = u * UNIT + j
                        m = mm(p_sc[u % 2][:, j, 0:CH], stage.kk[i][:, t * P:t * P + P],
                               stage.q[i][:, bass.ds(c * CH, CH)], start=True, stop=True)
                    m.then_inc(s_rdy, 1)

                def tail_scores(i, c, it):
                    pe.wait_ge(te_rdy, it + 1)
                    mm(p_tl[:, 0:CH], stage.kk[i][:, (KT - 1) * P:KT * P], stage.q[i][:, bass.ds(c * CH, CH)],
                       start=True, stop=True).then_inc(t_rdy, 1)

                def mix(i, it, u):
                    if u == 0:
                        pe.wait_ge(mx_out, it)
                    pe.wait_ge(e_rdy, it * UNITS + u + 3)
                    for j in range(UNIT):
                        t = u * UNIT + j
                        g = t % GROUPS
                        m = mm(p_mx[32 * g:32 * g + HD + 1, 0:CH], vst[i][:, t, :], probs[:, u % RING, j, :],
                               start=(t < GROUPS), stop=(t >= KT - 1 - GROUPS))
                    m.then_inc(used, 1)

                def tail_mix(i, it):
                    pe.wait_ge(te_rdy, it + 2)
                    mm(p_mx[0:HD + 1, 0:CH], vst[i][:, KT - 1, :], ptail[:], start=False, stop=False).then_inc(t_used, 1)

                def chunk(i, c, bh, after):
                    it = bh * NCH + c
                    tail_scores(i, c, it)
                    for u in range(UNITS - 1):
                        scores(i, c, it, u + 1)
                        mix(i, it, u)
                        if u == 1:
                            tail_mix(i, it)
                    if after is not None:
                        after()
                    mix(i, it, UNITS - 1)

                pe.sem_inc(used, RING)
                pe.sem_inc(t_used, 1)
                pe.wait_ge(tail_clean, 1)
                pe.wait_ge(sums_clean, 1)
                pe.wait_ge(stage.const_in, 64)
                with pe.Fori(0, PAIRS) as pair:
                    for i in range(2):
                        bh = pair * 2 + i
                        if i == 0:
                            pe.wait_ge(staged[0], (pair + 1) * 16 * Stage.LOADS)
                            scores(0, 0, bh * NCH, 0)
                        with pe.Fori(0, NCH - 1) as c:
                            pe.wait_ge(v_staged[i], pair + 1)
                            chunk(i, c, bh, lambda: scores(i, c + 1, bh * NCH + c + 1, 0))

                        def next_head():
                            if i == 0:
                                pe.wait_ge(staged[1], (pair + 1) * 16 * Stage.LOADS)
                                scores(1, 0, bh * NCH + NCH, 0)
                        chunk(i, NCH - 1, bh, next_head)

            @block.scalar
            def _(act):
                act.sem_inc(e_rdy, 2)
                act.sem_inc(te_rdy, 1)
                act.wait_ge(tail_clean, 1)
                a = nc.scalar.activation
                with act.Fori(0, B * H * NCH) as it:
                    for u in range(UNITS):
                        act.wait_ge(s_rdy, it * UNITS + u + 1)
                        act.wait_ge(used, it * UNITS + u + 1)
                        a(probs[:, u % RING], p_sc[u % 2][:, :, 0:CH], ACT.Exp).then_inc(e_rdy, 1)
                        if u == 0:
                            act.wait_ge(t_rdy, it + 1)
                            act.wait_ge(t_used, it + 1)
                            a(ptail[0:TAIL, :], p_tl[0:TAIL, 0:CH], ACT.Exp).then_inc(te_rdy, 1)

            @block.vector
            def _(dve):
                v = nc.vector
                v.memset(p_mx[:], 0.0).then_inc(sums_clean, 1)
                with dve.Fori(0, PAIRS) as pair:
                    for i in range(2):
                        with dve.Fori(0, NCH) as c:
                            it = (pair * 2 + i) * NCH + c
                            dve.wait_ge(stored[i], pair * (16 * GROUPS))
                            dve.wait_ge(used, it * UNITS + UNITS + RING)
                            v.tensor_copy(mixed[i][:, bass.ds(c * CH, CH)], p_mx[:, 0:CH]).then_inc(mx_out, 1)


def project_phase(k):
    nc = k.nc
    SEG = N * H // P
    with ExitStack() as ctx:
        def sem(name):
            return ctx.enter_context(nc.semaphore(name))

        def sb(name, shape, dt):
            return ctx.enter_context(nc.sbuf_tensor(name, shape, dt))

        den = sb("denominators", [P, B, GROUPS, SEG], F32)
        dsum = sb("denominator_sums", [P, B, SEG], F32)
        rec = sb("denominator_recips_sb", [P, B, SEG], F32)
        num = [sb(f"numerators{i}", [P, GROUPS, CH], F32) for i in range(2)]
        rcb = [sb(f"recips{i}", [P, CH], F32) for i in range(2)]
        low = [sb(f"num_low{i}", [P, CH], F32) for i in range(2)]
        high = [sb(f"num_high{i}", [P, CH], F32) for i in range(2)]
        o = [sb(f"attn_out{i}", [P, CH], F32) for i in range(2)]
        p_y = [ctx.enter_context(nc.psum_tensor(f"p_y{i}", [P, 2, 512], F32)) for i in range(2)]
        den_in = sem("denominators_in")
        rec_rdy = sem("recips_ready")
        rec_out = sem("recips_stored")
        num_in = [sem(f"numerators_in{i}") for i in range(2)]
        hi_rdy = sem("high_sums_ready")
        steps = sem("project_step")
        o_rdy = sem("out_ready")
        y_sum = sem("projected")
        y_rdy = sem("residual_added")
        IT = B * NCH // 2

        with nc.Block() as block:
            @block.sync
            def _(sp):
                for b in range(B):
                    for g in range(GROUPS):
                        sp.dma_start(den[:, b, g, :], k.d_mix[b * H:b * H + H, g, HD, :].rearrange(
                            "h (j n) -> h j n", n=SEG)).then_inc(den_in, 16)
                sp.wait_ge(rec_rdy, 2)
                for b in range(B):
                    sp.dma_start(k.d_recip[b * H:b * H + H, :].rearrange("h (j n) -> (h j) n", n=SEG),
                                 rec[:, b, :]).then_inc(rec_out, 16)
                sp.wait_ge(rec_out, 16 * B)
                with sp.Fori(0, 2) as b:
                    for c in range(NCH):
                        it = b * NCH + c
                        i = c % 2
                        sp.wait_ge(o_rdy, b * NCH + max(0, c - 1))
                        cols = slice(c * CH, c * CH + CH)
                        for half in range(2):
                            at = slice(half * C, half * C + C)
                            heads = bass.ds(b * H + half * 2 * H, H)
                            for g in range(GROUPS):
                                sp.dma_start(num[i][at, g, :], k.d_mix[heads, g, 0:HD, cols]).then_inc(num_in[i], 16)
                            sp.dma_start(rcb[i][at, :], k.d_recip[heads, cols].unsqueeze(1).to_broadcast(
                                [H, HD, CH])).then_inc(num_in[i], 16)

            @block.gpsimd
            def _(pool):
                with pool.Fori(0, 2) as b:
                    for c in range(NCH):
                        i = c % 2
                        n = (NCH + 1) // 2 if i == 0 else NCH // 2
                        pool.wait_ge(o_rdy, b * NCH + max(0, c - 1))
                        pool.wait_ge(num_in[i], b * (n * 160) + (c // 2 + 1) * 160)
                        nc.gpsimd.tensor_tensor(high[i][:], num[i][:, 2, :], num[i][:, 3, :], ALU.add).then_inc(hi_rdy, 1)

            @block.vector
            def _(dve):
                v = nc.vector
                dve.wait_ge(den_in, 16 * B * GROUPS)
                v.tensor_reduce(dsum[:], den[:].rearrange("p b g n -> p b n g"), AX.X, ALU.add).then_inc(rec_rdy, 1)
                dve.wait_ge(rec_rdy, 1)
                v.reciprocal(rec[:], dsum[:]).then_inc(rec_rdy, 1)
                step = Steps(dve, steps)
                with dve.Fori(0, 2) as b:
                    for c in range(NCH):
                        it = b * NCH + c
                        i = c % 2
                        n = (NCH + 1) // 2 if i == 0 else NCH // 2
                        step.loop(it * 2)
                        dve.wait_ge(num_in[i], b * (n * 160) + (c // 2 + 1) * 160)
                        step(v.tensor_tensor(low[i][:], num[i][:, 0, :], num[i][:, 1, :], ALU.add))
                        dve.wait_ge(hi_rdy, it + 1)
                        step(v.tensor_tensor(low[i][:], low[i][:], high[i][:], ALU.add))
                        dve.wait_ge(y_sum, b * NCH + max(0, c - 1))
                        v.tensor_tensor(o[i][:], low[i][:], rcb[i][:], ALU.mult).then_inc(o_rdy, 1)
                        dve.wait_ge(y_sum, it + 1)
                        for half in range(2):
                            x = k.x_tm[:, bass.ds(b * NT + half * 2 * NT + c * 4, 4), :]
                            v.tensor_tensor(x, x, p_y[i][0:TM, half, 0:4 * C].rearrange("p (t c) -> p t c", c=C),
                                            ALU.add).then_inc(y_rdy, 1)

            @block.tensor
            def _(pe):
                with pe.Fori(0, 2) as b:
                    for c in range(NCH):
                        it = b * NCH + c
                        i = c % 2
                        pe.wait_ge(y_rdy, b * (2 * NCH) + 2 * max(0, c - 1))
                        pe.wait_ge(o_rdy, it + 1)
                        for half in range(2):
                            at = slice(half * C, half * C + C)
                            for j in range(4):
                                m = nc.tensor.matmul(p_y[i][0:TM, half, j * C:j * C + C],
                                                     o[i][at, j * TM:j * TM + TM], k.wo[at, :], start=True, stop=True)
                        m.then_inc(y_sum, 1)


class Norm:

    STEPS = 4

    def __init__(self, k, ctx, name):
        nc = k.nc
        self.k = k
        self.sq = [ctx.enter_context(nc.sbuf_tensor(f"{name}_squares{i}", [TM, NT, C], F32)) for i in range(2)]
        self.stat = ctx.enter_context(nc.sbuf_tensor(f"{name}_stats", [TM, 4, B, NT], F32))
        self.eps = ctx.enter_context(nc.sbuf_tensor(f"{name}_eps", [TM, 1], F32))
        self.centred = ctx.enter_context(nc.semaphore(f"{name}_centred"))
        self.squared = ctx.enter_context(nc.semaphore(f"{name}_squared"))
        self.summed = ctx.enter_context(nc.semaphore(f"{name}_summed"))
        self.rooted = ctx.enter_context(nc.semaphore(f"{name}_rooted"))
        self.done = ctx.enter_context(nc.semaphore(f"{name}_done"))
        self.step = Steps(nc.vector, ctx.enter_context(nc.semaphore(f"{name}_step")))
        self.eps_set = ctx.enter_context(nc.semaphore(f"{name}_eps_set"))

    def vector(self, dve, x, before=None, after=None):
        v, st, step = self.k.nc.vector, self.stat, self.step
        v.memset(self.eps[:], EPS).then_inc(self.eps_set, 1)

        def centre(b):
            if before is not None:
                before(b)
            xb = x[:, b * NT:b * NT + NT, :]
            step(v.tensor_reduce(st[:, 0, b, :], xb, AX.X, ALU.add))
            step(v.tensor_scalar(st[:, 0, b, :], st[:, 0, b, :], 1.0 / C, None, ALU.mult))
            v.tensor_tensor(xb, xb, st[:, 0, b, :].unsqueeze(2).to_broadcast([TM, NT, C]),
                            ALU.subtract).then_inc(self.centred, 1)

        def scale(b):
            xb = x[:, b * NT:b * NT + NT, :]
            dve.wait_ge(self.squared, b + 1)
            v.tensor_reduce(st[:, 1, b, :], self.sq[b % 2][:], AX.X, ALU.add).then_inc(self.summed, 1)
            dve.wait_ge(self.rooted, b + 1)
            step(v.reciprocal(st[:, 3, b, :], st[:, 2, b, :]))
            step(v.tensor_tensor(xb, xb, st[:, 3, b, :].unsqueeze(2).to_broadcast([TM, NT, C]), ALU.mult))
            if after is not None:
                after(b)
            v.memset(st[0:1, 0, b, 0:1], 0.0).then_inc(self.done, 1)

        centre(0)
        for b in range(B):
            if b + 1 < B:
                centre(b + 1)
            scale(b)

    def scalar(self, act, x):
        a, st = self.k.nc.scalar.activation, self.stat

        def square(b):
            act.wait_ge(self.centred, b + 1)
            if b >= 2:
                act.wait_ge(self.summed, b - 1)
            a(self.sq[b % 2][:], x[:, b * NT:b * NT + NT, :], ACT.Square).then_inc(self.squared, 1)

        act.wait_ge(self.eps_set, 1)
        square(0)
        for b in range(B):
            if b + 1 < B:
                square(b + 1)
            act.wait_ge(self.summed, b + 1)
            a(st[:, 2, b, :], st[:, 1, b, :], ACT.Sqrt, bias=self.eps[:], scale=1.0 / C).then_inc(self.rooted, 1)


def moe_phase(k):
    nc, io = k.nc, k.io
    x_tm = k.x_tm
    NTA = B * NT
    with ExitStack() as ctx:
        def sem(name):
            return ctx.enter_context(nc.semaphore(name))

        def sb(name, shape, dt):
            return ctx.enter_context(nc.sbuf_tensor(name, shape, dt))

        def split3(step, v, raw, parts, rest):
            step(v.tensor_copy(parts[0], raw))
            step(v.tensor_tensor(rest, raw, parts[0], ALU.subtract))
            step(v.tensor_copy(parts[1], rest))
            step(v.tensor_tensor(rest, rest, parts[1], ALU.subtract))
            step(v.tensor_copy(parts[2], rest))

        w1l = sb("expert_w1_parts", [P, 3, EXP, FF], BF16)
        gwl = sb("gate_w_parts", [P, 3, EXP], BF16)
        w2f = sb("expert_w2", [FF, EXP, C], F32)
        b1t = sb("expert_b1", [FF, EXP], F32)
        b2l = sb("expert_b2_parts", [3 * EXP, 3, C], BF16)
        sel = sb("expert_selector", [3 * EXP, EXP, FF], BF16)
        fold = sb("fold", [P, C], F32)
        gb = sb("gate_b", [TM, EXP], F32)
        gamma = sb("gamma", [TM, C], F32)
        beta = sb("beta", [TM, C], F32)
        eidx = sb("expert_index", [TM, EXP], F32)
        x_hm = sb("x_hi_mid", [P, B * N], BF16)
        x_hl = sb("x_hi_lo", [P, B * N], BF16)
        gates = sb("gate_parts", [TM, NTA, 3 * EXP], BF16)
        loaded = sem("moe_loaded")
        LOADED = 16 * 15
        carrier = sem("wait_carrier")

        with ExitStack() as c1:
            norm = Norm(k, c1, "norm1")
            w1raw = c1.enter_context(nc.sbuf_tensor("w1_raw", [P, EXP, FF], F32))
            w1rest = c1.enter_context(nc.sbuf_tensor("w1_rest", [P, EXP, FF], F32))
            w1part = c1.enter_context(nc.sbuf_tensor("w1_part", [P, 3, EXP, FF], BF16))
            gwraw = c1.enter_context(nc.sbuf_tensor("gw_raw", [P, EXP], F32))
            gwrest = c1.enter_context(nc.sbuf_tensor("gw_rest", [P, EXP], F32))
            gwpart = c1.enter_context(nc.sbuf_tensor("gw_part", [P, 3, EXP], BF16))
            b1raw = c1.enter_context(nc.sbuf_tensor("b1_raw", [EXP, FF], F32))
            b2raw = c1.enter_context(nc.sbuf_tensor("eb2_raw", [3 * EXP, C], F32))
            b2rest = c1.enter_context(nc.sbuf_tensor("b2_rest", [3 * EXP, C], F32))
            pb = c1.enter_context(nc.psum_tensor("p_b1", [P, 512], F32))
            b1_in = c1.enter_context(nc.semaphore("b1_in"))
            b1_flip = c1.enter_context(nc.semaphore("b1_flipped"))
            wsteps = c1.enter_context(nc.semaphore("moe_weight_step"))
            with nc.Block() as block:
                @block.sync
                def _(sp):
                    sp.dma_start(b1raw[:], io["L0_ffn_b1"]).then_inc(b1_in, 16)

                    def load(dst, src):
                        sp.dma_start(dst, src).then_inc(loaded, 16)

                    for half in range(2):
                        at = slice(half * C, half * C + C)
                        load(w1raw[at], io["L0_ffn_w1"].rearrange("e c f -> c e f"))
                        load(gwraw[at], io["L0_ffn_gate_w"])
                        load(fold[at, :], io["c_ident"][0:C, 0:C])
                    for a in range(3):
                        load(b2raw[a * EXP:a * EXP + EXP, :], io["L0_ffn_b2"])
                    load(sel[:], io["c_select"])
                    load(w2f[:], io["L0_ffn_w2"].rearrange("e f c -> f e c"))
                    load(eidx[:], io["c_index"][0:TM, 0:EXP])
                    for t, name in ((gb, "gate_b"), (gamma, "gamma"), (beta, "beta")):
                        load(t[:], io["L0_ffn_" + name].partition_broadcast(TM))

                @block.tensor
                def _(pe):
                    pe.wait_ge(b1_in, 16)
                    nc.tensor.transpose(pb[:, 0:EXP], b1raw[:], k.ident[0:EXP, 0:EXP]).then_inc(b1_flip, 1)

                @block.scalar
                def _(act):
                    norm.scalar(act, x_tm)

                @block.vector
                def _(dve):
                    v = nc.vector
                    norm.vector(dve, x_tm)
                    step = Steps(dve, wsteps)
                    dve.wait_ge(loaded, LOADED)
                    split3(step, v, w1raw[:], [w1part[:, a] for a in range(3)], w1rest[:])
                    split3(step, v, gwraw[:], [gwpart[:, a] for a in range(3)], gwrest[:])
                    split3(step, v, b2raw[:], [b2l[:, a] for a in range(3)], b2rest[:])
                    for dst, src in ((w1l, w1part), (gwl, gwpart)):
                        step(v.tensor_copy(dst[:, 0:2], src[:, 0:2]))
                        step(v.tensor_copy(dst[0:C, 2], src[0:C, 2]))
                        step(v.tensor_copy(dst[C:P, 2], src[C:P, 0]))
                    dve.wait_ge(b1_flip, 1)
                    step(v.tensor_copy(b1t[:], pb[:, 0:EXP]))

        with ExitStack() as c2:
            def sb2(name, shape, dt):
                return c2.enter_context(nc.sbuf_tensor(name, shape, dt))

            def sem2(name):
                return c2.enter_context(nc.semaphore(name))

            xd = [sb2(f"x_doubled{i}", [TM, 4, 2, C], F32) for i in range(2)]
            rest = sb2("x_rest", [P, CH], F32)
            lg = sb2("logits", [TM, 4, EXP], F32)
            m8 = sb2("largest", [TM, 4, 8], F32)
            i8 = sb2("largest_index", [TM, 4, 8], U32)
            top = sb2("top_logits", [TM, NTA, 2], F32)
            topi = sb2("top_index", [TM, NTA, 2], F32)
            wgt = sb2("top_weights", [TM, 4, NTA], F32)
            one_hot = sb2("gate_one_hot", [TM, NTA, EXP], F32)
            gate = sb2("gate_full", [TM, NTA, EXP], F32)
            p_x = [c2.enter_context(nc.psum_tensor(f"p_x{i}", [P, 512], F32)) for i in range(2)]
            p_lg = c2.enter_context(nc.psum_tensor("p_logits", [P, 512], F32))
            doubled = sem2("x_doubled_ready")
            flipped = sem2("x_flipped")
            hi_rdy = sem2("x_hi_ready")
            rest_rdy = sem2("x_rest_ready")
            mid_rdy = sem2("x_mid_ready")
            lo_rdy = sem2("x_lo_ready")
            lg_sum = sem2("logits_summed")
            lg_rdy = sem2("logits_ready")
            tops = sem2("router_step")
            diff = sem2("difference_ready")
            expd = sem2("difference_exp")
            gstep = sem2("gate_step")
            with nc.Block() as block:
                @block.gpsimd
                def _(pool):
                    with pool.Fori(0, NTA // 8) as it2:
                        for i in range(2):
                            it = it2 * 2 + i
                            pool.wait_ge(flipped, it2 * 2)
                            for d in range(2):
                                nc.gpsimd.tensor_copy(xd[i][:, :, d, :], x_tm[:, bass.ds(it * 4, 4), :]).then_inc(doubled, 1)

                @block.tensor
                def _(pe):
                    def flip(i, it):
                        pe.wait_ge(doubled, it * 2 + 2)
                        pe.wait_ge(rest_rdy, it - i)
                        for j in range(4):
                            m = nc.tensor.transpose(p_x[i][:, j * TM:j * TM + TM],
                                                    xd[i][:, j].rearrange("p d c -> p (d c)"), k.ident[0:TM, 0:TM])
                        m.then_inc(flipped, 1)

                    with pe.Fori(0, NTA // 8) as it2:
                        for i in range(2):
                            it = it2 * 2 + i
                            flip(i, it)
                            pe.wait_ge(mid_rdy, it + 1)
                            pe.wait_ge(lo_rdy, it + 1)
                            pe.wait_ge(lg_rdy, it)
                            for j in range(4):
                                at = bass.ds(it * CH + j * TM, TM)
                                for a, xs in enumerate((x_hm, x_hm, x_hl)):
                                    m = nc.tensor.matmul(p_lg[0:TM, j * EXP:j * EXP + EXP], xs[:, at], gwl[:, a, :],
                                                         start=(a == 0), stop=(a == 2))
                            m.then_inc(lg_sum, 1)

                @block.scalar
                def _(act):
                    a = nc.scalar.activation
                    with act.Fori(0, NTA // 8) as it2:
                        for i in range(2):
                            it = it2 * 2 + i
                            act.wait_ge(flipped, it + 1)
                            at = bass.ds(it * CH, CH)
                            a(x_hm[:, at], p_x[i][:, 0:CH], ACT.Identity).then_inc(hi_rdy, 1)
                            a(x_hl[0:C, at], p_x[i][0:C, 0:CH], ACT.Identity).then_inc(hi_rdy, 1)
                    act.wait_ge(diff, 1)
                    a(wgt[:, 1, :], wgt[:, 0, :], ACT.Exp).then_inc(expd, 1)

                @block.vector
                def _(dve):
                    v = nc.vector
                    step = Steps(dve, tops)
                    with dve.Fori(0, NTA // 8) as it2:
                        for i in range(2):
                            it = it2 * 2 + i
                            at = bass.ds(it * CH, CH)
                            dve.wait_ge(hi_rdy, it * 2 + 2)
                            dve.wait_ge(lo_rdy, it)
                            v.tensor_tensor(rest[:], p_x[i][:, 0:CH], x_hm[:, at], ALU.subtract).then_inc(rest_rdy, 1)
                            dve.wait_ge(rest_rdy, it + 1)
                            v.tensor_copy(x_hm[C:P, at], rest[C:P, :]).then_inc(mid_rdy, 1)
                            dve.wait_ge(mid_rdy, it + 1)
                            v.tensor_tensor(x_hl[C:P, at], rest[C:P, :], x_hm[C:P, at], ALU.subtract).then_inc(lo_rdy, 1)
                            dve.wait_ge(lg_sum, it + 1)
                            v.tensor_tensor(lg[:], p_lg[0:TM, 0:4 * EXP].rearrange("p (t e) -> p t e", e=EXP),
                                            gb[:].unsqueeze(1).to_broadcast([TM, 4, EXP]), ALU.add).then_inc(lg_rdy, 1)
                            dve.wait_ge(lg_rdy, it + 1)
                            dve.sem_inc(carrier, 1)
                            step.loop(it * 4)
                            for j in range(4):
                                m = v.max(m8[:, j, :], lg[:, j, :])
                            step(m)
                            dve.sem_inc(carrier, 1)
                            for j in range(4):
                                m = v.max_index(i8[:, j, :], m8[:, j, :], lg[:, j, :])
                            step(m)
                            step(v.tensor_copy(top[:, bass.ds(it * 4, 4), :], m8[:, :, 0:2]))
                            step(v.tensor_copy(topi[:, bass.ds(it * 4, 4), :], i8[:, :, 0:2]))
                    v.tensor_tensor(wgt[:, 0, :], top[:, :, 1], top[:, :, 0], ALU.subtract).then_inc(diff, 1)
                    dve.wait_ge(expd, 1)
                    step = Steps(dve, gstep)
                    step(v.tensor_scalar(wgt[:, 0, :], wgt[:, 1, :], 1.0, None, ALU.add))
                    step(v.reciprocal(wgt[:, 2, :], wgt[:, 0, :]))
                    step(v.tensor_tensor(wgt[:, 3, :], wgt[:, 1, :], wgt[:, 2, :], ALU.mult))
                    full = [TM, NTA, EXP]
                    for a, buf in ((0, gate), (1, one_hot)):
                        step(v.tensor_tensor(buf[:], eidx[:].unsqueeze(1).to_broadcast(full),
                                             topi[:, :, a:a + 1].to_broadcast(full), ALU.is_equal))
                        step(v.tensor_tensor(buf[:], buf[:], wgt[:, 2 + a, :].unsqueeze(2).to_broadcast(full), ALU.mult))
                    step(v.tensor_tensor(gate[:], gate[:], one_hot[:], ALU.add))
                    split3(step, v, gate[:], [gates[:, :, a * EXP:a * EXP + EXP] for a in range(3)], one_hot[:])

        y_tm = sb("y_token_major", [TM, NTA, C], F32)
        with ExitStack() as c3:
            def sb3(name, shape, dt):
                return c3.enter_context(nc.sbuf_tensor(name, shape, dt))

            def bank(name):
                return c3.enter_context(nc.psum_tensor(name, [P, 512], F32))

            def sem3(name):
                return c3.enter_context(nc.semaphore(name))

            gst = sb3("gate_chunk", [TM, 4, 3 * EXP], BF16)
            gT = [sb3(f"gates_T{i}", [3 * EXP, CH], BF16) for i in range(2)]
            hid = sb3("hidden_relu", [FF, 2, CH], F32)
            hg = sb3("hidden_gated", [FF, 4, CH], F32)
            zs = sb3("expert_sums", [P, CH], F32)
            p_hid = [bank("p_hid0"), bank("p_hid1")]
            p_gb = [bank("p_gb0"), bank("p_gb1")]
            p_out = bank("p_out")
            p_z = bank("p_z")
            p_gt = c3.enter_context(nc.psum_tensor("p_gt", [P, 1024], BF16))
            staged = sem3("gate_chunk_ready")
            gflip = sem3("gates_flipped")
            g_rdy = sem3("gates_T_ready")
            h_sum = sem3("hid_summed")
            h_rdy = sem3("hid_ready")
            b_sum = sem3("gate_spread")
            hg_rdy = sem3("hid_gated")
            hg_used = sem3("hid_gated_used")
            out_sum = sem3("expert_out_summed")
            z_rdy = sem3("expert_out_ready")
            z_sum = sem3("folded")
            y_rdy = sem3("y_ready")
            CHUNKS = B * NCH
            with nc.Block() as block:
                @block.gpsimd
                def _(pool):
                    with pool.Fori(0, CHUNKS) as it:
                        pool.wait_ge(gflip, it)
                        nc.gpsimd.tensor_copy(gst[:], gates[:, bass.ds(it * 4, 4), :]).then_inc(staged, 1)

                @block.tensor
                def _(pe):
                    mm = nc.tensor.matmul

                    def flip_gates(it):
                        pe.wait_ge(g_rdy, it)
                        pe.wait_ge(staged, it + 1)
                        pe.sem_inc(carrier, 1)
                        for j in range(4):
                            m = nc.tensor.transpose(p_gt[0:3 * EXP, j * TM:j * TM + TM], gst[:, j, :],
                                                    k.ident_bf[0:TM, 0:TM])
                        m.then_inc(gflip, 1)

                    with pe.Fori(0, CHUNKS // 2) as it2:
                        for i in range(2):
                            it = it2 * 2 + i
                            flip_gates(it)
                            at = bass.ds(it * CH, CH)

                            def first(e):
                                pe.wait_ge(h_rdy, it * EXP + e - (1 if e else 0))
                                for a, xs in enumerate((x_hm, x_hm, x_hl)):
                                    m = mm(p_hid[e % 2][:, 0:CH], w1l[:, a, e, :], xs[:, at], start=(a == 0), stop=(a == 2))
                                m.then_inc(h_sum, 1)
                                if e == 0:
                                    pe.wait_ge(g_rdy, it + 1)
                                pe.wait_ge(hg_rdy, it * EXP + e - (1 if e else 0))
                                mm(p_gb[e % 2][:, 0:CH], sel[:, e, :], gT[i][:], start=True, stop=True).then_inc(b_sum, 1)

                            def second(e):
                                pe.wait_ge(hg_rdy, it * EXP + e + 1)
                                o = (e % 2) * C
                                if e == 0:
                                    pe.wait_ge(z_rdy, it)
                                    pe.sem_inc(carrier, 1)
                                    for a in range(3):
                                        mm(p_out[0:C, 0:CH], b2l[:, a, :], gT[i][:], start=(a == 0), stop=False)
                                m = mm(p_out[o:o + C, 0:CH], w2f[:, e, :], hg[:, e % 4, :], start=(e == 1), stop=(e >= EXP - 2))
                                m.then_inc(hg_used, 1)

                            first(0)
                            first(1)
                            for e in range(EXP):
                                if e + 2 < EXP:
                                    first(e + 2)
                                second(e)
                            pe.wait_ge(z_rdy, it + 1)
                            pe.wait_ge(y_rdy, it)
                            for j in range(4):
                                m = mm(p_z[0:TM, j * C:j * C + C], zs[:, j * TM:j * TM + TM], fold[:], start=True, stop=True)
                            m.then_inc(z_sum, 1)

                @block.scalar
                def _(act):
                    a = nc.scalar.activation
                    with act.Fori(0, CHUNKS // 2) as it2:
                        for i in range(2):
                            it = it2 * 2 + i
                            act.wait_ge(gflip, it + 1)
                            act.wait_ge(hg_used, it2 * (2 * EXP))
                            a(gT[i][:], p_gt[0:3 * EXP, 0:CH], ACT.Identity).then_inc(g_rdy, 1)
                            for e in range(EXP):
                                act.wait_ge(h_sum, it * EXP + e + 1)
                                act.wait_ge(hg_rdy, it * EXP + e - (1 if e else 0))
                                a(hid[:, e % 2, :], p_hid[e % 2][:, 0:CH], ACT.Relu, bias=b1t[:, e:e + 1]).then_inc(h_rdy, 1)
                            act.wait_ge(hg_used, it * EXP + EXP)
                            act.wait_ge(z_sum, it)
                            a(zs[:], p_out[:, 0:CH], ACT.Identity).then_inc(z_rdy, 1)

                @block.vector
                def _(dve):
                    v = nc.vector
                    with dve.Fori(0, CHUNKS // 2) as it2:
                        for i in range(2):
                            it = it2 * 2 + i
                            for e in range(EXP):
                                dve.wait_ge(h_rdy, it * EXP + e + 1)
                                dve.wait_ge(b_sum, it * EXP + e + 1)
                                dve.wait_ge(hg_used, it * EXP + max(0, e - 3))
                                v.tensor_tensor(hg[:, e % 4, :], p_gb[e % 2][:, 0:CH], hid[:, e % 2, :],
                                                ALU.mult).then_inc(hg_rdy, 1)
                            dve.wait_ge(z_sum, it + 1)
                            v.tensor_tensor(y_tm[:, bass.ds(it * 4, 4), :], x_tm[:, bass.ds(it * 4, 4), :],
                                            p_z[0:TM, 0:4 * C].rearrange("p (t c) -> p t c", c=C), ALU.add).then_inc(y_rdy, 1)

        with ExitStack() as c4:
            norm = Norm(k, c4, "norm2")
            final = Norm(k, c4, "norm3")
            out_done = c4.enter_context(nc.semaphore("out_stored"))
            with nc.Block() as block:
                @block.scalar
                def _(act):
                    norm.scalar(act, y_tm)
                    final.scalar(act, y_tm)

                @block.vector
                def _(dve):
                    v = nc.vector

                    def affine(b):
                        full = [TM, NT, C]
                        y = y_tm[:, b * NT:b * NT + NT, :]
                        norm.step(v.tensor_tensor(y, y, gamma[:].unsqueeze(1).to_broadcast(full), ALU.mult))
                        norm.step(v.tensor_tensor(y, y, beta[:].unsqueeze(1).to_broadcast(full), ALU.add))
                        norm.step(v.tensor_tensor(y, y, x_tm[:, b * NT:b * NT + NT, :], ALU.add))

                    norm.vector(dve, y_tm, after=affine)
                    final.vector(dve, y_tm)

                @block.sync
                def _(sp):
                    for b in range(B):
                        sp.wait_ge(final.done, b + 1)
                        sp.dma_start(k.out[b].rearrange("(t p) c -> p t c", p=TM),
                                     y_tm[:, b * NT:b * NT + NT, :]).then_inc(out_done, 16)
                    sp.wait_ge(out_done, 16 * B)


def constants():
    p = np.arange(P)
    weight = np.zeros((P, 2), np.float32)
    weight[p, p % 2] = np.exp2(p - 64.0)
    select = np.zeros((3, EXP, EXP, FF), np.float32)
    for e in range(EXP):
        select[:, e, e, :] = 1.0
    bf16 = mybir.dt.np(BF16)
    return {
        "c_ident": np.eye(P, dtype=np.float32),
        "c_index": np.tile(np.arange(P, dtype=np.float32), (P, 1)),
        "c_weight": weight,
        "c_head_sum": np.kron(np.eye(H), np.ones((HD, HD))).astype(np.float32),
        "c_ones": np.ones((3, NP), bf16),
        "c_select": select.reshape(3 * EXP, EXP, FF).astype(bf16),
    }


def build(nc, io, out):
    with ExitStack() as ctx:
        k = Core(nc, io, out, ctx)
        setup_phase(k)
        tok_phase(k)
        maximum_phase(k)
        attention_phase(k)
        project_phase(k)
        moe_phase(k)


def kernel(**inputs):
    import concourse.bacc as bacc
    from concourse.bass_utils import run_bass_kernel_spmd

    nc = bacc.Bacc("TRN2", target_bir_lowering=False, num_devices=1)
    arrays, io = {}, {}
    for name, a in {**inputs, **constants()}.items():
        a = np.ascontiguousarray(a)
        arrays[f"in_{name}"] = a
        io[name] = nc.dram_tensor(f"in_{name}", a.shape, mybir.dt.from_np(a.dtype), kind="ExternalInput").ap()
    out = nc.dram_tensor("out_0", (B, N, C), F32, kind="ExternalOutput").ap()
    build(nc, io, out)
    r = run_bass_kernel_spmd(nc, [arrays], core_ids=[0])
    return r.results[0]["out_0"]
```

```python
from contextlib import ExitStack

import numpy as np

import concourse.bass as bass
from concourse import mybir

ALU = mybir.AluOpType
ACT = mybir.ActivationFunctionType
AX = mybir.AxisListType
F32 = mybir.dt.float32
BF16 = mybir.dt.bfloat16
I32 = mybir.dt.int32
U32 = mybir.dt.uint32

B, C, HW, K = 4, 64, 56, 3
N = HW * HW
PADW = HW + 2
H, HD = 8, 8
E_EDGES = 16384
EXP, FF = 16, 128
P = 128

CH = 8 * HW
NCH = N // CH
TM = CH // 4
NT = N // TM
KT = -(-N // P)
NP = KT * P
TAIL = N - (KT - 1) * P
TPC = N - TAIL

TAPS_LO = [0, 1, 2, 6, 8]
TAPS_HI = [3, 4, 5, 7]
NSLOT = len(TAPS_LO)

BIAS_ROW = 9 * HD
SHIFT_ROW = BIAS_ROW + 3
GROUPS = 4
SCORE_LIMIT = 56.0
EPS = 1e-5
KEY_BASE = 63 * P




class Steps:

    def __init__(self, eng, sem):
        self.eng, self.sem, self.base, self.n = eng, sem, 0, 0

    def loop(self, base):
        self.base, self.n = base, 0

    def __call__(self, ins):
        self.n += 1
        ins.then_inc(self.sem, 1)
        self.eng.wait_ge(self.sem, self.base + self.n)


class Core:

    def __init__(self, nc, io, out, ctx):
        self.nc, self.io, self.out, self.ctx = nc, io, out, ctx

        def keep(name, shape, dt):
            return ctx.enter_context(nc.sbuf_tensor(name, shape, dt))

        def scratch(name, shape, dt):
            return nc.dram_tensor(name, shape, dt, kind="Internal").ap()

        self.w1 = keep("tok_w1", [P, NSLOT, C], F32)
        self.w2 = keep("tok_w2", [C, NSLOT, P], F32)
        self.w3 = keep("tok_w3", [P, NSLOT, C], F32)
        self.b1 = keep("tok_b1", [C, 1], F32)
        self.b2 = keep("tok_b2_half", [P, NSLOT], F32)
        self.b3 = keep("tok_b3", [C, 1], F32)
        self.wqk = keep("attn_wqk", [C, 2 * C], F32)
        self.bqk = keep("attn_bqk", [2 * C, 1], F32)
        self.wv = keep("attn_wv_bv", [C + 1, C], F32)
        self.eye_bo = keep("eye_bo", [C + 1, C], F32)
        self.wo = keep("attn_wo", [P, C], F32)
        self.ident = keep("ident", [P, P], F32)
        self.ident_bf = keep("ident_bf", [P, P], BF16)
        self.x_tm = keep("x_token_major", [TM, B * NT, C], F32)
        self.values = keep("values", [P, B * H, KT, HD + 1], F32)
        self.flag = keep("need_maximum", [1, 1], I32)
        self.d_qk = scratch("qk_parts", [3, 2, B * C, N], BF16)
        self.d_bias = scratch("bias_parts", [B * H, 3, NP], BF16)
        self.d_shift = scratch("shift_parts", [B * H, 3, NP], BF16)
        self.d_recip = scratch("denominator_recips", [B * H, N], F32)
        self.d_mix = scratch("mixed", [B * H, GROUPS, HD + 1, N], F32)


def setup_phase(k):
    nc, io = k.nc, k.io
    with ExitStack() as ctx:
        def sb(name, shape, dt):
            return ctx.enter_context(nc.sbuf_tensor(name, shape, dt))

        def sem(name):
            return ctx.enter_context(nc.semaphore(name))

        EC = E_EDGES // P
        PER = 10
        NB = -(-EC // PER)
        W = KT * 2
        w2raw = sb("w2_raw", [C, K * K * C], F32)
        b2raw = sb("b2_raw", [P, K * K], F32)
        tgt = sb("edge_target", [P, EC], I32)
        tlo = sb("target_lo", [P, EC], I32)
        thi = sb("target_hi", [P, EC], I32)
        tlof = sb("target_lo_f", [P, EC], F32)
        thif = sb("target_hi_f", [P, EC], F32)
        index = sb("index_row", [P, P], F32)
        weight = sb("edge_weight", [P, 2], F32)
        onelo = sb("one_hot_lo", [P, EC, P], BF16)
        onehi = sb("one_hot_hi", [P, EC, KT], BF16)
        rhs = sb("weighted_hi", [P, EC, KT, 2], BF16)
        keyi = sb("key_bits", [P, EC, W], I32)
        keyf = onelo[:, :, 0:2 * W].bitcast(F32)
        best = sb("best_key", [P, KT], F32)
        has = sb("has_edge", [P, KT], F32)
        edge = sb("edge_index", [P, KT], U32)
        attr = sb("edge_attr", [P, KT, 3], F32)
        we = sb("edge_w", [P, 3 * H], F32)
        be = sb("edge_b", [P, H], F32)
        term = sb("bias_term", [P, KT, H], F32)
        bias = sb("key_bias", [P, KT, H], F32)
        masked = sb("bias_masked", [P, KT, H], F32)
        bmax = sb("bias_max", [P, H], F32)
        gmax = sb("bias_max_all", [P, H], F32)
        parts = sb("bias_parts_tm", [P, KT, H, 3], BF16)
        rows = sb("bias_rows", [3 * H, NP], BF16)
        zero = sb("zero_rows", [3, NP], BF16)
        ps = [ctx.enter_context(nc.psum_tensor(f"edge_ps{i}", [P, 512], F32)) for i in range(2)]
        pt = [ctx.enter_context(nc.psum_tensor(f"bias_ps{i}", [P, 1024], BF16)) for i in range(4)]

        loaded = sem("setup_loaded")
        edges_in = sem("edges_loaded")
        onehot = sem("one_hots_ready")
        counted = sem("edges_counted")
        taken = sem("counts_taken")
        indexed = sem("edge_index_ready")
        gathered = sem("attrs_gathered")
        bmax_own = sem("bias_max_ready")
        bmax_all = sem("bias_max_shared")
        split = sem("bias_split")
        turned = sem("bias_turned")
        rowed = sem("bias_rows_ready")
        written = sem("setup_written")
        zeroed = sem("zero_rows_ready")
        dve_step = sem("setup_dve_step")
        n_load = [0]

        with nc.Block() as block:
            @block.sync
            def _(sp):
                ei = io["L0_attn_edge_index"]
                sp.dma_start(tgt[:], ei[1].rearrange("(p c) -> p c", p=P)).then_inc(edges_in, 16)
                sp.dma_start(index[:], io["c_index"]).then_inc(edges_in, 16)
                sp.dma_start(weight[:], io["c_weight"]).then_inc(edges_in, 16)
                sp.dma_start(we[:], io["L0_attn_We"].rearrange("a h -> (a h)").partition_broadcast(P)).then_inc(edges_in, 16)
                sp.dma_start(be[:], io["L0_attn_be"].partition_broadcast(P)).then_inc(edges_in, 16)

                def load(dst, src):
                    n_load[0] += 16
                    sp.dma_start(dst, src).then_inc(loaded, 16)

                for w, name in ((k.w1, "L0_tok_W1"), (k.w3, "L0_tok_W3")):
                    by_tap = io[name].rearrange("(c t) m -> t c m", t=K * K)
                    for s, t in enumerate(TAPS_LO):
                        load(w[0:C, s, :], by_tap[t])
                    for s, t in enumerate(TAPS_HI):
                        load(w[C:P, s, :], by_tap[t])
                load(w2raw[:], io["L0_tok_W2"])
                for half in range(2):
                    load(b2raw[half * C:half * C + C, :], io["L0_tok_b2"].rearrange("(c t) -> c t", t=K * K))
                load(k.b1[:], io["L0_tok_b1"].unsqueeze(1))
                load(k.b3[:], io["L0_tok_b3"].unsqueeze(1))
                for i, s in enumerate("qk"):
                    load(k.wqk[:, i * C:i * C + C], io["L0_attn_W" + s])
                    load(k.bqk[i * C:i * C + C, :], io["L0_attn_b" + s].unsqueeze(1))
                load(k.wv[0:C, :], io["L0_attn_Wv"])
                load(k.wv[C:C + 1, :], io["L0_attn_bv"].unsqueeze(0))
                load(k.eye_bo[0:C, :], io["c_ident"][0:C, 0:C])
                load(k.eye_bo[C:C + 1, :], io["L0_attn_bo"].unsqueeze(0))
                for half in range(2):
                    load(k.wo[half * C:half * C + C, :], io["L0_attn_Wo"])
                load(k.ident[:], io["c_ident"])
                sp.wait_ge(zeroed, 1)
                for bh in range(B * H):
                    sp.dma_start(k.d_shift[bh], zero[:]).then_inc(written, 16)
                sp.wait_ge(rowed, 1)
                for b in range(B):
                    sp.dma_start(k.d_bias[b * H:b * H + H].rearrange("h a n -> (h a) n"), rows[:]).then_inc(written, 16)
                sp.wait_ge(written, 16 * (B * H + B))

            @block.gpsimd
            def _(pool):
                nc.gpsimd.memset(zero[:], 0.0).then_inc(zeroed, 1)
                pool.wait_ge(indexed, 1)
                for t in range(KT):
                    nc.gpsimd.indirect_dma_start(
                        attr[:, t, :], None, io["L0_attn_edge_attr"],
                        bass.IndirectOffsetOnAxis(ap=edge[:, t:t + 1], axis=0)).then_inc(gathered, 16)
                pool.wait_ge(bmax_own, 1)
                nc.gpsimd.partition_all_reduce(gmax[:], bmax[:], P, bass.bass_isa.ReduceOp.max).then_inc(bmax_all, 1)

            @block.tensor
            def _(pe):
                pe.wait_ge(onehot, 1)
                for c in range(EC):
                    g = c // PER
                    if c % PER == 0 and g >= 2:
                        pe.wait_ge(taken, g - 1)
                    o = (c % PER) * W
                    mm = nc.tensor.matmul(ps[g % 2][:, o:o + W], onelo[:, c, :],
                                          rhs[:, c, :, :].rearrange("p h r -> p (h r)"), start=True, stop=True)
                    if c % PER == PER - 1 or c == EC - 1:
                        mm.then_inc(counted, 1)
                pe.wait_ge(split, 1)
                for t in range(KT):
                    tr = nc.tensor.transpose(pt[t // 8][0:3 * H, (t % 8) * P:(t % 8 + 1) * P],
                                             parts[:, t, :, :].rearrange("p h a -> p (h a)"), k.ident_bf[:])
                tr.then_inc(turned, 1)

            @block.vector
            def _(dve):
                v = nc.vector
                step = Steps(dve, dve_step)
                dve.wait_ge(edges_in, 16 * 5)
                step(v.tensor_scalar(tlo[:], tgt[:], P - 1, None, ALU.bitwise_and))
                step(v.tensor_scalar(thi[:], tgt[:], 7, None, ALU.logical_shift_right))
                step(v.tensor_copy(tlof[:], tlo[:]))
                step(v.tensor_copy(thif[:], thi[:]))
                step(v.tensor_tensor(onehi[:], index[:, 0:KT].unsqueeze(1).to_broadcast([P, EC, KT]),
                                     thif[:].unsqueeze(2).to_broadcast([P, EC, KT]), ALU.is_equal))
                for r in range(2):
                    step(v.tensor_scalar(rhs[:, :, :, r], onehi[:], weight[:, r:r + 1], None, ALU.mult))
                v.tensor_tensor(onelo[:], index[:].unsqueeze(1).to_broadcast([P, EC, P]),
                                tlof[:].unsqueeze(2).to_broadcast([P, EC, P]), ALU.is_equal).then_inc(onehot, 1)
                for g in range(NB):
                    n = min(PER, EC - g * PER)
                    dve.wait_ge(counted, g + 1)
                    v.tensor_scalar(keyi[:, g * PER:g * PER + n, :].rearrange("p c w -> p (c w)"),
                                    ps[g % 2][:, 0:n * W].bitcast(I32), 16, 0xFF80,
                                    ALU.logical_shift_right, ALU.bitwise_and).then_inc(taken, 1)
                dve.wait_ge(taken, NB)
                step(v.tensor_tensor(keyf, keyi[:], index[:].unsqueeze(2).to_broadcast([P, EC, W]), ALU.add))
                step(v.tensor_reduce(best[:], keyf.rearrange("p c (h r) -> p h c r", r=2), AX.XY, ALU.max))
                step(v.tensor_scalar(has[:], best[:], float(KEY_BASE), None, ALU.is_ge))
                v.tensor_scalar(edge[:], best[:], float(-KEY_BASE), 0.0, ALU.add, ALU.max).then_inc(indexed, 1)
                dve.wait_ge(loaded, n_load[0])
                for s, t in enumerate(TAPS_LO):
                    step(v.tensor_copy(k.w2[:, s, 0:C], w2raw[:, t::K * K]))
                    step(v.tensor_scalar(k.b2[0:C, s:s + 1], b2raw[0:C, t:t + 1], 0.5, None, ALU.mult))
                for s, t in enumerate(TAPS_HI):
                    step(v.tensor_copy(k.w2[:, s, C:P], w2raw[:, t::K * K]))
                    step(v.tensor_scalar(k.b2[C:P, s:s + 1], b2raw[C:P, t:t + 1], 0.5, None, ALU.mult))
                step(v.memset(k.w1[C:P, NSLOT - 1, :], 0.0))
                step(v.memset(k.w2[:, NSLOT - 1, C:P], 0.0))
                step(v.memset(k.w3[C:P, NSLOT - 1, :], 0.0))
                step(v.memset(k.b2[C:P, NSLOT - 1:NSLOT], 0.0))
                step(v.tensor_scalar(k.w3[:], k.w3[:], 0.5, None, ALU.mult))
                step(v.tensor_scalar(k.wqk[:, 0:C], k.wqk[:, 0:C], float(HD) ** -0.5, None, ALU.mult))
                step(v.tensor_scalar(k.bqk[0:C, :], k.bqk[0:C, :], float(HD) ** -0.5, None, ALU.mult))
                step(v.tensor_copy(k.ident_bf[:], k.ident[:]))
                dve.wait_ge(gathered, 16 * KT)
                for a in range(3):
                    w = we[:, a * H:a * H + H].unsqueeze(1).to_broadcast([P, KT, H])
                    x = attr[:, :, a:a + 1].to_broadcast([P, KT, H])
                    step(v.tensor_tensor((term if a else bias)[:], x, w, ALU.mult))
                    if a:
                        step(v.tensor_tensor(bias[:], bias[:], term[:], ALU.add))
                step(v.tensor_tensor(bias[:], bias[:], be[:].unsqueeze(1).to_broadcast([P, KT, H]), ALU.add))
                step(v.tensor_tensor(bias[:], bias[:], has[:].unsqueeze(2).to_broadcast([P, KT, H]), ALU.mult))
                step(v.tensor_copy(masked[:], bias[:]))
                step(v.memset(masked[TAIL:P, KT - 1, :], -3.0e38))
                v.tensor_reduce(bmax[:], masked[:].rearrange("p t h -> p h t"), AX.X, ALU.max).then_inc(bmax_own, 1)
                dve.wait_ge(bmax_all, 1)
                step(v.tensor_tensor(bias[:], bias[:], gmax[:].unsqueeze(1).to_broadcast([P, KT, H]), ALU.subtract))
                step(v.tensor_copy(parts[:, :, :, 0], bias[:]))
                step(v.tensor_tensor(bias[:], bias[:], parts[:, :, :, 0], ALU.subtract))
                step(v.tensor_copy(parts[:, :, :, 1], bias[:]))
                step(v.tensor_tensor(bias[:], bias[:], parts[:, :, :, 1], ALU.subtract))
                v.tensor_copy(parts[:, :, :, 2], bias[:]).then_inc(split, 1)
                dve.wait_ge(turned, 1)
                for g in range(4):
                    n = min(1024, NP - 1024 * g)
                    step(v.tensor_copy(rows[:, 1024 * g:1024 * g + n], pt[g][0:3 * H, 0:n]))
                v.memset(k.values[:], 0.0).then_inc(rowed, 1)


def tok_phase(k):
    nc, io = k.nc, k.io
    with ExitStack() as ctx:
        def sb(name, shape, dt):
            return ctx.enter_context(nc.sbuf_tensor(name, shape, dt))

        def bank(name):
            return ctx.enter_context(nc.psum_tensor(name, [P, 512], F32))

        def sem(name):
            return ctx.enter_context(nc.semaphore(name))

        raw = sb("image", [P, N], F32)
        pad_row = sb("padded_and_a_row_on", [P, PADW, PADW], F32)
        pad_col = sb("padded_and_a_column_on", [P, PADW, PADW], F32)
        h1 = sb("hidden", [C, CH], F32)
        th = sb("gate_tanh", [P, 2, CH], F32)
        ts = sb("gated_taps", [P, NSLOT, CH], F32)
        hT = sb("h_chunk", [C + 1, CH], F32)
        hTb = sb("h_image", [C + 1, NP], F32)
        part = sb("qk_parts_chunk", [P, 3, CH], BF16)
        rest = sb("qk_rest", [P, CH], F32)
        amax = sb("qk_abs_max", [P, B * NCH], F32)
        amax_b = sb("qk_abs_max_image", [P, B], F32)
        kmax = sb("k_abs_max", [C, B], F32)
        bound = sb("score_bound", [C, B], F32)
        head_sum = sb("head_sum", [C, C], F32)
        bmx = sb("bound_max", [C, 1], F32)
        bmx_all = sb("bound_max_all", [C, 1], F32)
        p_h1 = bank("p_h1")
        p_s = [bank("p_s0"), bank("p_s1")]
        p_h = bank("p_h")
        p_qk = bank("p_qk")
        p_tm = bank("p_tm")
        p_v = [bank("p_v0"), bank("p_v1")]

        img_in = sem("image_loaded")
        pad_zero = sem("padding_zeroed")
        padded = sem("image_padded")
        dve_pad = sem("image_padded_dve")
        h1_sum = sem("hidden_summed")
        h1_rdy = sem("hidden_ready")
        s_sum = sem("gate_summed")
        th_rdy = sem("tanh_ready")
        ts_rdy = sem("gated_ready")
        h_sum = sem("h_summed")
        h_rdy = sem("h_ready")
        hc_rdy = sem("h_chunk_ready")
        qk_sum = sem("qk_summed")
        hi_rdy = sem("hi_ready")
        r1_rdy = sem("rest_ready")
        mid_rdy = sem("mid_ready")
        lo_rdy = sem("lo_ready")
        stored = sem("qk_stored")
        tm_sum = sem("token_major_summed")
        tm_rdy = sem("token_major_ready")
        v_sum = sem("values_summed")
        v_rdy = sem("values_ready")
        step_s = sem("ones_set")
        am_rdy = sem("abs_max_of_chunk_ready")
        kmv = sem("k_max_moved")
        bsum = sem("bounds_summed")
        ball = sem("bound_shared")
        bown = sem("abs_max_ready")
        bmul = sem("bound_products_ready")
        bone = sem("bound_of_heads_ready")
        const_in = sem("head_sum_loaded")
        flagged = sem("flag_ready")

        NV = -(-KT // 8)

        def window(buf, c, tap):
            ki, kj = tap // K, tap % K
            return buf[:, bass.ds(c * 8 + ki, 8), kj:kj + HW]

        SLOT_BUF = [pad_row] * 3 + [pad_col, pad_row]

        with nc.Block() as block:
            @block.sync
            def _(sp):
                sp.sem_inc(stored, 1)
                sp.dma_start(head_sum[:], io["c_head_sum"]).then_inc(const_in, 16)
                with sp.Fori(0, B) as b:
                    sp.wait_ge(padded, b * 2 + 2)
                    sp.wait_ge(dve_pad, b * 2 + 2)
                    for half in range(2):
                        sp.dma_start(raw[half * C:half * C + C, :],
                                     io["x"][b].rearrange("c h w -> c (h w)")).then_inc(img_in, 16)
                    with sp.Fori(0, NCH) as c:
                        it = b * NCH + c
                        sp.wait_ge(lo_rdy, it + 2)
                        for j in range(3):
                            for i in range(2):
                                sp.dma_start(k.d_qk[j, i, bass.ds(b * C, C), bass.ds(c * CH, CH)],
                                             part[i * C:i * C + C, j, :]).then_inc(stored, 16)
                sp.wait_ge(bown, 1)
                sp.dma_start(kmax[:], amax_b[C:P, :]).then_inc(kmv, 16)
                sp.wait_ge(stored, 16 * 6 * B * NCH + 1)

            @block.gpsimd
            def _(pool):
                pool.sem_inc(lo_rdy, 1)
                step = Steps(pool, padded)
                step(nc.gpsimd.memset(pad_row[:], 0.0))
                step(nc.gpsimd.memset(hTb[C:C + 1, :], 1.0))
                with pool.Fori(0, B * NCH) as it:
                    pool.wait_ge(stored, it * 96 + 1)
                    pool.wait_ge(mid_rdy, it + 1)
                    nc.gpsimd.tensor_tensor(part[:, 2, :], rest[:], part[:, 1, :], ALU.subtract).then_inc(lo_rdy, 1)
                pool.wait_ge(bone, 1)
                nc.gpsimd.partition_all_reduce(bmx_all[:], bmx[:], C, bass.bass_isa.ReduceOp.max).then_inc(ball, 1)

            @block.tensor
            def _(pe):
                pe.sem_inc(h_sum, 1)
                pe.sem_inc(s_sum, 1)
                pe.sem_inc(qk_sum, 1)
                pe.sem_inc(tm_sum, 1)
                pe.sem_inc(v_sum, 1)
                mm = nc.tensor.matmul
                pe.wait_ge(step_s, 1)
                with pe.Fori(0, B) as b:
                    with pe.Fori(0, NCH) as c:
                        it = b * NCH + c
                        pe.wait_ge(padded, b * 2 + 4)
                        pe.wait_ge(dve_pad, b * 2 + 4)
                        pe.wait_ge(h1_rdy, it + 1)
                        for s in range(NSLOT):
                            i = mm(p_h1[0:C, 0:CH], k.w1[:, s, :], window(SLOT_BUF[s], c, TAPS_LO[s]),
                                   start=(s == 0), stop=(s == NSLOT - 1))
                        i.then_inc(h1_sum, 1)
                        pe.wait_ge(h1_rdy, it + 2)

                        def gate(s):
                            pe.wait_ge(th_rdy, it * NSLOT + max(0, s - 1) + 1)
                            mm(p_s[s % 2][:, 0:CH], k.w2[:, s, :], h1[:], start=True, stop=True).then_inc(s_sum, 1)

                        def mix(s):
                            if s == 0:
                                pe.wait_ge(h_rdy, it + 1)
                            pe.wait_ge(ts_rdy, it * NSLOT + s + 2)
                            i = mm(p_h[0:C, 0:CH], k.w3[:, s, :], ts[:, s, :],
                                   start=(s == 0), stop=(s == NSLOT - 1))
                            if s == NSLOT - 1:
                                i.then_inc(h_sum, 1)

                        gate(0)
                        gate(1)
                        for s in range(2, NSLOT):
                            gate(s)
                            mix(s - 2)
                        mix(NSLOT - 2)
                        mix(NSLOT - 1)
                        pe.wait_ge(hc_rdy, it + 1)
                        pe.wait_ge(r1_rdy, it + 1)
                        mm(p_qk[:, 0:CH], k.wqk[:], hT[0:C, :], start=True, stop=True).then_inc(qk_sum, 1)
                        pe.wait_ge(tm_rdy, it + 1)
                        for j in range(4):
                            i = mm(p_tm[0:TM, j * C:j * C + C], hT[:, j * TM:j * TM + TM], k.eye_bo[:],
                                   start=True, stop=True)
                        i.then_inc(tm_sum, 1)
                    pe.wait_ge(h_rdy, b * NCH + NCH + 1)
                    for t in range(KT):
                        g = t // 8
                        if t % 8 == 0:
                            pe.wait_ge(v_rdy, b * NV + max(0, g - 1) + 1)
                        m = min(P, N - t * P)
                        i = mm(p_v[g % 2][0:m, (t % 8) * C:(t % 8) * C + C], hTb[:, t * P:t * P + m], k.wv[:],
                               start=True, stop=True)
                        if t % 8 == 7 or t == KT - 1:
                            i.then_inc(v_sum, 1)
                pe.wait_ge(bmul, 1)
                pe.wait_ge(const_in, 16)
                mm(p_h1[0:C, 0:B], head_sum[:], bound[:], start=True, stop=True).then_inc(bsum, 1)

            @block.scalar
            def _(act):
                act.sem_inc(h1_rdy, 1)
                act.sem_inc(th_rdy, 1)
                act.sem_inc(h_rdy, 1)
                a = nc.scalar.activation
                with act.Fori(0, B) as b:
                    act.wait_ge(img_in, b * 32 + 32)
                    act.wait_ge(h_sum, b * NCH + 1)
                    act.wait_ge(padded, 2)
                    x = raw[:].rearrange("p (r c) -> p r c", r=HW)
                    a(pad_row[0:C, 1:HW + 1, 1:HW + 1], x[0:C], ACT.Copy).then_inc(padded, 1)
                    a(pad_row[C:P, 0:HW, 1:HW + 1], x[C:P], ACT.Copy).then_inc(padded, 1)
                    with act.Fori(0, NCH) as c:
                        it = b * NCH + c
                        act.wait_ge(h1_sum, it + 1)
                        act.wait_ge(s_sum, it * NSLOT + 1)
                        a(h1[:], p_h1[0:C, 0:CH], ACT.Relu, bias=k.b1[:]).then_inc(h1_rdy, 1)
                        for s in range(NSLOT):
                            act.wait_ge(s_sum, it * NSLOT + s + 2)
                            act.wait_ge(ts_rdy, it * NSLOT + max(0, s - 1) + 1)
                            a(th[:, s % 2, :], p_s[s % 2][:, 0:CH], ACT.Tanh, bias=k.b2[:, s:s + 1],
                              scale=0.5).then_inc(th_rdy, 1)
                        act.wait_ge(h_sum, it + 2)
                        act.wait_ge(qk_sum, it + 1)
                        act.wait_ge(tm_sum, it + 1)
                        act.wait_ge(v_sum, b * NV + 1)
                        a(hT[0:C, :], p_h[0:C, 0:CH], ACT.Identity, bias=k.b3[:]).then_inc(hc_rdy, 1)
                        a(hTb[0:C, bass.ds(c * CH, CH)], p_h[0:C, 0:CH], ACT.Identity, bias=k.b3[:]).then_inc(h_rdy, 1)
                        act.wait_ge(qk_sum, it + 2)
                        act.wait_ge(stored, it * 96 + 1)
                        act.wait_ge(am_rdy, it + 1)
                        a(part[:, 0, :], p_qk[:, 0:CH], ACT.Identity, bias=k.bqk[:]).then_inc(hi_rdy, 1)

            @block.vector
            def _(dve):
                dve.sem_inc(ts_rdy, 1)
                dve.sem_inc(r1_rdy, 1)
                dve.sem_inc(tm_rdy, 1)
                dve.sem_inc(v_rdy, 1)
                dve.sem_inc(am_rdy, 1)
                v = nc.vector
                v.memset(hT[C:C + 1, :], 1.0).then_inc(step_s, 1)
                v.memset(k.values[:, :, 0:KT - 1, HD], 1.0).then_inc(step_s, 1)
                v.memset(k.values[0:TAIL, :, KT - 1, HD], 1.0).then_inc(step_s, 1)
                v.memset(pad_col[:], 0.0).then_inc(dve_pad, 2)
                dve.wait_ge(dve_pad, 2)
                with dve.Fori(0, B) as b:
                    dve.wait_ge(img_in, b * 32 + 32)
                    dve.wait_ge(h_sum, b * NCH + 1)
                    x = raw[:].rearrange("p (r c) -> p r c", r=HW)
                    v.tensor_copy(pad_col[0:C, 1:HW + 1, 1:HW + 1], x[0:C]).then_inc(dve_pad, 1)
                    v.tensor_copy(pad_col[C:P, 1:HW + 1, 0:HW], x[C:P]).then_inc(dve_pad, 1)
                    with dve.Fori(0, NCH) as c:
                        it = b * NCH + c
                        dve.wait_ge(dve_pad, b * 2 + 4)
                        dve.wait_ge(padded, b * 2 + 4)
                        for s in range(NSLOT):
                            dve.wait_ge(th_rdy, it * NSLOT + s + 2)
                            if s == 0:
                                dve.wait_ge(h_sum, it + 1)
                            v.scalar_tensor_tensor(
                                out=ts[:, s, :].rearrange("p (r c) -> p r c", r=8),
                                in0=th[:, s % 2, :].rearrange("p (r c) -> p r c", r=8), scalar=1.0,
                                in1=window(SLOT_BUF[s], c, TAPS_LO[s]), op0=ALU.add,
                                op1=ALU.mult).then_inc(ts_rdy, 1)
                        dve.wait_ge(tm_sum, it + 2)
                        v.tensor_copy(k.x_tm[:, bass.ds(it * 4, 4), :].rearrange("p t c -> p (t c)"),
                                      p_tm[0:TM, 0:4 * C]).then_inc(tm_rdy, 1)
                        dve.wait_ge(hi_rdy, it + 1)
                        dve.wait_ge(lo_rdy, it + 1)
                        v.scalar_tensor_tensor(out=rest[:], in0=p_qk[:, 0:CH], scalar=k.bqk[:], in1=part[:, 0, :],
                                               op0=ALU.add, op1=ALU.subtract).then_inc(r1_rdy, 1)
                        dve.wait_ge(stored, it * 96 + 1)
                        dve.wait_ge(r1_rdy, it + 2)
                        v.tensor_copy(part[:, 1, :], rest[:]).then_inc(mid_rdy, 1)
                        v.tensor_reduce(amax[:, bass.ds(it, 1)], part[:, 0, :], AX.X, ALU.max,
                                        apply_absolute_value=True).then_inc(am_rdy, 1)
                    for g in range(NV):
                        dve.wait_ge(v_sum, b * NV + g + 2)
                        n = min(8, KT - 8 * g)
                        m = P if n == 8 else TAIL
                        v.tensor_copy(
                            k.values[0:m, bass.ds(b * H, H), 8 * g:8 * g + n, 0:HD],
                            p_v[g % 2][0:m, 0:n * C].rearrange("p (t h d) -> p h t d", h=H, d=HD)).then_inc(v_rdy, 1)
                dve.wait_ge(am_rdy, B * NCH + 1)
                v.tensor_reduce(amax_b[:], amax[:].rearrange("p (b c) -> p b c", c=NCH), AX.X,
                                ALU.max).then_inc(bown, 1)
                dve.wait_ge(bown, 1)
                dve.wait_ge(kmv, 16)
                v.tensor_tensor(bound[:], amax_b[0:C, :], kmax[:], ALU.mult).then_inc(bmul, 1)
                dve.wait_ge(bsum, 1)
                v.tensor_reduce(bmx[:], p_h1[0:C, 0:B], AX.X, ALU.max).then_inc(bone, 1)
                dve.wait_ge(ball, 1)
                v.tensor_scalar(k.flag[:], bmx_all[0:1, :], SCORE_LIMIT, None, ALU.is_gt).then_inc(flagged, 1)
                dve.wait_ge(flagged, 1)


class Stage:

    LOADS = 8

    def __init__(self, k, ctx, name, n):
        nc = k.nc
        self.k = k
        self.q = [ctx.enter_context(nc.sbuf_tensor(f"{name}_q{i}", [P, NP], BF16)) for i in range(n)]
        self.kk = [ctx.enter_context(nc.sbuf_tensor(f"{name}_k{i}", [P, NP], BF16)) for i in range(n)]
        self.const_in = ctx.enter_context(nc.semaphore(f"{name}_constants"))
        self.cleared = ctx.enter_context(nc.semaphore(f"{name}_cleared"))

    def clear(self):
        for t in self.q + self.kk:
            self.k.nc.gpsimd.memset(t[:], 0.0).then_inc(self.cleared, 1)

    def constants(self, sp):
        sp.wait_ge(self.cleared, 2 * len(self.q))
        for q, kk in zip(self.q, self.kk):
            sp.dma_start(q[BIAS_ROW:SHIFT_ROW, :], self.k.io["c_ones"]).then_inc(self.const_in, 16)
            sp.dma_start(kk[SHIFT_ROW:SHIFT_ROW + 3, :], self.k.io["c_ones"]).then_inc(self.const_in, 16)

    def load(self, sp, i, bh, sem):
        k = self.k
        r = 3 * HD
        for a in range(3):
            src = k.d_qk[a, 0, bass.ds(bh * HD, HD), :].unsqueeze(0).to_broadcast([3, HD, N])
            sp.dma_start(self.q[i][a * r:a * r + r, 0:N], src).then_inc(sem, 16)
            src = k.d_qk[:, 1, bass.ds(bh * HD, HD), :]
            sp.dma_start(self.kk[i][a * r:a * r + r, 0:N], src).then_inc(sem, 16)
        sp.dma_start(self.kk[i][BIAS_ROW:SHIFT_ROW, 0:N],
                     k.d_bias[bass.ds(bh, 1), :, 0:N].rearrange("o a n -> (o a) n")).then_inc(sem, 16)
        sp.dma_start(self.q[i][SHIFT_ROW:SHIFT_ROW + 3, :],
                     k.d_shift[bass.ds(bh, 1)].rearrange("o a n -> (o a) n")).then_inc(sem, 16)


def maximum_phase(k):
    nc = k.nc
    with ExitStack() as ctx:
        def sem(name):
            return ctx.enter_context(nc.semaphore(name))

        def sb(name, shape, dt):
            return ctx.enter_context(nc.sbuf_tensor(name, shape, dt))

        stage = Stage(k, ctx, "max", 1)
        rowmax = sb("row_max", [P, KT], F32)
        parts = sb("shift_parts_tm", [P, 3, KT], BF16)
        rows = sb("shift_rows", [3 * KT, P], BF16)
        scores = ctx.enter_context(nc.psum_tensor("max_scores", [P, NCH, 512], F32))
        turned = ctx.enter_context(nc.psum_tensor("max_turned", [P, 1024], BF16))
        staged = sem("max_staged")
        scored = sem("max_scored")
        reduced = sem("max_reduced")
        split = sem("max_split")
        flipped = sem("max_flipped")
        rowed = sem("max_rowed")
        stored = sem("max_stored")
        one = sem("max_step")
        with nc.Block() as block:
            @block.gpsimd
            def _(pool):
                stage.clear()

            @block.sync
            def _(sp):
                sp.sem_inc(stored, 1)
                stage.constants(sp)
                sp.wait_ge(stage.const_in, 32)
                need = sp.value_load(k.flag[0:1, 0:1], min_val=0, max_val=1)
                with sp.If(need > 0):
                    with sp.Fori(0, B * H) as bh:
                        sp.wait_ge(split, bh + 1)
                        stage.load(sp, 0, bh, staged)
                        sp.wait_ge(rowed, bh + 1)
                        sp.dma_start(k.d_shift[bass.ds(bh, 1)].rearrange("o a (t p) -> (o a t) p", p=P),
                                     rows[:]).then_inc(stored, 16)
                    sp.wait_ge(stored, 16 * B * H + 1)

            @block.tensor
            def _(pe):
                pe.wait_ge(stage.const_in, 32)
                need = pe.value_load(k.flag[0:1, 0:1], min_val=0, max_val=1)
                with pe.If(need > 0):
                    with pe.Fori(0, B * H) as bh:
                        with pe.Fori(0, KT) as t:
                            pe.wait_ge(staged, bh * (16 * Stage.LOADS) + 16 * Stage.LOADS)
                            pe.wait_ge(reduced, bh * KT + t + 1)
                            for c in range(NCH):
                                mm = nc.tensor.matmul(scores[:, c, 0:CH], stage.q[0][:, bass.ds(t * P, P)],
                                                      stage.kk[0][:, c * CH:c * CH + CH], start=True, stop=True)
                            mm.then_inc(scored, 1)
                        pe.wait_ge(split, bh + 2)
                        pe.wait_ge(stage.const_in, 32)
                        nc.tensor.transpose(turned[0:3 * KT, 0:P], parts[:].rearrange("p a t -> p (a t)"),
                                            k.ident_bf[:]).then_inc(flipped, 1)

            @block.vector
            def _(dve):
                dve.sem_inc(split, 1)
                dve.sem_inc(reduced, 1)
                v = nc.vector
                step = Steps(dve, one)
                dve.wait_ge(stage.const_in, 32)
                need = dve.value_load(k.flag[0:1, 0:1], min_val=0, max_val=1)
                with dve.If(need > 0):
                    with dve.Fori(0, B * H) as bh:
                        with dve.Fori(0, KT) as t:
                            dve.wait_ge(scored, bh * KT + t + 1)
                            v.tensor_reduce(rowmax[:, bass.ds(t, 1)], scores[:, :, 0:CH], AX.XY,
                                            ALU.max).then_inc(reduced, 1)
                        dve.wait_ge(reduced, bh * KT + KT + 1)
                        step.loop(bh * 5)
                        step(v.tensor_scalar(rowmax[:], rowmax[:], -1.0, None, ALU.mult))
                        step(v.tensor_copy(parts[:, 0, :], rowmax[:]))
                        step(v.tensor_tensor(rowmax[:], rowmax[:], parts[:, 0, :], ALU.subtract))
                        step(v.tensor_copy(parts[:, 1, :], rowmax[:]))
                        step(v.tensor_tensor(rowmax[:], rowmax[:], parts[:, 1, :], ALU.subtract))
                        v.tensor_copy(parts[:, 2, :], rowmax[:]).then_inc(split, 1)
                        dve.wait_ge(stored, bh * 16 + 1)
                        dve.wait_ge(flipped, bh + 1)
                        v.tensor_copy(rows[:], turned[0:3 * KT, 0:P]).then_inc(rowed, 1)


def attention_phase(k):
    nc = k.nc
    UNIT = 2
    UNITS = (KT - 1) // UNIT
    AHEAD = 3
    RING = 6
    PAIRS = B * H // 2
    TAIL_EXP_AT, TAIL_AT = 2, 6
    BATCHES = (KT - 1) // GROUPS
    SPARE = RING * UNIT // GROUPS
    assert UNITS % AHEAD == 0 and UNITS % RING == 0 and BATCHES * GROUPS == UNITS * UNIT

    def unit_of(g):
        return (g * GROUPS + GROUPS - 1) // UNIT

    def freed_by(u):
        return ((u - RING) * UNIT + UNIT - 1) // GROUPS + 1
    with ExitStack() as ctx:
        def sem(name):
            return ctx.enter_context(nc.semaphore(name))

        def sb(name, shape, dt):
            return ctx.enter_context(nc.sbuf_tensor(name, shape, dt))

        def psum(name, shape):
            return ctx.enter_context(nc.psum_tensor(name, shape, F32))

        stage = Stage(k, ctx, "stage", 2)
        vst = [sb(f"stage_v{i}", [P, KT, HD + 1], F32) for i in range(2)]
        probs = sb("probs", [P, RING * UNIT, CH], F32)
        ptail = sb("probs_tail", [P, CH], F32)
        mixed = [sb(f"mixed{i}", [P, N], F32) for i in range(2)]
        p_sc = [psum(f"p_scores{i}", [P, UNIT, 512]) for i in range(AHEAD)]
        p_tl = psum("p_tail", [P, 512])
        p_mx = psum("p_mixed", [P, 512])

        staged = [sem(f"staged{i}") for i in range(2)]
        v_staged = [sem(f"values_staged{i}") for i in range(2)]
        s_rdy = sem("scores_ready")
        e_rdy = sem("exps_ready")
        used = sem("exps_used")
        t_rdy = sem("tail_ready")
        te_rdy = sem("tail_exp_ready")
        t_used = sem("tail_exp_used")
        mx_out = sem("mixed_taken")
        stored = [sem(f"mixed_stored{i}") for i in range(2)]
        tail_clean = sem("tail_slot_zeroed")
        sums_clean = sem("sums_bank_zeroed")

        with nc.Block() as block:
            @block.gpsimd
            def _(pool):
                stage.clear()
                nc.gpsimd.memset(ptail[:], 0.0).then_inc(tail_clean, 1)
                for i in range(2):
                    nc.gpsimd.tensor_copy(vst[i][:], k.values[:, i]).then_inc(v_staged[i], 1)
                with pool.Fori(0, PAIRS - 1) as pair:
                    for i in range(2):
                        pool.wait_ge(used, (pair * 2 + i + 1) * (BATCHES * NCH) + SPARE)
                        nc.gpsimd.tensor_copy(vst[i][:], k.values[:, bass.ds(pair * 2 + 2 + i, 1)].rearrange(
                            "p o t d -> p (o t) d")).then_inc(v_staged[i], 1)

            @block.sync
            def _(sp):
                sp.sem_inc(stored[0], 1)
                sp.sem_inc(stored[1], 1)
                def store(i, pair):
                    sp.wait_ge(mx_out, (pair * 2 + i) * NCH + NCH + 1)
                    for g in range(GROUPS):
                        sp.dma_start(k.d_mix[bass.ds(pair * 2 + i, 1), g].rearrange("o r n -> (o r) n"),
                                     mixed[i][32 * g:32 * g + HD + 1, :]).then_inc(stored[i], 16)

                stage.constants(sp)
                for i in range(2):
                    stage.load(sp, i, i, staged[i])
                with sp.Fori(0, PAIRS - 1) as pair:
                    for i in range(2):
                        store(i, pair)
                        sp.wait_ge(s_rdy, (pair * 2 + i + 1) * (UNITS * NCH))
                        stage.load(sp, i, pair * 2 + 2 + i, staged[i])
                for i in range(2):
                    store(i, PAIRS - 1)
                for i in range(2):
                    sp.wait_ge(stored[i], 16 * GROUPS * PAIRS + 1)

            @block.tensor
            def _(pe):
                mm = nc.tensor.matmul

                def scores(i, c, it, u):
                    pe.wait_ge(e_rdy, it * UNITS + u + 1)
                    for j in range(UNIT):
                        t = u * UNIT + j
                        m = mm(p_sc[u % AHEAD][:, j, 0:CH], stage.kk[i][:, t * P:t * P + P],
                               stage.q[i][:, bass.ds(c * CH, CH)], start=True, stop=True)
                    m.then_inc(s_rdy, 1)

                def tail_scores(i, c, it):
                    pe.wait_ge(te_rdy, it + 1)
                    mm(p_tl[:, 0:CH], stage.kk[i][:, (KT - 1) * P:KT * P], stage.q[i][:, bass.ds(c * CH, CH)],
                       start=True, stop=True).then_inc(t_rdy, 1)

                def mix(i, it, g):
                    if g == 0:
                        pe.wait_ge(mx_out, it + 1)
                    pe.wait_ge(e_rdy, it * UNITS + unit_of(g) + 1 + AHEAD)
                    for j in range(GROUPS):
                        t = g * GROUPS + j
                        m = mm(p_mx[32 * j:32 * j + HD + 1, 0:CH], vst[i][:, t, :], probs[:, t % (RING * UNIT), :],
                               start=(g == 0), stop=(g == BATCHES - 1))
                    m.then_inc(used, 1)

                def tail_mix(i, it):
                    pe.wait_ge(te_rdy, it + 2)
                    mm(p_mx[0:HD + 1, 0:CH], vst[i][:, KT - 1, :], ptail[:], start=False, stop=False).then_inc(t_used, 1)

                def chunk(i, c, bh, ahead):
                    it = bh * NCH + c
                    tail_scores(i, c, it)
                    for u in range(UNITS):
                        if u + AHEAD < UNITS:
                            scores(i, c, it, u + AHEAD)
                        else:
                            ahead(u + AHEAD - UNITS)
                        batches = [g for g in range(BATCHES) if unit_of(g) == u]
                        for g in batches:
                            mix(i, it, g)
                        if u == TAIL_AT:
                            tail_mix(i, it)

                pe.sem_inc(used, SPARE)
                pe.sem_inc(t_used, 1)
                pe.wait_ge(tail_clean, 1)
                pe.wait_ge(sums_clean, 1)
                pe.wait_ge(stage.const_in, 64)
                def head(pair, i, last):
                    bh = pair * 2 + i
                    with pe.Fori(0, NCH - 1) as c:
                        pe.wait_ge(v_staged[i], pair + 1)
                        chunk(i, c, bh, lambda u: scores(i, c + 1, bh * NCH + c + 1, u))

                    def next_head(u):
                        if not last:
                            if u == 0:
                                pe.wait_ge(staged[1 - i], (pair + 1 + i) * 16 * Stage.LOADS)
                            scores(1 - i, 0, bh * NCH + NCH, u)
                    chunk(i, NCH - 1, bh, next_head)

                pe.wait_ge(staged[0], 16 * Stage.LOADS)
                for u in range(AHEAD):
                    scores(0, 0, 0, u)
                with pe.Fori(0, PAIRS - 1) as pair:
                    head(pair, 0, False)
                    head(pair, 1, False)
                head(PAIRS - 1, 0, False)
                head(PAIRS - 1, 1, True)

            @block.scalar
            def _(act):
                act.sem_inc(e_rdy, AHEAD)
                act.sem_inc(te_rdy, 1)
                act.wait_ge(tail_clean, 1)
                a = nc.scalar.activation
                with act.Fori(0, B * H * NCH) as it:
                    for u in range(UNITS):
                        act.wait_ge(s_rdy, it * UNITS + u + 1)
                        act.wait_ge(used, it * BATCHES + freed_by(u) + SPARE)
                        at = (u % RING) * UNIT
                        a(probs[:, at:at + UNIT, :], p_sc[u % AHEAD][:, :, 0:CH], ACT.Exp).then_inc(e_rdy, 1)
                        if u == TAIL_EXP_AT:
                            act.wait_ge(t_rdy, it + 1)
                            act.wait_ge(t_used, it + 1)
                            a(ptail[0:TAIL, :], p_tl[0:TAIL, 0:CH], ACT.Exp).then_inc(te_rdy, 1)

            @block.vector
            def _(dve):
                dve.sem_inc(mx_out, 1)
                v = nc.vector
                v.memset(p_mx[:], 0.0).then_inc(sums_clean, 1)
                with dve.Fori(0, PAIRS) as pair:
                    for i in range(2):
                        with dve.Fori(0, NCH) as c:
                            it = (pair * 2 + i) * NCH + c
                            dve.wait_ge(stored[i], pair * (16 * GROUPS) + 1)
                            dve.wait_ge(used, it * BATCHES + BATCHES + SPARE)
                            v.tensor_copy(mixed[i][:, bass.ds(c * CH, CH)], p_mx[:, 0:CH]).then_inc(mx_out, 1)


def project_phase(k):
    nc = k.nc
    SEG = N * H // P
    with ExitStack() as ctx:
        def sem(name):
            return ctx.enter_context(nc.semaphore(name))

        def sb(name, shape, dt):
            return ctx.enter_context(nc.sbuf_tensor(name, shape, dt))

        den = sb("denominators", [P, B, GROUPS, SEG], F32)
        dsum = sb("denominator_sums", [P, B, SEG], F32)
        rec = sb("denominator_recips_sb", [P, B, SEG], F32)
        num = [sb(f"numerators{i}", [P, GROUPS, CH], F32) for i in range(2)]
        rcb = [sb(f"recips{i}", [P, CH], F32) for i in range(2)]
        low = [sb(f"num_low{i}", [P, CH], F32) for i in range(2)]
        high = [sb(f"num_high{i}", [P, CH], F32) for i in range(2)]
        o = [sb(f"attn_out{i}", [P, CH], F32) for i in range(2)]
        p_y = [ctx.enter_context(nc.psum_tensor(f"p_y{i}", [P, 2, 512], F32)) for i in range(2)]
        den_in = sem("denominators_in")
        rec_rdy = sem("recips_ready")
        rec_out = sem("recips_stored")
        num_in = [sem(f"numerators_in{i}") for i in range(2)]
        hi_rdy = sem("high_sums_ready")
        steps = sem("project_step")
        o_rdy = sem("out_ready")
        y_sum = sem("projected")
        y_rdy = sem("residual_added")
        IT = B * NCH // 2

        with nc.Block() as block:
            @block.sync
            def _(sp):
                for b in range(B):
                    for g in range(GROUPS):
                        sp.dma_start(den[:, b, g, :], k.d_mix[b * H:b * H + H, g, HD, :].rearrange(
                            "h (j n) -> h j n", n=SEG)).then_inc(den_in, 16)
                sp.wait_ge(rec_rdy, 2)
                for b in range(B):
                    sp.dma_start(k.d_recip[b * H:b * H + H, :].rearrange("h (j n) -> (h j) n", n=SEG),
                                 rec[:, b, :]).then_inc(rec_out, 16)
                sp.wait_ge(rec_out, 16 * B)
                with sp.Fori(0, 2) as b:
                    for c in range(NCH):
                        it = b * NCH + c
                        i = c % 2
                        sp.wait_ge(o_rdy, b * NCH + max(0, c - 1) + 1)
                        cols = slice(c * CH, c * CH + CH)
                        for half in range(2):
                            at = slice(half * C, half * C + C)
                            heads = bass.ds(b * H + half * 2 * H, H)
                            for g in range(GROUPS):
                                sp.dma_start(num[i][at, g, :], k.d_mix[heads, g, 0:HD, cols]).then_inc(num_in[i], 16)
                            sp.dma_start(rcb[i][at, :], k.d_recip[heads, cols].unsqueeze(1).to_broadcast(
                                [H, HD, CH])).then_inc(num_in[i], 16)

            @block.gpsimd
            def _(pool):
                with pool.Fori(0, 2) as b:
                    for c in range(NCH):
                        i = c % 2
                        n = (NCH + 1) // 2 if i == 0 else NCH // 2
                        pool.wait_ge(o_rdy, b * NCH + max(0, c - 1) + 1)
                        pool.wait_ge(num_in[i], b * (n * 160) + (c // 2 + 1) * 160)
                        nc.gpsimd.tensor_tensor(high[i][:], num[i][:, 2, :], num[i][:, 3, :], ALU.add).then_inc(hi_rdy, 1)

            @block.vector
            def _(dve):
                dve.sem_inc(o_rdy, 1)
                dve.sem_inc(y_rdy, 1)
                v = nc.vector
                dve.wait_ge(den_in, 16 * B * GROUPS)
                v.tensor_reduce(dsum[:], den[:].rearrange("p b g n -> p b n g"), AX.X, ALU.add).then_inc(rec_rdy, 1)
                dve.wait_ge(rec_rdy, 1)
                v.reciprocal(rec[:], dsum[:]).then_inc(rec_rdy, 1)
                step = Steps(dve, steps)
                with dve.Fori(0, 2) as b:
                    for c in range(NCH):
                        it = b * NCH + c
                        i = c % 2
                        n = (NCH + 1) // 2 if i == 0 else NCH // 2
                        step.loop(it * 2)
                        dve.wait_ge(num_in[i], b * (n * 160) + (c // 2 + 1) * 160)
                        step(v.tensor_tensor(low[i][:], num[i][:, 0, :], num[i][:, 1, :], ALU.add))
                        dve.wait_ge(hi_rdy, it + 1)
                        step(v.tensor_tensor(low[i][:], low[i][:], high[i][:], ALU.add))
                        dve.wait_ge(y_sum, b * NCH + max(0, c - 1) + 1)
                        v.tensor_tensor(o[i][:], low[i][:], rcb[i][:], ALU.mult).then_inc(o_rdy, 1)
                        dve.wait_ge(y_sum, it + 2)
                        for half in range(2):
                            x = k.x_tm[:, bass.ds(b * NT + half * 2 * NT + c * 4, 4), :]
                            v.tensor_tensor(x, x, p_y[i][0:TM, half, 0:4 * C].rearrange("p (t c) -> p t c", c=C),
                                            ALU.add).then_inc(y_rdy, 1)

            @block.tensor
            def _(pe):
                pe.sem_inc(y_sum, 1)
                with pe.Fori(0, 2) as b:
                    for c in range(NCH):
                        it = b * NCH + c
                        i = c % 2
                        pe.wait_ge(y_rdy, b * (2 * NCH) + 2 * max(0, c - 1) + 1)
                        pe.wait_ge(o_rdy, it + 2)
                        for half in range(2):
                            at = slice(half * C, half * C + C)
                            for j in range(4):
                                m = nc.tensor.matmul(p_y[i][0:TM, half, j * C:j * C + C],
                                                     o[i][at, j * TM:j * TM + TM], k.wo[at, :], start=True, stop=True)
                        m.then_inc(y_sum, 1)


class Norm:

    STEPS = 4

    def __init__(self, k, ctx, name):
        nc = k.nc
        self.k = k
        self.sq = [ctx.enter_context(nc.sbuf_tensor(f"{name}_squares{i}", [TM, NT, C], F32)) for i in range(2)]
        self.stat = ctx.enter_context(nc.sbuf_tensor(f"{name}_stats", [TM, 4, B, NT], F32))
        self.eps = ctx.enter_context(nc.sbuf_tensor(f"{name}_eps", [TM, 1], F32))
        self.centred = ctx.enter_context(nc.semaphore(f"{name}_centred"))
        self.squared = ctx.enter_context(nc.semaphore(f"{name}_squared"))
        self.summed = ctx.enter_context(nc.semaphore(f"{name}_summed"))
        self.rooted = ctx.enter_context(nc.semaphore(f"{name}_rooted"))
        self.done = ctx.enter_context(nc.semaphore(f"{name}_done"))
        self.step = Steps(nc.vector, ctx.enter_context(nc.semaphore(f"{name}_step")))
        self.eps_set = ctx.enter_context(nc.semaphore(f"{name}_eps_set"))

    def vector(self, dve, x, before=None, after=None):
        v, st, step = self.k.nc.vector, self.stat, self.step
        v.memset(self.eps[:], EPS).then_inc(self.eps_set, 1)

        def centre(b):
            if before is not None:
                before(b)
            xb = x[:, b * NT:b * NT + NT, :]
            step(v.tensor_reduce(st[:, 0, b, :], xb, AX.X, ALU.add))
            step(v.tensor_scalar(st[:, 0, b, :], st[:, 0, b, :], 1.0 / C, None, ALU.mult))
            v.tensor_tensor(xb, xb, st[:, 0, b, :].unsqueeze(2).to_broadcast([TM, NT, C]),
                            ALU.subtract).then_inc(self.centred, 1)

        def scale(b):
            xb = x[:, b * NT:b * NT + NT, :]
            dve.wait_ge(self.squared, b + 1)
            v.tensor_reduce(st[:, 1, b, :], self.sq[b % 2][:], AX.X, ALU.add).then_inc(self.summed, 1)
            dve.wait_ge(self.rooted, b + 1)
            step(v.reciprocal(st[:, 3, b, :], st[:, 2, b, :]))
            step(v.tensor_tensor(xb, xb, st[:, 3, b, :].unsqueeze(2).to_broadcast([TM, NT, C]), ALU.mult))
            if after is not None:
                after(b)
            v.memset(st[0:1, 0, b, 0:1], 0.0).then_inc(self.done, 1)

        centre(0)
        for b in range(B):
            if b + 1 < B:
                centre(b + 1)
            scale(b)

    def scalar(self, act, x):
        a, st = self.k.nc.scalar.activation, self.stat

        def square(b):
            act.wait_ge(self.centred, b + 1)
            if b >= 2:
                act.wait_ge(self.summed, b - 1)
            a(self.sq[b % 2][:], x[:, b * NT:b * NT + NT, :], ACT.Square).then_inc(self.squared, 1)

        act.wait_ge(self.eps_set, 1)
        square(0)
        for b in range(B):
            if b + 1 < B:
                square(b + 1)
            act.wait_ge(self.summed, b + 1)
            a(st[:, 2, b, :], st[:, 1, b, :], ACT.Sqrt, bias=self.eps[:], scale=1.0 / C).then_inc(self.rooted, 1)


def moe_phase(k):
    nc, io = k.nc, k.io
    x_tm = k.x_tm
    NTA = B * NT
    with ExitStack() as ctx:
        def sem(name):
            return ctx.enter_context(nc.semaphore(name))

        def sb(name, shape, dt):
            return ctx.enter_context(nc.sbuf_tensor(name, shape, dt))

        def split3(step, v, raw, parts, rest):
            step(v.tensor_copy(parts[0], raw))
            step(v.tensor_tensor(rest, raw, parts[0], ALU.subtract))
            step(v.tensor_copy(parts[1], rest))
            step(v.tensor_tensor(rest, rest, parts[1], ALU.subtract))
            step(v.tensor_copy(parts[2], rest))

        w1l = sb("expert_w1_parts", [P, 3, EXP, FF], BF16)
        gwl = sb("gate_w_parts", [P, 3, EXP], BF16)
        w2f = sb("expert_w2", [FF, EXP, C], F32)
        b1t = sb("expert_b1", [FF, EXP], F32)
        b2l = sb("expert_b2_parts", [3 * EXP, 3, C], BF16)
        sel = sb("expert_selector", [3 * EXP, EXP, FF], BF16)
        fold = sb("fold", [P, C], F32)
        gb = sb("gate_b", [TM, EXP], F32)
        gamma = sb("gamma", [TM, C], F32)
        beta = sb("beta", [TM, C], F32)
        eidx = sb("expert_index", [TM, EXP], F32)
        x_hm = sb("x_hi_mid", [P, B * N], BF16)
        x_hl = sb("x_hi_lo", [P, B * N], BF16)
        gates = sb("gate_parts", [TM, NTA, 3 * EXP], BF16)
        loaded = sem("moe_loaded")
        LOADED = 16 * 15
        carrier = sem("wait_carrier")

        with ExitStack() as c1:
            norm = Norm(k, c1, "norm1")
            w1raw = c1.enter_context(nc.sbuf_tensor("w1_raw", [P, EXP, FF], F32))
            w1rest = c1.enter_context(nc.sbuf_tensor("w1_rest", [P, EXP, FF], F32))
            w1part = c1.enter_context(nc.sbuf_tensor("w1_part", [P, 3, EXP, FF], BF16))
            gwraw = c1.enter_context(nc.sbuf_tensor("gw_raw", [P, EXP], F32))
            gwrest = c1.enter_context(nc.sbuf_tensor("gw_rest", [P, EXP], F32))
            gwpart = c1.enter_context(nc.sbuf_tensor("gw_part", [P, 3, EXP], BF16))
            b1raw = c1.enter_context(nc.sbuf_tensor("b1_raw", [EXP, FF], F32))
            b2raw = c1.enter_context(nc.sbuf_tensor("eb2_raw", [3 * EXP, C], F32))
            b2rest = c1.enter_context(nc.sbuf_tensor("b2_rest", [3 * EXP, C], F32))
            pb = c1.enter_context(nc.psum_tensor("p_b1", [P, 512], F32))
            b1_in = c1.enter_context(nc.semaphore("b1_in"))
            b1_flip = c1.enter_context(nc.semaphore("b1_flipped"))
            wsteps = c1.enter_context(nc.semaphore("moe_weight_step"))
            with nc.Block() as block:
                @block.sync
                def _(sp):
                    sp.dma_start(b1raw[:], io["L0_ffn_b1"]).then_inc(b1_in, 16)

                    def load(dst, src):
                        sp.dma_start(dst, src).then_inc(loaded, 16)

                    for half in range(2):
                        at = slice(half * C, half * C + C)
                        load(w1raw[at], io["L0_ffn_w1"].rearrange("e c f -> c e f"))
                        load(gwraw[at], io["L0_ffn_gate_w"])
                        load(fold[at, :], io["c_ident"][0:C, 0:C])
                    for a in range(3):
                        load(b2raw[a * EXP:a * EXP + EXP, :], io["L0_ffn_b2"])
                    load(sel[:], io["c_select"])
                    load(w2f[:], io["L0_ffn_w2"].rearrange("e f c -> f e c"))
                    load(eidx[:], io["c_index"][0:TM, 0:EXP])
                    for t, name in ((gb, "gate_b"), (gamma, "gamma"), (beta, "beta")):
                        load(t[:], io["L0_ffn_" + name].partition_broadcast(TM))

                @block.tensor
                def _(pe):
                    pe.wait_ge(b1_in, 16)
                    nc.tensor.transpose(pb[:, 0:EXP], b1raw[:], k.ident[0:EXP, 0:EXP]).then_inc(b1_flip, 1)

                @block.scalar
                def _(act):
                    norm.scalar(act, x_tm)

                @block.vector
                def _(dve):
                    v = nc.vector
                    norm.vector(dve, x_tm)
                    step = Steps(dve, wsteps)
                    dve.wait_ge(loaded, LOADED)
                    split3(step, v, w1raw[:], [w1part[:, a] for a in range(3)], w1rest[:])
                    split3(step, v, gwraw[:], [gwpart[:, a] for a in range(3)], gwrest[:])
                    split3(step, v, b2raw[:], [b2l[:, a] for a in range(3)], b2rest[:])
                    for dst, src in ((w1l, w1part), (gwl, gwpart)):
                        step(v.tensor_copy(dst[:, 0:2], src[:, 0:2]))
                        step(v.tensor_copy(dst[0:C, 2], src[0:C, 2]))
                        step(v.tensor_copy(dst[C:P, 2], src[C:P, 0]))
                    dve.wait_ge(b1_flip, 1)
                    step(v.tensor_copy(b1t[:], pb[:, 0:EXP]))

        with ExitStack() as c2:
            def sb2(name, shape, dt):
                return c2.enter_context(nc.sbuf_tensor(name, shape, dt))

            def sem2(name):
                return c2.enter_context(nc.semaphore(name))

            xd = [sb2(f"x_doubled{i}", [TM, 4, 2, C], F32) for i in range(2)]
            rest = sb2("x_rest", [P, CH], F32)
            lg = sb2("logits", [TM, 4, EXP], F32)
            m8 = sb2("largest", [TM, 4, 8], F32)
            i8 = sb2("largest_index", [TM, 4, 8], U32)
            top = sb2("top_logits", [TM, NTA, 2], F32)
            topi = sb2("top_index", [TM, NTA, 2], F32)
            wgt = sb2("top_weights", [TM, 4, NTA], F32)
            one_hot = sb2("gate_one_hot", [TM, NTA, EXP], F32)
            gate = sb2("gate_full", [TM, NTA, EXP], F32)
            p_x = [c2.enter_context(nc.psum_tensor(f"p_x{i}", [P, 512], F32)) for i in range(2)]
            p_lg = c2.enter_context(nc.psum_tensor("p_logits", [P, 512], F32))
            doubled = sem2("x_doubled_ready")
            flipped = sem2("x_flipped")
            hi_rdy = sem2("x_hi_ready")
            rest_rdy = sem2("x_rest_ready")
            mid_rdy = sem2("x_mid_ready")
            lo_rdy = sem2("x_lo_ready")
            lg_sum = sem2("logits_summed")
            lg_rdy = sem2("logits_ready")
            tops = sem2("router_step")
            diff = sem2("difference_ready")
            expd = sem2("difference_exp")
            gstep = sem2("gate_step")
            with nc.Block() as block:
                @block.gpsimd
                def _(pool):
                    with pool.Fori(0, NTA // 8) as it2:
                        for i in range(2):
                            it = it2 * 2 + i
                            pool.wait_ge(flipped, it2 * 2 + 1)
                            for d in range(2):
                                nc.gpsimd.tensor_copy(xd[i][:, :, d, :], x_tm[:, bass.ds(it * 4, 4), :]).then_inc(doubled, 1)

                @block.tensor
                def _(pe):
                    pe.sem_inc(flipped, 1)
                    def flip(i, it):
                        pe.wait_ge(doubled, it * 2 + 2)
                        pe.wait_ge(rest_rdy, it - i + 1)
                        for j in range(4):
                            m = nc.tensor.transpose(p_x[i][:, j * TM:j * TM + TM],
                                                    xd[i][:, j].rearrange("p d c -> p (d c)"), k.ident[0:TM, 0:TM])
                        m.then_inc(flipped, 1)

                    with pe.Fori(0, NTA // 8) as it2:
                        for i in range(2):
                            it = it2 * 2 + i
                            flip(i, it)
                            pe.wait_ge(mid_rdy, it + 1)
                            pe.wait_ge(lo_rdy, it + 2)
                            pe.wait_ge(lg_rdy, it + 1)
                            for j in range(4):
                                at = bass.ds(it * CH + j * TM, TM)
                                for a, xs in enumerate((x_hm, x_hm, x_hl)):
                                    m = nc.tensor.matmul(p_lg[0:TM, j * EXP:j * EXP + EXP], xs[:, at], gwl[:, a, :],
                                                         start=(a == 0), stop=(a == 2))
                            m.then_inc(lg_sum, 1)

                @block.scalar
                def _(act):
                    a = nc.scalar.activation
                    with act.Fori(0, NTA // 8) as it2:
                        for i in range(2):
                            it = it2 * 2 + i
                            act.wait_ge(flipped, it + 2)
                            at = bass.ds(it * CH, CH)
                            a(x_hm[:, at], p_x[i][:, 0:CH], ACT.Identity).then_inc(hi_rdy, 1)
                            a(x_hl[0:C, at], p_x[i][0:C, 0:CH], ACT.Identity).then_inc(hi_rdy, 1)
                    act.wait_ge(diff, 1)
                    a(wgt[:, 1, :], wgt[:, 0, :], ACT.Exp).then_inc(expd, 1)

                @block.vector
                def _(dve):
                    dve.sem_inc(rest_rdy, 1)
                    dve.sem_inc(lg_rdy, 1)
                    dve.sem_inc(lo_rdy, 1)
                    v = nc.vector
                    step = Steps(dve, tops)
                    with dve.Fori(0, NTA // 8) as it2:
                        for i in range(2):
                            it = it2 * 2 + i
                            at = bass.ds(it * CH, CH)
                            dve.wait_ge(hi_rdy, it * 2 + 2)
                            dve.wait_ge(lo_rdy, it + 1)
                            v.tensor_tensor(rest[:], p_x[i][:, 0:CH], x_hm[:, at], ALU.subtract).then_inc(rest_rdy, 1)
                            dve.wait_ge(rest_rdy, it + 2)
                            v.tensor_copy(x_hm[C:P, at], rest[C:P, :]).then_inc(mid_rdy, 1)
                            dve.wait_ge(mid_rdy, it + 1)
                            v.tensor_tensor(x_hl[C:P, at], rest[C:P, :], x_hm[C:P, at], ALU.subtract).then_inc(lo_rdy, 1)
                            dve.wait_ge(lg_sum, it + 1)
                            v.tensor_tensor(lg[:], p_lg[0:TM, 0:4 * EXP].rearrange("p (t e) -> p t e", e=EXP),
                                            gb[:].unsqueeze(1).to_broadcast([TM, 4, EXP]), ALU.add).then_inc(lg_rdy, 1)
                            dve.wait_ge(lg_rdy, it + 2)
                            dve.sem_inc(carrier, 1)
                            step.loop(it * 4)
                            for j in range(4):
                                m = v.max(m8[:, j, :], lg[:, j, :])
                            step(m)
                            dve.sem_inc(carrier, 1)
                            for j in range(4):
                                m = v.max_index(i8[:, j, :], m8[:, j, :], lg[:, j, :])
                            step(m)
                            step(v.tensor_copy(top[:, bass.ds(it * 4, 4), :], m8[:, :, 0:2]))
                            step(v.tensor_copy(topi[:, bass.ds(it * 4, 4), :], i8[:, :, 0:2]))
                    v.tensor_tensor(wgt[:, 0, :], top[:, :, 1], top[:, :, 0], ALU.subtract).then_inc(diff, 1)
                    dve.wait_ge(expd, 1)
                    step = Steps(dve, gstep)
                    step(v.tensor_scalar(wgt[:, 0, :], wgt[:, 1, :], 1.0, None, ALU.add))
                    step(v.reciprocal(wgt[:, 2, :], wgt[:, 0, :]))
                    step(v.tensor_tensor(wgt[:, 3, :], wgt[:, 1, :], wgt[:, 2, :], ALU.mult))
                    full = [TM, NTA, EXP]
                    for a, buf in ((0, gate), (1, one_hot)):
                        step(v.tensor_tensor(buf[:], eidx[:].unsqueeze(1).to_broadcast(full),
                                             topi[:, :, a:a + 1].to_broadcast(full), ALU.is_equal))
                        step(v.tensor_tensor(buf[:], buf[:], wgt[:, 2 + a, :].unsqueeze(2).to_broadcast(full), ALU.mult))
                    step(v.tensor_tensor(gate[:], gate[:], one_hot[:], ALU.add))
                    split3(step, v, gate[:], [gates[:, :, a * EXP:a * EXP + EXP] for a in range(3)], one_hot[:])

        y_tm = sb("y_token_major", [TM, NTA, C], F32)
        with ExitStack() as c3:
            def sb3(name, shape, dt):
                return c3.enter_context(nc.sbuf_tensor(name, shape, dt))

            def bank(name):
                return c3.enter_context(nc.psum_tensor(name, [P, 512], F32))

            def sem3(name):
                return c3.enter_context(nc.semaphore(name))

            gst = sb3("gate_chunk", [TM, 4, 3 * EXP], BF16)
            gT = [sb3(f"gates_T{i}", [3 * EXP, CH], BF16) for i in range(2)]
            hid = sb3("hidden_relu", [FF, 2, CH], F32)
            hg = sb3("hidden_gated", [FF, 4, CH], F32)
            zs = sb3("expert_sums", [P, CH], F32)
            p_hid = [bank("p_hid0"), bank("p_hid1")]
            p_gb = [bank("p_gb0"), bank("p_gb1")]
            p_out = bank("p_out")
            p_z = bank("p_z")
            p_gt = c3.enter_context(nc.psum_tensor("p_gt", [P, 1024], BF16))
            staged = sem3("gate_chunk_ready")
            gflip = sem3("gates_flipped")
            g_rdy = sem3("gates_T_ready")
            h_sum = sem3("hid_summed")
            h_rdy = sem3("hid_ready")
            b_sum = sem3("gate_spread")
            hg_rdy = sem3("hid_gated")
            hg_used = sem3("hid_gated_used")
            out_sum = sem3("expert_out_summed")
            z_rdy = sem3("expert_out_ready")
            z_sum = sem3("folded")
            y_rdy = sem3("y_ready")
            CHUNKS = B * NCH
            with nc.Block() as block:
                @block.gpsimd
                def _(pool):
                    with pool.Fori(0, CHUNKS) as it:
                        pool.wait_ge(gflip, it + 1)
                        nc.gpsimd.tensor_copy(gst[:], gates[:, bass.ds(it * 4, 4), :]).then_inc(staged, 1)

                @block.tensor
                def _(pe):
                    pe.sem_inc(gflip, 1)
                    pe.sem_inc(hg_used, 1)
                    pe.sem_inc(z_sum, 1)
                    mm = nc.tensor.matmul

                    def flip_gates(it):
                        pe.wait_ge(g_rdy, it + 1)
                        pe.wait_ge(staged, it + 1)
                        pe.sem_inc(carrier, 1)
                        for j in range(4):
                            m = nc.tensor.transpose(p_gt[0:3 * EXP, j * TM:j * TM + TM], gst[:, j, :],
                                                    k.ident_bf[0:TM, 0:TM])
                        m.then_inc(gflip, 1)

                    with pe.Fori(0, CHUNKS // 2) as it2:
                        for i in range(2):
                            it = it2 * 2 + i
                            flip_gates(it)
                            at = bass.ds(it * CH, CH)

                            def first(e):
                                pe.wait_ge(h_rdy, it * EXP + e - (1 if e else 0) + 1)
                                for a, xs in enumerate((x_hm, x_hm, x_hl)):
                                    m = mm(p_hid[e % 2][:, 0:CH], w1l[:, a, e, :], xs[:, at], start=(a == 0), stop=(a == 2))
                                m.then_inc(h_sum, 1)
                                if e == 0:
                                    pe.wait_ge(g_rdy, it + 2)
                                pe.wait_ge(hg_rdy, it * EXP + e - (1 if e else 0) + 1)
                                mm(p_gb[e % 2][:, 0:CH], sel[:, e, :], gT[i][:], start=True, stop=True).then_inc(b_sum, 1)

                            def second(e):
                                o = (e % 2) * C
                                if e == 0:
                                    pe.wait_ge(z_rdy, it + 1)
                                    pe.sem_inc(carrier, 1)
                                    for a in range(3):
                                        mm(p_out[0:C, 0:CH], b2l[:, a, :], gT[i][:], start=(a == 0), stop=False)
                                m = mm(p_out[o:o + C, 0:CH], w2f[:, e, :], hg[:, e % 4, :], start=(e == 1), stop=(e >= EXP - 2))
                                m.then_inc(hg_used, 1)

                            first(0)
                            first(1)
                            for e in range(0, EXP, 2):
                                if e + 2 < EXP:
                                    first(e + 2)
                                    first(e + 3)
                                pe.wait_ge(hg_rdy, it * EXP + e + 3)
                                second(e)
                                second(e + 1)
                            pe.wait_ge(z_rdy, it + 2)
                            pe.wait_ge(y_rdy, it + 1)
                            for j in range(4):
                                m = mm(p_z[0:TM, j * C:j * C + C], zs[:, j * TM:j * TM + TM], fold[:], start=True, stop=True)
                            m.then_inc(z_sum, 1)

                @block.scalar
                def _(act):
                    act.sem_inc(g_rdy, 1)
                    act.sem_inc(h_rdy, 1)
                    act.sem_inc(z_rdy, 1)
                    a = nc.scalar.activation
                    with act.Fori(0, CHUNKS // 2) as it2:
                        for i in range(2):
                            it = it2 * 2 + i
                            act.wait_ge(gflip, it + 2)
                            act.wait_ge(hg_used, it2 * (2 * EXP) + 1)
                            a(gT[i][:], p_gt[0:3 * EXP, 0:CH], ACT.Identity).then_inc(g_rdy, 1)
                            for e in range(EXP):
                                act.wait_ge(h_sum, it * EXP + e + 1)
                                act.wait_ge(hg_rdy, it * EXP + e - (1 if e else 0) + 1)
                                a(hid[:, e % 2, :], p_hid[e % 2][:, 0:CH], ACT.Relu, bias=b1t[:, e:e + 1]).then_inc(h_rdy, 1)
                            act.wait_ge(hg_used, it * EXP + EXP + 1)
                            act.wait_ge(z_sum, it + 1)
                            a(zs[:], p_out[:, 0:CH], ACT.Identity).then_inc(z_rdy, 1)

                @block.vector
                def _(dve):
                    dve.sem_inc(hg_rdy, 1)
                    dve.sem_inc(y_rdy, 1)
                    v = nc.vector
                    with dve.Fori(0, CHUNKS // 2) as it2:
                        for i in range(2):
                            it = it2 * 2 + i
                            for e in range(EXP):
                                dve.wait_ge(h_rdy, it * EXP + e + 2)
                                dve.wait_ge(b_sum, it * EXP + e + 1)
                                dve.wait_ge(hg_used, it * EXP + max(0, e - 3) + 1)
                                v.tensor_tensor(hg[:, e % 4, :], p_gb[e % 2][:, 0:CH], hid[:, e % 2, :],
                                                ALU.mult).then_inc(hg_rdy, 1)
                            dve.wait_ge(z_sum, it + 2)
                            v.tensor_tensor(y_tm[:, bass.ds(it * 4, 4), :], x_tm[:, bass.ds(it * 4, 4), :],
                                            p_z[0:TM, 0:4 * C].rearrange("p (t c) -> p t c", c=C), ALU.add).then_inc(y_rdy, 1)

        with ExitStack() as c4:
            norm = Norm(k, c4, "norm2")
            final = Norm(k, c4, "norm3")
            out_done = c4.enter_context(nc.semaphore("out_stored"))
            with nc.Block() as block:
                @block.scalar
                def _(act):
                    norm.scalar(act, y_tm)
                    final.scalar(act, y_tm)

                @block.vector
                def _(dve):
                    v = nc.vector

                    def affine(b):
                        full = [TM, NT, C]
                        y = y_tm[:, b * NT:b * NT + NT, :]
                        norm.step(v.tensor_tensor(y, y, gamma[:].unsqueeze(1).to_broadcast(full), ALU.mult))
                        norm.step(v.tensor_tensor(y, y, beta[:].unsqueeze(1).to_broadcast(full), ALU.add))
                        norm.step(v.tensor_tensor(y, y, x_tm[:, b * NT:b * NT + NT, :], ALU.add))

                    norm.vector(dve, y_tm, after=affine)
                    final.vector(dve, y_tm)

                @block.sync
                def _(sp):
                    for b in range(B):
                        sp.wait_ge(final.done, b + 1)
                        sp.dma_start(k.out[b].rearrange("(t p) c -> p t c", p=TM),
                                     y_tm[:, b * NT:b * NT + NT, :]).then_inc(out_done, 16)
                    sp.wait_ge(out_done, 16 * B)


def constants():
    p = np.arange(P)
    weight = np.zeros((P, 2), np.float32)
    weight[p, p % 2] = np.exp2(p - 64.0)
    select = np.zeros((3, EXP, EXP, FF), np.float32)
    for e in range(EXP):
        select[:, e, e, :] = 1.0
    bf16 = mybir.dt.np(BF16)
    return {
        "c_ident": np.eye(P, dtype=np.float32),
        "c_index": np.tile(np.arange(P, dtype=np.float32), (P, 1)),
        "c_weight": weight,
        "c_head_sum": np.kron(np.eye(H), np.ones((HD, HD))).astype(np.float32),
        "c_ones": np.ones((3, NP), bf16),
        "c_select": select.reshape(3 * EXP, EXP, FF).astype(bf16),
    }


def build(nc, io, out):
    with ExitStack() as ctx:
        k = Core(nc, io, out, ctx)
        setup_phase(k)
        tok_phase(k)
        maximum_phase(k)
        attention_phase(k)
        project_phase(k)
        moe_phase(k)


def kernel(**inputs):
    import concourse.bacc as bacc
    from concourse.bass_utils import run_bass_kernel_spmd

    nc = bacc.Bacc("TRN2", target_bir_lowering=False, num_devices=1)
    arrays, io = {}, {}
    for name, a in {**inputs, **constants()}.items():
        a = np.ascontiguousarray(a)
        arrays[f"in_{name}"] = a
        io[name] = nc.dram_tensor(f"in_{name}", a.shape, mybir.dt.from_np(a.dtype), kind="ExternalInput").ap()
    out = nc.dram_tensor("out_0", (B, N, C), F32, kind="ExternalOutput").ap()
    build(nc, io, out)
    r = run_bass_kernel_spmd(nc, [arrays], core_ids=[0])
    return r.results[0]["out_0"]
```

```python
from contextlib import ExitStack

import numpy as np

import concourse.bass as bass
from concourse import mybir

ALU = mybir.AluOpType
ACT = mybir.ActivationFunctionType
AX = mybir.AxisListType
F32 = mybir.dt.float32
BF16 = mybir.dt.bfloat16
I32 = mybir.dt.int32
U32 = mybir.dt.uint32

B, C, HW, K = 4, 64, 56, 3
N = HW * HW
PADW = HW + 2
H, HD = 8, 8
E_EDGES = 16384
EXP, FF = 16, 128
P = 128

CH = 8 * HW
NCH = N // CH
TM = CH // 4
NT = N // TM
KT = -(-N // P)
NP = KT * P
TAIL = N - (KT - 1) * P
TPC = N - TAIL

TAPS_LO = [0, 1, 2, 6, 8]
TAPS_HI = [3, 4, 5, 7]
NSLOT = len(TAPS_LO)

BIAS_ROW = 9 * HD
SHIFT_ROW = BIAS_ROW + 3
GROUPS = 4
SCORE_LIMIT = 56.0
EPS = 1e-5
KEY_BASE = 63 * P




class Steps:

    def __init__(self, eng, sem):
        self.eng, self.sem, self.base, self.n = eng, sem, 0, 0

    def loop(self, base):
        self.base, self.n = base, 0

    def __call__(self, ins):
        self.n += 1
        ins.then_inc(self.sem, 1)
        self.eng.wait_ge(self.sem, self.base + self.n)


class Core:

    def __init__(self, nc, io, out, ctx):
        self.nc, self.io, self.out, self.ctx = nc, io, out, ctx

        def keep(name, shape, dt):
            return ctx.enter_context(nc.sbuf_tensor(name, shape, dt))

        def scratch(name, shape, dt):
            return nc.dram_tensor(name, shape, dt, kind="Internal").ap()

        self.w1 = keep("tok_w1", [P, NSLOT, C], F32)
        self.w2 = keep("tok_w2", [C, NSLOT, P], F32)
        self.w3 = keep("tok_w3", [P, NSLOT, C], F32)
        self.b1 = keep("tok_b1", [C, 1], F32)
        self.b2 = keep("tok_b2_half", [P, NSLOT], F32)
        self.b3 = keep("tok_b3", [P, 1], F32)
        self.wqk = keep("attn_wqk", [P, 2 * C], F32)
        self.bqk = keep("attn_bqk", [2 * C, 1], F32)
        self.wv = keep("attn_wv", [P, C], F32)
        self.bv = keep("attn_bv", [P, C], F32)
        self.bo = keep("attn_bo", [TM, C], F32)
        self.wo = keep("attn_wo", [P, C], F32)
        self.ident = keep("ident", [P, P], F32)
        self.ident_bf = keep("ident_bf", [P, P], BF16)
        self.x_tm = keep("x_token_major", [TM, B * NT, C], F32)
        self.values = keep("values", [P, B * H, KT, HD + 1], F32)
        self.flag = keep("need_maximum", [1, 1], I32)
        self.d_qk = scratch("qk_parts", [3, 2, B * C, N], BF16)
        self.d_bias = scratch("bias_parts", [B * H, 3, NP], BF16)
        self.d_shift = scratch("shift_parts", [B * H, 3, NP], BF16)
        self.d_recip = scratch("denominator_recips", [B * H, N], F32)
        self.d_mix = scratch("mixed", [B * H * HD, GROUPS, N], F32)
        self.d_den = scratch("denominators_by_group", [GROUPS, B * H, N], F32)


def setup_phase(k):
    nc, io = k.nc, k.io
    with ExitStack() as ctx:
        def sb(name, shape, dt):
            return ctx.enter_context(nc.sbuf_tensor(name, shape, dt))

        def sem(name):
            return ctx.enter_context(nc.semaphore(name))

        EC = E_EDGES // P
        PER = 10
        NB = -(-EC // PER)
        W = KT * 2
        w2raw = sb("w2_raw", [C, K * K * C], F32)
        b2raw = sb("b2_raw", [P, K * K], F32)
        tgt = sb("edge_target", [P, EC], I32)
        tlo = sb("target_lo", [P, EC], I32)
        thi = sb("target_hi", [P, EC], I32)
        tlof = sb("target_lo_f", [P, EC], F32)
        thif = sb("target_hi_f", [P, EC], F32)
        index = sb("index_row", [P, P], F32)
        weight = sb("edge_weight", [P, 2], F32)
        onelo = sb("one_hot_lo", [P, EC, P], BF16)
        onehi = sb("one_hot_hi", [P, EC, KT], BF16)
        rhs = sb("weighted_hi", [P, EC, KT, 2], BF16)
        keyi = sb("key_bits", [P, EC, W], I32)
        keyf = onelo[:, :, 0:2 * W].bitcast(F32)
        best = sb("best_key", [P, KT], F32)
        has = sb("has_edge", [P, KT], F32)
        edge = sb("edge_index", [P, KT], U32)
        attr = sb("edge_attr", [P, KT, 3], F32)
        we = sb("edge_w", [P, 3 * H], F32)
        be = sb("edge_b", [P, H], F32)
        term = sb("bias_term", [P, KT, H], F32)
        bias = sb("key_bias", [P, KT, H], F32)
        masked = sb("bias_masked", [P, KT, H], F32)
        bmax = sb("bias_max", [P, H], F32)
        gmax = sb("bias_max_all", [P, H], F32)
        parts = sb("bias_parts_tm", [P, KT, H, 3], BF16)
        rows = sb("bias_rows", [3 * H, NP], BF16)
        zero = sb("zero_rows", [3, NP], BF16)
        ps = [ctx.enter_context(nc.psum_tensor(f"edge_ps{i}", [P, 512], F32)) for i in range(2)]
        pt = [ctx.enter_context(nc.psum_tensor(f"bias_ps{i}", [P, 1024], BF16)) for i in range(4)]

        loaded = sem("setup_loaded")
        edges_in = sem("edges_loaded")
        onehot = sem("one_hots_ready")
        counted = sem("edges_counted")
        taken = sem("counts_taken")
        indexed = sem("edge_index_ready")
        gathered = sem("attrs_gathered")
        bmax_own = sem("bias_max_ready")
        bmax_all = sem("bias_max_shared")
        split = sem("bias_split")
        turned = sem("bias_turned")
        rowed = sem("bias_rows_ready")
        written = sem("setup_written")
        zeroed = sem("zero_rows_ready")
        dve_step = sem("setup_dve_step")
        n_load = [0]

        with nc.Block() as block:
            @block.sync
            def _(sp):
                ei = io["L0_attn_edge_index"]
                sp.dma_start(tgt[:], ei[1].rearrange("(p c) -> p c", p=P)).then_inc(edges_in, 16)
                sp.dma_start(index[:], io["c_index"]).then_inc(edges_in, 16)
                sp.dma_start(weight[:], io["c_weight"]).then_inc(edges_in, 16)
                sp.dma_start(we[:], io["L0_attn_We"].rearrange("a h -> (a h)").partition_broadcast(P)).then_inc(edges_in, 16)
                sp.dma_start(be[:], io["L0_attn_be"].partition_broadcast(P)).then_inc(edges_in, 16)

                def load(dst, src):
                    n_load[0] += 16
                    sp.dma_start(dst, src).then_inc(loaded, 16)

                for w, name in ((k.w1, "L0_tok_W1"), (k.w3, "L0_tok_W3")):
                    by_tap = io[name].rearrange("(c t) m -> t c m", t=K * K)
                    for s, t in enumerate(TAPS_LO):
                        load(w[0:C, s, :], by_tap[t])
                    for s, t in enumerate(TAPS_HI):
                        load(w[C:P, s, :], by_tap[t])
                load(w2raw[:], io["L0_tok_W2"])
                for half in range(2):
                    load(b2raw[half * C:half * C + C, :], io["L0_tok_b2"].rearrange("(c t) -> c t", t=K * K))
                load(k.b1[:], io["L0_tok_b1"].unsqueeze(1))
                load(k.b3[C:P, :], io["L0_tok_b3"].unsqueeze(1))
                for i, s in enumerate("qk"):
                    load(k.wqk[C:P, i * C:i * C + C], io["L0_attn_W" + s])
                    load(k.bqk[i * C:i * C + C, :], io["L0_attn_b" + s].unsqueeze(1))
                load(k.wv[C:P, :], io["L0_attn_Wv"])
                load(k.bv[:], io["L0_attn_bv"].partition_broadcast(P))
                load(k.bo[:], io["L0_attn_bo"].partition_broadcast(TM))
                for half in range(2):
                    load(k.wo[half * C:half * C + C, :], io["L0_attn_Wo"])
                load(k.ident[:], io["c_ident"])
                sp.wait_ge(zeroed, 1)
                for bh in range(B * H):
                    sp.dma_start(k.d_shift[bh], zero[:]).then_inc(written, 16)
                sp.wait_ge(rowed, 1)
                for b in range(B):
                    sp.dma_start(k.d_bias[b * H:b * H + H].rearrange("h a n -> (h a) n"), rows[:]).then_inc(written, 16)
                sp.wait_ge(written, 16 * (B * H + B))

            @block.gpsimd
            def _(pool):
                nc.gpsimd.memset(zero[:], 0.0).then_inc(zeroed, 1)
                pool.wait_ge(indexed, 1)
                for t in range(KT):
                    nc.gpsimd.indirect_dma_start(
                        attr[:, t, :], None, io["L0_attn_edge_attr"],
                        bass.IndirectOffsetOnAxis(ap=edge[:, t:t + 1], axis=0)).then_inc(gathered, 16)
                pool.wait_ge(bmax_own, 1)
                nc.gpsimd.partition_all_reduce(gmax[:], bmax[:], P, bass.bass_isa.ReduceOp.max).then_inc(bmax_all, 1)

            @block.tensor
            def _(pe):
                pe.wait_ge(onehot, 1)
                for c in range(EC):
                    g = c // PER
                    if c % PER == 0 and g >= 2:
                        pe.wait_ge(taken, g - 1)
                    o = (c % PER) * W
                    mm = nc.tensor.matmul(ps[g % 2][:, o:o + W], onelo[:, c, :],
                                          rhs[:, c, :, :].rearrange("p h r -> p (h r)"), start=True, stop=True)
                    if c % PER == PER - 1 or c == EC - 1:
                        mm.then_inc(counted, 1)
                pe.wait_ge(split, 1)
                for t in range(KT):
                    tr = nc.tensor.transpose(pt[t // 8][0:3 * H, (t % 8) * P:(t % 8 + 1) * P],
                                             parts[:, t, :, :].rearrange("p h a -> p (h a)"), k.ident_bf[:])
                tr.then_inc(turned, 1)

            @block.vector
            def _(dve):
                v = nc.vector
                step = Steps(dve, dve_step)
                dve.wait_ge(edges_in, 16 * 5)
                step(v.tensor_scalar(tlo[:], tgt[:], P - 1, None, ALU.bitwise_and))
                step(v.tensor_scalar(thi[:], tgt[:], 7, None, ALU.logical_shift_right))
                step(v.tensor_copy(tlof[:], tlo[:]))
                step(v.tensor_copy(thif[:], thi[:]))
                step(v.tensor_tensor(onehi[:], index[:, 0:KT].unsqueeze(1).to_broadcast([P, EC, KT]),
                                     thif[:].unsqueeze(2).to_broadcast([P, EC, KT]), ALU.is_equal))
                for r in range(2):
                    step(v.tensor_scalar(rhs[:, :, :, r], onehi[:], weight[:, r:r + 1], None, ALU.mult))
                v.tensor_tensor(onelo[:], index[:].unsqueeze(1).to_broadcast([P, EC, P]),
                                tlof[:].unsqueeze(2).to_broadcast([P, EC, P]), ALU.is_equal).then_inc(onehot, 1)
                for g in range(NB):
                    n = min(PER, EC - g * PER)
                    dve.wait_ge(counted, g + 1)
                    v.tensor_scalar(keyi[:, g * PER:g * PER + n, :].rearrange("p c w -> p (c w)"),
                                    ps[g % 2][:, 0:n * W].bitcast(I32), 16, 0xFF80,
                                    ALU.logical_shift_right, ALU.bitwise_and).then_inc(taken, 1)
                dve.wait_ge(taken, NB)
                step(v.tensor_tensor(keyf, keyi[:], index[:].unsqueeze(2).to_broadcast([P, EC, W]), ALU.add))
                step(v.tensor_reduce(best[:], keyf.rearrange("p c (h r) -> p h c r", r=2), AX.XY, ALU.max))
                step(v.tensor_scalar(has[:], best[:], float(KEY_BASE), None, ALU.is_ge))
                v.tensor_scalar(edge[:], best[:], float(-KEY_BASE), 0.0, ALU.add, ALU.max).then_inc(indexed, 1)
                dve.wait_ge(loaded, n_load[0])
                for s, t in enumerate(TAPS_LO):
                    step(v.tensor_copy(k.w2[:, s, 0:C], w2raw[:, t::K * K]))
                    step(v.tensor_scalar(k.b2[0:C, s:s + 1], b2raw[0:C, t:t + 1], 0.5, None, ALU.mult))
                for s, t in enumerate(TAPS_HI):
                    step(v.tensor_copy(k.w2[:, s, C:P], w2raw[:, t::K * K]))
                    step(v.tensor_scalar(k.b2[C:P, s:s + 1], b2raw[C:P, t:t + 1], 0.5, None, ALU.mult))
                step(v.memset(k.w1[C:P, NSLOT - 1, :], 0.0))
                step(v.memset(k.w2[:, NSLOT - 1, C:P], 0.0))
                step(v.memset(k.w3[C:P, NSLOT - 1, :], 0.0))
                step(v.memset(k.b2[C:P, NSLOT - 1:NSLOT], 0.0))
                step(v.tensor_scalar(k.w3[:], k.w3[:], 0.5, None, ALU.mult))
                step(v.tensor_scalar(k.wqk[C:P, 0:C], k.wqk[C:P, 0:C], float(HD) ** -0.5, None, ALU.mult))
                step(v.tensor_scalar(k.bqk[0:C, :], k.bqk[0:C, :], float(HD) ** -0.5, None, ALU.mult))
                step(v.tensor_copy(k.ident_bf[:], k.ident[:]))
                dve.wait_ge(gathered, 16 * KT)
                for a in range(3):
                    w = we[:, a * H:a * H + H].unsqueeze(1).to_broadcast([P, KT, H])
                    x = attr[:, :, a:a + 1].to_broadcast([P, KT, H])
                    step(v.tensor_tensor((term if a else bias)[:], x, w, ALU.mult))
                    if a:
                        step(v.tensor_tensor(bias[:], bias[:], term[:], ALU.add))
                step(v.tensor_tensor(bias[:], bias[:], be[:].unsqueeze(1).to_broadcast([P, KT, H]), ALU.add))
                step(v.tensor_tensor(bias[:], bias[:], has[:].unsqueeze(2).to_broadcast([P, KT, H]), ALU.mult))
                step(v.tensor_copy(masked[:], bias[:]))
                step(v.memset(masked[TAIL:P, KT - 1, :], -3.0e38))
                v.tensor_reduce(bmax[:], masked[:].rearrange("p t h -> p h t"), AX.X, ALU.max).then_inc(bmax_own, 1)
                dve.wait_ge(bmax_all, 1)
                step(v.tensor_tensor(bias[:], bias[:], gmax[:].unsqueeze(1).to_broadcast([P, KT, H]), ALU.subtract))
                step(v.tensor_copy(parts[:, :, :, 0], bias[:]))
                step(v.tensor_tensor(bias[:], bias[:], parts[:, :, :, 0], ALU.subtract))
                step(v.tensor_copy(parts[:, :, :, 1], bias[:]))
                step(v.tensor_tensor(bias[:], bias[:], parts[:, :, :, 1], ALU.subtract))
                v.tensor_copy(parts[:, :, :, 2], bias[:]).then_inc(split, 1)
                dve.wait_ge(turned, 1)
                for g in range(4):
                    n = min(1024, NP - 1024 * g)
                    step(v.tensor_copy(rows[:, 1024 * g:1024 * g + n], pt[g][0:3 * H, 0:n]))
                v.memset(k.values[:, :, KT - 1, :], 0.0).then_inc(rowed, 1)


def tok_phase(k):
    nc, io = k.nc, k.io
    with ExitStack() as ctx:
        def sb(name, shape, dt):
            return ctx.enter_context(nc.sbuf_tensor(name, shape, dt))

        def bank(name):
            return ctx.enter_context(nc.psum_tensor(name, [P, 512], F32))

        def sem(name):
            return ctx.enter_context(nc.semaphore(name))

        raw = sb("image", [P, N], F32)
        pad_row = [sb(f"padded_and_a_row_on{i}", [P, PADW, PADW], F32) for i in range(2)]
        pad_col = [sb(f"padded_and_a_column_on{i}", [P, PADW, PADW], F32) for i in range(2)]
        h1 = sb("hidden", [C, CH], F32)
        th = sb("gate_tanh", [P, 2, CH], F32)
        ts = sb("gated_taps", [P, NSLOT, CH], F32)
        hT = sb("h_chunk", [P, CH], F32)
        hTb = sb("h_image", [P, NP], F32)
        part = sb("qk_parts_chunk", [P, 3, CH], BF16)
        rest = sb("qk_rest", [P, CH], F32)
        amax = sb("qk_abs_max", [P, B * NCH], F32)
        amax_b = sb("qk_abs_max_image", [P, B], F32)
        kmax = sb("k_abs_max", [C, B], F32)
        bound = sb("score_bound", [C, B], F32)
        head_sum = sb("head_sum", [C, C], F32)
        bmx = sb("bound_max", [C, 1], F32)
        bmx_all = sb("bound_max_all", [C, 1], F32)
        p_h1 = bank("p_h1")
        p_s = [bank("p_s0"), bank("p_s1")]
        p_h = bank("p_h")
        p_qk = bank("p_qk")
        p_tm = bank("p_tm")
        p_v = [bank("p_v0"), bank("p_v1")]

        img_in = sem("image_loaded")
        zero_pool = sem("padding_zeroed_pool")
        zero_dve = sem("padding_zeroed_dve")
        pad_act = sem("first_image_padded_act")
        pad_dve = sem("first_image_padded_dve")
        pad_next = sem("image_padded")
        h1_sum = sem("hidden_summed")
        h1_rdy = sem("hidden_ready")
        s_sum = sem("gate_summed")
        th_rdy = sem("tanh_ready")
        ts_rdy = sem("gated_ready")
        h_sum = sem("h_summed")
        h_rdy = sem("h_ready")
        hc_rdy = sem("h_chunk_ready")
        qk_sum = sem("qk_summed")
        hi_rdy = sem("hi_ready")
        r1_rdy = sem("rest_ready")
        mid_rdy = sem("mid_ready")
        lo_rdy = sem("lo_ready")
        stored = sem("qk_stored")
        tm_sum = sem("token_major_summed")
        tm_rdy = sem("token_major_ready")
        v_sum = sem("values_summed")
        v_rdy = sem("values_ready")
        am_rdy = sem("abs_max_of_chunk_ready")
        kmv = sem("k_max_moved")
        bsum = sem("bounds_summed")
        ball = sem("bound_shared")
        bown = sem("abs_max_ready")
        bmul = sem("bound_products_ready")
        bone = sem("bound_of_heads_ready")
        const_in = sem("head_sum_loaded")
        flagged = sem("flag_ready")
        ones = sem("ones_set")

        NV = -(-KT // 8)
        LAST = B * NCH - 1
        PIECES = 4 * NCH

        def window(buf, c, tap):
            ki, kj = tap // K, tap % K
            return buf[:, bass.ds(c * 8 + ki, 8), kj:kj + HW]

        def slot_buf(b, s):
            return (pad_col if s == 3 else pad_row)[b % 2]

        def shifted(b, r, rows):
            at = bass.ds(r + 1, rows)
            return ((pad_row[b % 2][0:C, at, 1:HW + 1], slice(0, C)),
                    (pad_row[b % 2][C:P, bass.ds(r, rows), 1:HW + 1], slice(C, P)),
                    (pad_col[b % 2][0:C, at, 1:HW + 1], slice(0, C)),
                    (pad_col[b % 2][C:P, at, 0:HW], slice(C, P)))

        def image_chunks(eng, b, chunk):
            first = 2 if b == 0 else 1
            for c in range(first):
                chunk(c, c + b * NCH, min(2, c + b * NCH))
            with eng.Fori(first, NCH - 1) as c:
                chunk(c, c + b * NCH, 2)
            chunk(NCH - 1, b * NCH + NCH - 1, 2)

        image = raw[:].rearrange("p (r c) -> p r c", r=HW)

        with nc.Block() as block:
            @block.sync
            def _(sp):
                sp.sem_inc(stored, 1)

                def load(b):
                    for half in range(2):
                        sp.dma_start(raw[half * C:half * C + C, :],
                                     io["x"][b].rearrange("c h w -> c (h w)")).then_inc(img_in, 16)

                load(0)
                sp.dma_start(head_sum[:], io["c_head_sum"]).then_inc(const_in, 16)
                sp.wait_ge(pad_act, 2)
                sp.wait_ge(pad_dve, 2)
                load(1)

                def store(b, c):
                    sp.wait_ge(lo_rdy, c + b * NCH + 2)
                    for i in range(2):
                        sp.dma_start(k.d_qk[:, i, b * C:b * C + C, bass.ds(c * CH, CH)].rearrange("j r n -> r j n"),
                                     part[i * C:i * C + C]).then_inc(stored, 16)

                for b in range(B):
                    with sp.Fori(0, NCH - 2) as c:
                        store(b, c)
                    if b + 2 < B:
                        sp.wait_ge(pad_next, (b + 1) * PIECES)
                        load(b + 2)
                    store(b, NCH - 2)
                    store(b, NCH - 1)
                sp.wait_ge(bown, 1)
                sp.dma_start(kmax[:], amax_b[C:P, :]).then_inc(kmv, 16)
                sp.wait_ge(stored, 16 * 2 * B * NCH + 1)

            @block.gpsimd
            def _(pool):
                pool.sem_inc(lo_rdy, 1)
                nc.gpsimd.memset(pad_row[0][:], 0.0).then_inc(zero_pool, 1)
                nc.gpsimd.memset(pad_row[1][:], 0.0).then_inc(zero_pool, 1)
                nc.gpsimd.memset(pad_col[1][:], 0.0).then_inc(zero_pool, 1)
                pool.wait_ge(zero_pool, 3)

                def low_part(it):
                    pool.wait_ge(stored, it * 32 + 1)
                    pool.wait_ge(mid_rdy, it + 1)
                    nc.gpsimd.tensor_tensor(part[:, 2, :], rest[:], part[:, 1, :], ALU.subtract).then_inc(lo_rdy, 1)

                with pool.Fori(0, B * NCH) as it:
                    low_part(it)
                pool.wait_ge(bone, 1)
                nc.gpsimd.partition_all_reduce(bmx_all[:], bmx[:], C, bass.bass_isa.ReduceOp.max).then_inc(ball, 1)

            @block.tensor
            def _(pe):
                pe.sem_inc(h_sum, 1)
                pe.sem_inc(s_sum, 1)
                pe.sem_inc(qk_sum, 1)
                pe.sem_inc(tm_sum, 1)
                pe.sem_inc(v_sum, 1)
                mm = nc.tensor.matmul

                def hidden(b, c, s):
                    m = mm(p_h1[0:C, 0:CH], k.w1[:, s, :], window(slot_buf(b, s), c, TAPS_LO[s]),
                           start=(s == 0), stop=(s == NSLOT - 1))
                    if s == NSLOT - 1:
                        m.then_inc(h1_sum, 1)

                def gate(it, s):
                    if s == 0:
                        pe.wait_ge(h1_rdy, it + 2)
                    pe.wait_ge(th_rdy, it * NSLOT + max(0, s - 1) + 1)
                    mm(p_s[s % 2][:, 0:CH], k.w2[:, s, :], h1[:], start=True, stop=True).then_inc(s_sum, 1)

                def mix(it, s):
                    if s == 0:
                        pe.wait_ge(h_rdy, it + 1)
                    pe.wait_ge(ts_rdy, it * NSLOT + s + 2)
                    m = mm(p_h[C:P, 0:CH], k.w3[:, s, :], ts[:, s, :], start=(s == 0), stop=(s == NSLOT - 1))
                    if s == NSLOT - 1:
                        m.then_inc(h_sum, 1)

                def products(it):
                    pe.wait_ge(hc_rdy, it + 1)
                    pe.wait_ge(r1_rdy, it + 1)
                    mm(p_qk[:, 0:CH], k.wqk[C:P, :], hT[C:P, :], start=True, stop=True).then_inc(qk_sum, 1)
                    pe.wait_ge(tm_rdy, it + 1)
                    for j in range(4):
                        m = mm(p_tm[0:TM, j * C:j * C + C], hT[C:P, j * TM:j * TM + TM], k.ident[C:P, C:P],
                               start=True, stop=True)
                    m.then_inc(tm_sum, 1)

                pe.wait_ge(pad_act, 2)
                pe.wait_ge(pad_dve, 2)
                for s in range(NSLOT):
                    hidden(0, 0, s)
                for b in range(B):
                    def chunk(c, it, age):
                        last = isinstance(c, int) and c == NCH - 1
                        gate(it, 0)
                        gate(it, 1)
                        for s in range(NSLOT):
                            if s + 2 < NSLOT:
                                gate(it, s + 2)
                            if not last:
                                hidden(b, c + 1, s)
                            elif b + 1 < B:
                                if s == 0:
                                    pe.wait_ge(pad_next, (b + 1) * PIECES)
                                hidden(b + 1, 0, s)
                            mix(it, s)
                        if age:
                            products(it - 1)
                    image_chunks(pe, b, chunk)
                    pe.wait_ge(h_rdy, b * NCH + NCH + 1)
                    for t in range(KT):
                        g = t // 8
                        if t % 8 == 0:
                            pe.wait_ge(v_rdy, b * NV + max(0, g - 1) + 1)
                        m = min(P, N - t * P)
                        i = mm(p_v[g % 2][0:m, (t % 8) * C:(t % 8) * C + C], hTb[C:P, t * P:t * P + m], k.wv[C:P, :],
                               start=True, stop=True)
                        if t % 8 == 7 or t == KT - 1:
                            i.then_inc(v_sum, 1)
                products(LAST)
                pe.wait_ge(bmul, 1)
                pe.wait_ge(const_in, 16)
                mm(p_h1[0:C, 0:B], head_sum[:], bound[:], start=True, stop=True).then_inc(bsum, 1)

            @block.scalar
            def _(act):
                act.sem_inc(h1_rdy, 1)
                act.sem_inc(th_rdy, 1)
                act.sem_inc(h_rdy, 1)
                a = nc.scalar.activation
                act.wait_ge(img_in, 32)
                act.wait_ge(zero_pool, 1)
                for dst, at in shifted(0, 0, HW)[0:2]:
                    a(dst, image[at], ACT.Copy).then_inc(pad_act, 1)

                def take_h(b, c, it):
                    act.wait_ge(h_sum, it + 2)
                    act.wait_ge(qk_sum, it + 1)
                    act.wait_ge(tm_sum, it + 1)
                    act.wait_ge(v_sum, b * NV + 1)
                    a(hT[C:P, :], p_h[C:P, 0:CH], ACT.Identity, bias=k.b3[C:P, :]).then_inc(hc_rdy, 1)
                    a(hTb[C:P, bass.ds(c * CH, CH)], p_h[C:P, 0:CH], ACT.Identity, bias=k.b3[C:P, :]).then_inc(h_rdy, 1)

                def high_part(it):
                    act.wait_ge(qk_sum, it + 2)
                    act.wait_ge(stored, it * 32 + 1)
                    act.wait_ge(am_rdy, it + 1)
                    a(part[:, 0, :], p_qk[:, 0:CH], ACT.Identity, bias=k.bqk[:]).then_inc(hi_rdy, 1)

                for b in range(B):
                    def chunk(c, it, age):
                        opens = isinstance(c, int) and c == 0
                        act.wait_ge(h1_sum, it + 1)
                        act.wait_ge(s_sum, it * NSLOT + 1)
                        a(h1[:], p_h1[0:C, 0:CH], ACT.Relu, bias=k.b1[:]).then_inc(h1_rdy, 1)
                        if opens and b:
                            take_h(b - 1, NCH - 1, it - 1)
                        for s in range(NSLOT):
                            act.wait_ge(s_sum, it * NSLOT + s + 2)
                            act.wait_ge(ts_rdy, it * NSLOT + max(0, s - 1) + 1)
                            a(th[:, s % 2, :], p_s[s % 2][:, 0:CH], ACT.Tanh, bias=k.b2[:, s:s + 1],
                              scale=0.5).then_inc(th_rdy, 1)
                            if s == 0 and not opens:
                                take_h(b, c - 1, it - 1)
                            if s == 2 and age == 2:
                                high_part(it - 2)
                    image_chunks(act, b, chunk)
                take_h(B - 1, NCH - 1, LAST)
                high_part(LAST - 1)
                high_part(LAST)

            @block.vector
            def _(dve):
                dve.sem_inc(ts_rdy, 1)
                dve.sem_inc(r1_rdy, 1)
                dve.sem_inc(tm_rdy, 1)
                dve.sem_inc(v_rdy, 1)
                dve.sem_inc(am_rdy, 1)
                v = nc.vector
                v.memset(pad_col[0][:], 0.0).then_inc(zero_dve, 1)
                dve.wait_ge(zero_dve, 1)
                dve.wait_ge(img_in, 32)
                for dst, at in shifted(0, 0, HW)[2:4]:
                    v.tensor_copy(dst, image[at]).then_inc(pad_dve, 1)
                v.memset(k.values[:, :, 0:KT - 1, HD], 1.0).then_inc(ones, 1)
                v.memset(k.values[0:TAIL, :, KT - 1, HD], 1.0).then_inc(ones, 1)

                def take_products(it):
                    dve.wait_ge(tm_sum, it + 2)
                    v.tensor_tensor(k.x_tm[:, bass.ds(it * 4, 4), :], p_tm[0:TM, 0:4 * C].rearrange(
                        "p (t c) -> p t c", c=C), k.bo[:].unsqueeze(1).to_broadcast([TM, 4, C]), ALU.add).then_inc(tm_rdy, 1)
                    dve.wait_ge(hi_rdy, it + 1)
                    dve.wait_ge(lo_rdy, it + 1)
                    v.scalar_tensor_tensor(out=rest[:], in0=p_qk[:, 0:CH], scalar=k.bqk[:], in1=part[:, 0, :],
                                           op0=ALU.add, op1=ALU.subtract).then_inc(r1_rdy, 1)
                    dve.wait_ge(stored, it * 32 + 1)
                    dve.wait_ge(r1_rdy, it + 2)
                    v.tensor_copy(part[:, 1, :], rest[:]).then_inc(mid_rdy, 1)
                    v.tensor_reduce(amax[:, bass.ds(it, 1)], part[:, 0, :], AX.X, ALU.max,
                                    apply_absolute_value=True).then_inc(am_rdy, 1)

                for b in range(B):
                    if b == 0:
                        dve.wait_ge(zero_pool, 3)
                        dve.wait_ge(pad_act, 2)
                        dve.wait_ge(pad_dve, 2)
                    else:
                        dve.wait_ge(pad_next, b * PIECES)
                    if b + 1 < B:
                        dve.wait_ge(img_in, b * 32 + 64)
                        dve.wait_ge(h_sum, b * NCH + 1)

                    def chunk(c, it, age):
                        if b + 1 < B:
                            for dst, at in shifted(b + 1, c * 8, 8):
                                v.tensor_copy(dst, image[at, bass.ds(c * 8, 8), :]).then_inc(pad_next, 1)
                        for s in range(NSLOT):
                            dve.wait_ge(th_rdy, it * NSLOT + s + 2)
                            if s == 0:
                                dve.wait_ge(h_sum, it + 1)
                            v.scalar_tensor_tensor(
                                out=ts[:, s, :].rearrange("p (r c) -> p r c", r=8),
                                in0=th[:, s % 2, :].rearrange("p (r c) -> p r c", r=8), scalar=1.0,
                                in1=window(slot_buf(b, s), c, TAPS_LO[s]), op0=ALU.add,
                                op1=ALU.mult).then_inc(ts_rdy, 1)
                            if s == 2 and age == 2:
                                take_products(it - 2)
                    image_chunks(dve, b, chunk)
                    for g in range(NV):
                        dve.wait_ge(v_sum, b * NV + g + 2)
                        n = min(8, KT - 8 * g)
                        m = P if n == 8 else TAIL
                        out = k.values[0:m, b * H:b * H + H, 8 * g:8 * g + n, 0:HD]
                        bias = k.bv[0:m, :].rearrange("p (h d) -> p h d", d=HD).unsqueeze(2).to_broadcast([m, H, n, HD])
                        v.tensor_tensor(out, p_v[g % 2][0:m, 0:n * C].rearrange("p (t h d) -> p h t d", h=H, d=HD),
                                        bias, ALU.add).then_inc(v_rdy, 1)
                take_products(LAST - 1)
                take_products(LAST)
                dve.wait_ge(am_rdy, B * NCH + 1)
                v.tensor_reduce(amax_b[:], amax[:].rearrange("p (b c) -> p b c", c=NCH), AX.X,
                                ALU.max).then_inc(bown, 1)
                dve.wait_ge(bown, 1)
                dve.wait_ge(kmv, 16)
                v.tensor_tensor(bound[:], amax_b[0:C, :], kmax[:], ALU.mult).then_inc(bmul, 1)
                dve.wait_ge(bsum, 1)
                v.tensor_reduce(bmx[:], p_h1[0:C, 0:B], AX.X, ALU.max).then_inc(bone, 1)
                dve.wait_ge(ball, 1)
                v.tensor_scalar(k.flag[:], bmx_all[0:1, :], SCORE_LIMIT, None, ALU.is_gt).then_inc(flagged, 1)
                dve.wait_ge(flagged, 1)


class Stage:

    LOADS = 8

    def __init__(self, k, ctx, name, n):
        nc = k.nc
        self.k = k
        self.q = [ctx.enter_context(nc.sbuf_tensor(f"{name}_q{i}", [P, NP], BF16)) for i in range(n)]
        self.kk = [ctx.enter_context(nc.sbuf_tensor(f"{name}_k{i}", [P, NP], BF16)) for i in range(n)]
        self.const_in = ctx.enter_context(nc.semaphore(f"{name}_constants"))
        self.q_cleared = ctx.enter_context(nc.semaphore(f"{name}_q_cleared"))
        self.k_cleared = ctx.enter_context(nc.semaphore(f"{name}_k_cleared"))

    def clear_q(self):
        for t in self.q:
            self.k.nc.gpsimd.memset(t[:], 0.0).then_inc(self.q_cleared, 1)

    def clear_k(self):
        for t in self.kk:
            self.k.nc.vector.memset(t[:], 0.0).then_inc(self.k_cleared, 1)

    def constants(self, sp):
        sp.wait_ge(self.q_cleared, len(self.q))
        sp.wait_ge(self.k_cleared, len(self.kk))
        for q, kk in zip(self.q, self.kk):
            sp.dma_start(q[BIAS_ROW:SHIFT_ROW, :], self.k.io["c_ones"]).then_inc(self.const_in, 16)
            sp.dma_start(kk[SHIFT_ROW:SHIFT_ROW + 3, :], self.k.io["c_ones"]).then_inc(self.const_in, 16)

    def load(self, sp, i, bh, sem):
        k = self.k
        r = 3 * HD
        for a in range(3):
            src = k.d_qk[a, 0, bass.ds(bh * HD, HD), :].unsqueeze(0).to_broadcast([3, HD, N])
            sp.dma_start(self.q[i][a * r:a * r + r, 0:N], src).then_inc(sem, 16)
            src = k.d_qk[:, 1, bass.ds(bh * HD, HD), :]
            sp.dma_start(self.kk[i][a * r:a * r + r, 0:N], src).then_inc(sem, 16)
        sp.dma_start(self.kk[i][BIAS_ROW:SHIFT_ROW, 0:N],
                     k.d_bias[bass.ds(bh, 1), :, 0:N].rearrange("o a n -> (o a) n")).then_inc(sem, 16)
        sp.dma_start(self.q[i][SHIFT_ROW:SHIFT_ROW + 3, :],
                     k.d_shift[bass.ds(bh, 1)].rearrange("o a n -> (o a) n")).then_inc(sem, 16)


def maximum_phase(k):
    nc = k.nc
    with ExitStack() as ctx:
        def sem(name):
            return ctx.enter_context(nc.semaphore(name))

        def sb(name, shape, dt):
            return ctx.enter_context(nc.sbuf_tensor(name, shape, dt))

        stage = k.stage
        rowmax = sb("row_max", [P, KT], F32)
        parts = sb("shift_parts_tm", [P, 3, KT], BF16)
        rows = sb("shift_rows", [3 * KT, P], BF16)
        scores = ctx.enter_context(nc.psum_tensor("max_scores", [P, NCH, 512], F32))
        turned = ctx.enter_context(nc.psum_tensor("max_turned", [P, 1024], BF16))
        staged = sem("max_staged")
        scored = sem("max_scored")
        reduced = sem("max_reduced")
        split = sem("max_split")
        flipped = sem("max_flipped")
        rowed = sem("max_rowed")
        stored = sem("max_stored")
        one = sem("max_step")
        with nc.Block() as block:
            @block.gpsimd
            def _(pool):
                stage.clear_q()

            @block.sync
            def _(sp):
                sp.sem_inc(stored, 1)
                stage.constants(sp)
                sp.wait_ge(stage.const_in, 64)
                need = sp.value_load(k.flag[0:1, 0:1], min_val=0, max_val=1)
                with sp.If(need > 0):
                    with sp.Fori(0, B * H) as bh:
                        sp.wait_ge(split, bh + 1)
                        stage.load(sp, 0, bh, staged)
                        sp.wait_ge(rowed, bh + 1)
                        sp.dma_start(k.d_shift[bass.ds(bh, 1)].rearrange("o a (t p) -> (o a t) p", p=P),
                                     rows[:]).then_inc(stored, 16)
                    sp.wait_ge(stored, 16 * B * H + 1)

            @block.tensor
            def _(pe):
                pe.wait_ge(stage.const_in, 64)
                need = pe.value_load(k.flag[0:1, 0:1], min_val=0, max_val=1)
                with pe.If(need > 0):
                    with pe.Fori(0, B * H) as bh:
                        with pe.Fori(0, KT) as t:
                            pe.wait_ge(staged, bh * (16 * Stage.LOADS) + 16 * Stage.LOADS)
                            pe.wait_ge(reduced, bh * KT + t + 1)
                            for c in range(NCH):
                                mm = nc.tensor.matmul(scores[:, c, 0:CH], stage.q[0][:, bass.ds(t * P, P)],
                                                      stage.kk[0][:, c * CH:c * CH + CH], start=True, stop=True)
                            mm.then_inc(scored, 1)
                        pe.wait_ge(split, bh + 2)
                        pe.wait_ge(stage.const_in, 64)
                        nc.tensor.transpose(turned[0:3 * KT, 0:P], parts[:].rearrange("p a t -> p (a t)"),
                                            k.ident_bf[:]).then_inc(flipped, 1)

            @block.vector
            def _(dve):
                dve.sem_inc(split, 1)
                dve.sem_inc(reduced, 1)
                v = nc.vector
                step = Steps(dve, one)
                stage.clear_k()
                dve.wait_ge(stage.const_in, 64)
                need = dve.value_load(k.flag[0:1, 0:1], min_val=0, max_val=1)
                with dve.If(need > 0):
                    with dve.Fori(0, B * H) as bh:
                        with dve.Fori(0, KT) as t:
                            dve.wait_ge(scored, bh * KT + t + 1)
                            v.tensor_reduce(rowmax[:, bass.ds(t, 1)], scores[:, :, 0:CH], AX.XY,
                                            ALU.max).then_inc(reduced, 1)
                        dve.wait_ge(reduced, bh * KT + KT + 1)
                        step.loop(bh * 5)
                        step(v.tensor_scalar(rowmax[:], rowmax[:], -1.0, None, ALU.mult))
                        step(v.tensor_copy(parts[:, 0, :], rowmax[:]))
                        step(v.tensor_tensor(rowmax[:], rowmax[:], parts[:, 0, :], ALU.subtract))
                        step(v.tensor_copy(parts[:, 1, :], rowmax[:]))
                        step(v.tensor_tensor(rowmax[:], rowmax[:], parts[:, 1, :], ALU.subtract))
                        v.tensor_copy(parts[:, 2, :], rowmax[:]).then_inc(split, 1)
                        dve.wait_ge(stored, bh * 16 + 1)
                        dve.wait_ge(flipped, bh + 1)
                        v.tensor_copy(rows[:], turned[0:3 * KT, 0:P]).then_inc(rowed, 1)


class Denominators:

    SEG = N * H // P

    def __init__(self, k, ctx, name, images):
        nc = k.nc
        self.k, self.at = k, slice(images[0] * H, images[-1] * H + H)
        n = len(images)
        self.den = ctx.enter_context(nc.sbuf_tensor(f"{name}_denominators", [P, n, GROUPS, self.SEG], F32))
        self.total = ctx.enter_context(nc.sbuf_tensor(f"{name}_sums", [P, n, self.SEG], F32))
        self.rec = ctx.enter_context(nc.sbuf_tensor(f"{name}_recips", [P, n, self.SEG], F32))
        self.loaded = ctx.enter_context(nc.semaphore(f"{name}_denominators_in"))
        self.ready = ctx.enter_context(nc.semaphore(f"{name}_recips_ready"))
        self.written = ctx.enter_context(nc.semaphore(f"{name}_recips_stored"))

    def load(self, sp):
        for g in range(GROUPS):
            sp.dma_start(self.den[:, :, g, :], self.k.d_den[g, self.at].rearrange(
                "(b h) (j n) -> (h j) b n", h=H, n=self.SEG)).then_inc(self.loaded, 16)

    def vector(self, dve):
        v = self.k.nc.vector
        dve.wait_ge(self.loaded, 16 * GROUPS)
        v.tensor_reduce(self.total[:], self.den[:].rearrange("p b g n -> p b n g"), AX.X, ALU.add).then_inc(self.ready, 1)
        dve.wait_ge(self.ready, 1)
        v.reciprocal(self.rec[:], self.total[:]).then_inc(self.ready, 1)

    def store(self, sp):
        sp.wait_ge(self.ready, 2)
        sp.dma_start(self.k.d_recip[self.at].rearrange("(b h) (j n) -> (h j) b n", h=H, n=self.SEG),
                     self.rec[:]).then_inc(self.written, 16)


def attention_phase(k):
    nc = k.nc
    UNIT = 2
    UNITS = (KT - 1) // UNIT
    AHEAD = 3
    RING = 6
    PAIRS = B * H // 2
    TAIL_EXP_AT, TAIL_AT = 2, 6
    BATCHES = (KT - 1) // GROUPS
    SPARE = RING * UNIT // GROUPS
    assert UNITS % AHEAD == 0 and UNITS % RING == 0 and BATCHES * GROUPS == UNITS * UNIT

    def unit_of(g):
        return (g * GROUPS + GROUPS - 1) // UNIT

    def freed_by(u):
        return ((u - RING) * UNIT + UNIT - 1) // GROUPS + 1
    with ExitStack() as ctx:
        def sem(name):
            return ctx.enter_context(nc.semaphore(name))

        def sb(name, shape, dt):
            return ctx.enter_context(nc.sbuf_tensor(name, shape, dt))

        def psum(name, shape):
            return ctx.enter_context(nc.psum_tensor(name, shape, F32))

        stage = k.stage
        dens = Denominators(k, ctx, "first", range(B - 1))
        assert (B - 1) * H <= 2 * (PAIRS - 1)
        vst = [sb(f"stage_v{i}", [P, KT, HD + 1], F32) for i in range(2)]
        probs = sb("probs", [P, RING * UNIT, CH], F32)
        ptail = sb("probs_tail", [P, CH], F32)
        mixed = [sb(f"mixed{i}", [P, N], F32) for i in range(2)]
        p_sc = [psum(f"p_scores{i}", [P, UNIT, 512]) for i in range(AHEAD)]
        p_tl = psum("p_tail", [P, 512])
        p_mx = psum("p_mixed", [P, 512])

        staged = [sem(f"staged{i}") for i in range(2)]
        v_staged = [sem(f"values_staged{i}") for i in range(2)]
        s_rdy = sem("scores_ready")
        e_rdy = sem("exps_ready")
        used = sem("exps_used")
        t_rdy = sem("tail_ready")
        te_rdy = sem("tail_exp_ready")
        t_used = sem("tail_exp_used")
        mx_out = sem("mixed_taken")
        stored = [sem(f"mixed_stored{i}") for i in range(2)]
        tail_clean = sem("tail_slot_zeroed")
        sums_clean = sem("sums_bank_zeroed")

        with nc.Block() as block:
            @block.gpsimd
            def _(pool):
                nc.gpsimd.memset(ptail[:], 0.0).then_inc(tail_clean, 1)
                for i in range(2):
                    nc.gpsimd.tensor_copy(vst[i][:], k.values[:, i]).then_inc(v_staged[i], 1)
                with pool.Fori(0, PAIRS - 1) as pair:
                    for i in range(2):
                        pool.wait_ge(used, (pair * 2 + i + 1) * (BATCHES * NCH) + SPARE)
                        nc.gpsimd.tensor_copy(vst[i][:], k.values[:, bass.ds(pair * 2 + 2 + i, 1)].rearrange(
                            "p o t d -> p (o t) d")).then_inc(v_staged[i], 1)

            @block.sync
            def _(sp):
                sp.sem_inc(stored[0], 1)
                sp.sem_inc(stored[1], 1)
                def store(i, pair):
                    sp.wait_ge(mx_out, (pair * 2 + i) * NCH + NCH + 1)
                    for g in range(GROUPS):
                        bh = pair * 2 + i
                        sp.dma_start(k.d_mix[bass.ds(bh * HD, HD), g, :],
                                     mixed[i][32 * g:32 * g + HD, :]).then_inc(stored[i], 16)
                        sp.dma_start(k.d_den[g, bass.ds(bh, 1), :],
                                     mixed[i][32 * g + HD:32 * g + HD + 1, :]).then_inc(stored[i], 16)

                for i in range(2):
                    stage.load(sp, i, i, staged[i])
                with sp.Fori(0, PAIRS - 1) as pair:
                    for i in range(2):
                        store(i, pair)
                        sp.wait_ge(s_rdy, (pair * 2 + i + 1) * (UNITS * NCH))
                        stage.load(sp, i, pair * 2 + 2 + i, staged[i])
                for i in range(2):
                    sp.wait_ge(stored[i], 32 * GROUPS * (PAIRS - 1) + 1)
                dens.load(sp)
                for i in range(2):
                    store(i, PAIRS - 1)
                dens.store(sp)
                sp.wait_ge(dens.written, 16)
                for i in range(2):
                    sp.wait_ge(stored[i], 32 * GROUPS * PAIRS + 1)

            @block.tensor
            def _(pe):
                mm = nc.tensor.matmul

                def scores(i, c, it, u):
                    pe.wait_ge(e_rdy, it * UNITS + u + 1)
                    for j in range(UNIT):
                        t = u * UNIT + j
                        m = mm(p_sc[u % AHEAD][:, j, 0:CH], stage.kk[i][:, t * P:t * P + P],
                               stage.q[i][:, bass.ds(c * CH, CH)], start=True, stop=True)
                    m.then_inc(s_rdy, 1)

                def tail_scores(i, c, it):
                    pe.wait_ge(te_rdy, it + 1)
                    mm(p_tl[:, 0:CH], stage.kk[i][:, (KT - 1) * P:KT * P], stage.q[i][:, bass.ds(c * CH, CH)],
                       start=True, stop=True).then_inc(t_rdy, 1)

                def mix(i, it, g):
                    if g == 0:
                        pe.wait_ge(mx_out, it + 1)
                    pe.wait_ge(e_rdy, it * UNITS + unit_of(g) + 1 + AHEAD)
                    for j in range(GROUPS):
                        t = g * GROUPS + j
                        m = mm(p_mx[32 * j:32 * j + HD + 1, 0:CH], vst[i][:, t, :], probs[:, t % (RING * UNIT), :],
                               start=(g == 0), stop=(g == BATCHES - 1))
                    m.then_inc(used, 1)

                def tail_mix(i, it):
                    pe.wait_ge(te_rdy, it + 2)
                    mm(p_mx[0:HD + 1, 0:CH], vst[i][:, KT - 1, :], ptail[:], start=False, stop=False).then_inc(t_used, 1)

                def chunk(i, c, bh, ahead):
                    it = bh * NCH + c
                    tail_scores(i, c, it)
                    for u in range(UNITS):
                        if u + AHEAD < UNITS:
                            scores(i, c, it, u + AHEAD)
                        else:
                            ahead(u + AHEAD - UNITS)
                        batches = [g for g in range(BATCHES) if unit_of(g) == u]
                        for g in batches:
                            mix(i, it, g)
                        if u == TAIL_AT:
                            tail_mix(i, it)

                pe.sem_inc(used, SPARE)
                pe.sem_inc(t_used, 1)
                pe.wait_ge(tail_clean, 1)
                pe.wait_ge(sums_clean, 1)
                pe.wait_ge(stage.const_in, 64)
                def head(pair, i, last):
                    bh = pair * 2 + i
                    with pe.Fori(0, NCH - 1) as c:
                        pe.wait_ge(v_staged[i], pair + 1)
                        chunk(i, c, bh, lambda u: scores(i, c + 1, bh * NCH + c + 1, u))

                    def next_head(u):
                        if not last:
                            if u == 0:
                                pe.wait_ge(staged[1 - i], (pair + 1 + i) * 16 * Stage.LOADS)
                            scores(1 - i, 0, bh * NCH + NCH, u)
                    chunk(i, NCH - 1, bh, next_head)

                pe.wait_ge(staged[0], 16 * Stage.LOADS)
                for u in range(AHEAD):
                    scores(0, 0, 0, u)
                with pe.Fori(0, PAIRS - 1) as pair:
                    head(pair, 0, False)
                    head(pair, 1, False)
                head(PAIRS - 1, 0, False)
                head(PAIRS - 1, 1, True)

            @block.scalar
            def _(act):
                act.sem_inc(e_rdy, AHEAD)
                act.sem_inc(te_rdy, 1)
                act.wait_ge(tail_clean, 1)
                a = nc.scalar.activation
                with act.Fori(0, B * H * NCH) as it:
                    for u in range(UNITS):
                        act.wait_ge(s_rdy, it * UNITS + u + 1)
                        act.wait_ge(used, it * BATCHES + freed_by(u) + SPARE)
                        at = (u % RING) * UNIT
                        a(probs[:, at:at + UNIT, :], p_sc[u % AHEAD][:, :, 0:CH], ACT.Exp).then_inc(e_rdy, 1)
                        if u == TAIL_EXP_AT:
                            act.wait_ge(t_rdy, it + 1)
                            act.wait_ge(t_used, it + 1)
                            a(ptail[0:TAIL, :], p_tl[0:TAIL, 0:CH], ACT.Exp).then_inc(te_rdy, 1)

            @block.vector
            def _(dve):
                dve.sem_inc(mx_out, 1)
                v = nc.vector
                v.memset(p_mx[:], 0.0).then_inc(sums_clean, 1)

                def head(pair, i):
                    with dve.Fori(0, NCH) as c:
                        it = c + (pair * 2 + i) * NCH
                        dve.wait_ge(stored[i], pair * (32 * GROUPS) + 1)
                        dve.wait_ge(used, it * BATCHES + BATCHES + SPARE)
                        v.tensor_copy(mixed[i][:, bass.ds(c * CH, CH)], p_mx[:, 0:CH]).then_inc(mx_out, 1)

                with dve.Fori(0, PAIRS - 1) as pair:
                    head(pair, 0)
                    head(pair, 1)
                head(PAIRS - 1, 0)
                dens.vector(dve)
                head(PAIRS - 1, 1)


def project_phase(k):
    nc = k.nc
    with ExitStack() as ctx:
        def sem(name):
            return ctx.enter_context(nc.semaphore(name))

        def sb(name, shape, dt):
            return ctx.enter_context(nc.sbuf_tensor(name, shape, dt))

        dens = Denominators(k, ctx, "last", [B - 1])
        num = [sb(f"numerators{i}", [P, GROUPS, CH], F32) for i in range(2)]
        rcb = [sb(f"recips{i}", [P, CH], F32) for i in range(2)]
        low = [sb(f"num_low{i}", [P, CH], F32) for i in range(2)]
        high = [sb(f"num_high{i}", [P, CH], F32) for i in range(2)]
        o = [sb(f"attn_out{i}", [P, CH], F32) for i in range(2)]
        p_y = [ctx.enter_context(nc.psum_tensor(f"p_y{i}", [P, 2, 512], F32)) for i in range(2)]
        num_in = [sem(f"numerators_in{i}") for i in range(2)]
        hi_rdy = sem("high_sums_ready")
        steps = sem("project_step")
        o_rdy = sem("out_ready")
        y_sum = sem("projected")
        y_rdy = sem("residual_added")
        IT = B * NCH // 2

        with nc.Block() as block:
            @block.sync
            def _(sp):
                dens.load(sp)
                for b in range(2):
                    if b:
                        dens.store(sp)
                        sp.wait_ge(dens.written, 16)
                    for c in range(NCH):
                        i = c % 2
                        sp.wait_ge(o_rdy, b * NCH + max(0, c - 1) + 1)
                        cols = slice(c * CH, c * CH + CH)
                        for half in range(2):
                            at = slice(half * C, half * C + C)
                            rows = bass.ds(b * C + half * 2 * C, C)
                            heads = bass.ds(b * H + half * 2 * H, H)
                            sp.dma_start(num[i][at, :, :], k.d_mix[rows, :, cols]).then_inc(num_in[i], 16)
                            sp.dma_start(rcb[i][at, :], k.d_recip[heads, cols].unsqueeze(1).to_broadcast(
                                [H, HD, CH])).then_inc(num_in[i], 16)

            @block.gpsimd
            def _(pool):
                with pool.Fori(0, 2) as b:
                    for c in range(NCH):
                        i = c % 2
                        n = (NCH + 1) // 2 if i == 0 else NCH // 2
                        pool.wait_ge(o_rdy, b * NCH + max(0, c - 1) + 1)
                        pool.wait_ge(num_in[i], b * (n * 64) + (c // 2 + 1) * 64)
                        nc.gpsimd.tensor_tensor(high[i][:], num[i][:, 2, :], num[i][:, 3, :], ALU.add).then_inc(hi_rdy, 1)

            @block.vector
            def _(dve):
                dve.sem_inc(o_rdy, 1)
                dve.sem_inc(y_rdy, 1)
                v = nc.vector
                step = Steps(dve, steps)

                def add(b, c):
                    dve.wait_ge(y_sum, b * NCH + c + 2)
                    for half in range(2):
                        x = k.x_tm[:, bass.ds(b * NT + half * 2 * NT + c * 4, 4), :]
                        v.tensor_tensor(x, x, p_y[c % 2][0:TM, half, 0:4 * C].rearrange("p (t c) -> p t c", c=C),
                                        ALU.add).then_inc(y_rdy, 1)

                for b in range(2):
                    for c in range(NCH):
                        it = b * NCH + c
                        i = c % 2
                        n = (NCH + 1) // 2 if i == 0 else NCH // 2
                        step.loop(it * 2)
                        dve.wait_ge(num_in[i], b * (n * 64) + (c // 2 + 1) * 64)
                        step(v.tensor_tensor(low[i][:], num[i][:, 0, :], num[i][:, 1, :], ALU.add))
                        dve.wait_ge(hi_rdy, it + 1)
                        step(v.tensor_tensor(low[i][:], low[i][:], high[i][:], ALU.add))
                        dve.wait_ge(y_sum, b * NCH + max(0, c - 1) + 1)
                        v.tensor_tensor(o[i][:], low[i][:], rcb[i][:], ALU.mult).then_inc(o_rdy, 1)
                        if c:
                            add(b, c - 1)
                        if b == 0 and c == 1:
                            dens.vector(dve)
                    add(b, NCH - 1)

            @block.tensor
            def _(pe):
                pe.sem_inc(y_sum, 1)
                with pe.Fori(0, 2) as b:
                    for c in range(NCH):
                        it = b * NCH + c
                        i = c % 2
                        pe.wait_ge(y_rdy, b * (2 * NCH) + 2 * max(0, c - 1) + 1)
                        pe.wait_ge(o_rdy, it + 2)
                        for half in range(2):
                            at = slice(half * C, half * C + C)
                            for j in range(4):
                                m = nc.tensor.matmul(p_y[i][0:TM, half, j * C:j * C + C],
                                                     o[i][at, j * TM:j * TM + TM], k.wo[at, :], start=True, stop=True)
                        m.then_inc(y_sum, 1)


class Norm:

    STEPS = 4

    def __init__(self, k, ctx, name):
        nc = k.nc
        self.k = k
        self.sq = [ctx.enter_context(nc.sbuf_tensor(f"{name}_squares{i}", [TM, NT, C], F32)) for i in range(2)]
        self.stat = ctx.enter_context(nc.sbuf_tensor(f"{name}_stats", [TM, 4, B, NT], F32))
        self.eps = ctx.enter_context(nc.sbuf_tensor(f"{name}_eps", [TM, 1], F32))
        self.centred = ctx.enter_context(nc.semaphore(f"{name}_centred"))
        self.squared = ctx.enter_context(nc.semaphore(f"{name}_squared"))
        self.summed = ctx.enter_context(nc.semaphore(f"{name}_summed"))
        self.rooted = ctx.enter_context(nc.semaphore(f"{name}_rooted"))
        self.done = ctx.enter_context(nc.semaphore(f"{name}_done"))
        self.step = Steps(nc.vector, ctx.enter_context(nc.semaphore(f"{name}_step")))
        self.eps_set = ctx.enter_context(nc.semaphore(f"{name}_eps_set"))

    def vector(self, dve, x, before=None, after=None):
        v, st, step = self.k.nc.vector, self.stat, self.step
        v.memset(self.eps[:], EPS).then_inc(self.eps_set, 1)

        def centre(b):
            if before is not None:
                before(b)
            xb = x[:, b * NT:b * NT + NT, :]
            step(v.tensor_reduce(st[:, 0, b, :], xb, AX.X, ALU.add))
            step(v.tensor_scalar(st[:, 0, b, :], st[:, 0, b, :], 1.0 / C, None, ALU.mult))
            v.tensor_tensor(xb, xb, st[:, 0, b, :].unsqueeze(2).to_broadcast([TM, NT, C]),
                            ALU.subtract).then_inc(self.centred, 1)

        def scale(b):
            xb = x[:, b * NT:b * NT + NT, :]
            dve.wait_ge(self.squared, b + 1)
            v.tensor_reduce(st[:, 1, b, :], self.sq[b % 2][:], AX.X, ALU.add).then_inc(self.summed, 1)
            dve.wait_ge(self.rooted, b + 1)
            step(v.reciprocal(st[:, 3, b, :], st[:, 2, b, :]))
            step(v.tensor_tensor(xb, xb, st[:, 3, b, :].unsqueeze(2).to_broadcast([TM, NT, C]), ALU.mult))
            if after is not None:
                after(b)
            v.memset(st[0:1, 0, b, 0:1], 0.0).then_inc(self.done, 1)

        centre(0)
        for b in range(B):
            if b + 1 < B:
                centre(b + 1)
            scale(b)

    def scalar(self, act, x):
        a, st = self.k.nc.scalar.activation, self.stat

        def square(b):
            act.wait_ge(self.centred, b + 1)
            if b >= 2:
                act.wait_ge(self.summed, b - 1)
            a(self.sq[b % 2][:], x[:, b * NT:b * NT + NT, :], ACT.Square).then_inc(self.squared, 1)

        act.wait_ge(self.eps_set, 1)
        square(0)
        for b in range(B):
            if b + 1 < B:
                square(b + 1)
            act.wait_ge(self.summed, b + 1)
            a(st[:, 2, b, :], st[:, 1, b, :], ACT.Sqrt, bias=self.eps[:], scale=1.0 / C).then_inc(self.rooted, 1)


def moe_phase(k):
    nc, io = k.nc, k.io
    x_tm = k.x_tm
    NTA = B * NT
    CHUNKS = B * NCH
    with ExitStack() as ctx:
        def sem(name):
            return ctx.enter_context(nc.semaphore(name))

        def sb(name, shape, dt):
            return ctx.enter_context(nc.sbuf_tensor(name, shape, dt))

        def split3(step, v, raw, parts, rest):
            step(v.tensor_copy(parts[0], raw))
            step(v.tensor_tensor(rest, raw, parts[0], ALU.subtract))
            step(v.tensor_copy(parts[1], rest))
            step(v.tensor_tensor(rest, rest, parts[1], ALU.subtract))
            step(v.tensor_copy(parts[2], rest))

        w1l = sb("expert_w1_parts", [P, 3, EXP, FF], BF16)
        gwl = sb("gate_w_parts", [P, 3, EXP], BF16)
        w2f = sb("expert_w2", [FF, EXP, C], F32)
        b1t = sb("expert_b1", [FF, EXP], F32)
        b2l = sb("expert_b2_parts", [3 * EXP, 3, C], BF16)
        sel = sb("expert_selector", [3 * EXP, EXP, FF], BF16)
        fold = sb("fold", [P, C], F32)
        gb = sb("gate_b", [TM, EXP], F32)
        gamma = sb("gamma", [TM, C], F32)
        beta = sb("beta", [TM, C], F32)
        eidx = sb("expert_index", [TM, EXP], F32)
        x_hm = sb("x_hi_mid", [P, B * N], BF16)
        x_hl = sb("x_hi_lo", [P, B * N], BF16)
        gates = sb("gate_parts", [TM, NTA, 3 * EXP], BF16)
        loaded = sem("moe_loaded")
        LOADED = 16 * 15
        carrier = sem("wait_carrier")

        with ExitStack() as c1:
            norm = Norm(k, c1, "norm1")
            w1raw = c1.enter_context(nc.sbuf_tensor("w1_raw", [P, EXP, FF], F32))
            w1rest = c1.enter_context(nc.sbuf_tensor("w1_rest", [P, EXP, FF], F32))
            gwraw = c1.enter_context(nc.sbuf_tensor("gw_raw", [P, EXP], F32))
            gwrest = c1.enter_context(nc.sbuf_tensor("gw_rest", [P, EXP], F32))
            b1raw = c1.enter_context(nc.sbuf_tensor("b1_raw", [EXP, FF], F32))
            b2raw = c1.enter_context(nc.sbuf_tensor("eb2_raw", [3 * EXP, C], F32))
            b2rest = c1.enter_context(nc.sbuf_tensor("b2_rest", [3 * EXP, C], F32))
            pb = c1.enter_context(nc.psum_tensor("p_b1", [P, 512], F32))
            b1_in = c1.enter_context(nc.semaphore("b1_in"))
            b1_flip = c1.enter_context(nc.semaphore("b1_flipped"))
            wsteps = c1.enter_context(nc.semaphore("moe_weight_step"))
            with nc.Block() as block:
                @block.sync
                def _(sp):
                    sp.dma_start(b1raw[:], io["L0_ffn_b1"]).then_inc(b1_in, 16)

                    def load(dst, src):
                        sp.dma_start(dst, src).then_inc(loaded, 16)

                    for half in range(2):
                        at = slice(half * C, half * C + C)
                        load(w1raw[at], io["L0_ffn_w1"].rearrange("e c f -> c e f"))
                        load(gwraw[at], io["L0_ffn_gate_w"])
                        load(fold[at, :], io["c_ident"][0:C, 0:C])
                    for a in range(3):
                        load(b2raw[a * EXP:a * EXP + EXP, :], io["L0_ffn_b2"])
                    load(sel[:], io["c_select"])
                    load(w2f[:], io["L0_ffn_w2"].rearrange("e f c -> f e c"))
                    load(eidx[:], io["c_index"][0:TM, 0:EXP])
                    for t, name in ((gb, "gate_b"), (gamma, "gamma"), (beta, "beta")):
                        load(t[:], io["L0_ffn_" + name].partition_broadcast(TM))

                @block.tensor
                def _(pe):
                    pe.wait_ge(b1_in, 16)
                    nc.tensor.transpose(pb[:, 0:EXP], b1raw[:], k.ident[0:EXP, 0:EXP]).then_inc(b1_flip, 1)

                @block.scalar
                def _(act):
                    norm.scalar(act, x_tm)

                @block.vector
                def _(dve):
                    v = nc.vector
                    norm.vector(dve, x_tm)
                    step = Steps(dve, wsteps)
                    dve.wait_ge(loaded, LOADED)
                    split3(step, v, w1raw[:], [w1l[:, a] for a in range(3)], w1rest[:])
                    split3(step, v, gwraw[:], [gwl[:, a] for a in range(3)], gwrest[:])
                    split3(step, v, b2raw[:], [b2l[:, a] for a in range(3)], b2rest[:])
                    for w in (w1l, gwl):
                        step(v.tensor_copy(w[C:P, 2], w[C:P, 0]))
                    dve.wait_ge(b1_flip, 1)
                    step(v.tensor_copy(b1t[:], pb[:, 0:EXP]))

        with ExitStack() as c2:
            def sb2(name, shape, dt):
                return c2.enter_context(nc.sbuf_tensor(name, shape, dt))

            def sem2(name):
                return c2.enter_context(nc.semaphore(name))

            xd = [sb2(f"x_doubled{i}", [TM, 4, 2, C], F32) for i in range(2)]
            rest = sb2("x_rest", [P, CH], F32)
            lg = sb2("logits", [TM, 4, EXP], F32)
            m8 = sb2("largest", [TM, 4, 8], F32)
            i8 = sb2("largest_index", [TM, 4, 8], U32)
            top = sb2("top_logits", [TM, NTA, 2], F32)
            topi = sb2("top_index", [TM, NTA, 2], F32)
            wgt = sb2("top_weights", [TM, 4, NTA], F32)
            one_hot = sb2("gate_one_hot", [TM, NTA, EXP], F32)
            gate = sb2("gate_full", [TM, NTA, EXP], F32)
            p_x = [c2.enter_context(nc.psum_tensor(f"p_x{i}", [P, 512], F32)) for i in range(2)]
            p_lg = c2.enter_context(nc.psum_tensor("p_logits", [P, 512], F32))
            doubled = sem2("x_doubled_ready")
            flipped = sem2("x_flipped")
            hi_rdy = sem2("x_hi_ready")
            rest_rdy = sem2("x_rest_ready")
            mid_rdy = sem2("x_mid_ready")
            lo_rdy = sem2("x_lo_ready")
            lg_sum = sem2("logits_summed")
            lg_rdy = sem2("logits_ready")
            tops = sem2("router_step")
            diff = sem2("difference_ready")
            expd = sem2("difference_exp")
            gstep = sem2("gate_step")
            with nc.Block() as block:
                @block.gpsimd
                def _(pool):
                    with pool.Fori(0, NTA // 8) as it2:
                        for i in range(2):
                            it = it2 * 2 + i
                            pool.wait_ge(flipped, it + 1)
                            for d in range(2):
                                nc.gpsimd.tensor_copy(xd[i][:, :, d, :], x_tm[:, bass.ds(it * 4, 4), :]).then_inc(doubled, 1)

                @block.tensor
                def _(pe):
                    pe.sem_inc(flipped, 2)

                    def flip(i, it):
                        pe.wait_ge(doubled, it * 2 + 2)
                        pe.wait_ge(rest_rdy, it + 1)
                        for j in range(4):
                            m = nc.tensor.transpose(p_x[i][:, j * TM:j * TM + TM],
                                                    xd[i][:, j].rearrange("p d c -> p (d c)"), k.ident[0:TM, 0:TM])
                        m.then_inc(flipped, 1)

                    def logits(it):
                        pe.wait_ge(mid_rdy, it + 1)
                        pe.wait_ge(lo_rdy, it + 2)
                        pe.wait_ge(lg_rdy, it + 1)
                        for j in range(4):
                            at = bass.ds(it * CH + j * TM, TM)
                            for a, xs in enumerate((x_hm, x_hm, x_hl)):
                                m = nc.tensor.matmul(p_lg[0:TM, j * EXP:j * EXP + EXP], xs[:, at], gwl[:, a, :],
                                                     start=(a == 0), stop=(a == 2))
                        m.then_inc(lg_sum, 1)

                    flip(0, 0)
                    with pe.Fori(0, NTA // 8 - 1) as it2:
                        for i in range(2):
                            it = it2 * 2 + i
                            flip(1 - i, it + 1)
                            logits(it)
                    flip(1, CHUNKS - 1)
                    logits(CHUNKS - 2)
                    logits(CHUNKS - 1)

                @block.scalar
                def _(act):
                    a = nc.scalar.activation
                    with act.Fori(0, NTA // 8) as it2:
                        for i in range(2):
                            it = it2 * 2 + i
                            act.wait_ge(flipped, it + 3)
                            at = bass.ds(it * CH, CH)
                            a(x_hm[:, at], p_x[i][:, 0:CH], ACT.Identity).then_inc(hi_rdy, 1)
                            a(x_hl[0:C, at], p_x[i][0:C, 0:CH], ACT.Identity).then_inc(hi_rdy, 1)
                    act.wait_ge(diff, 1)
                    a(wgt[:, 1, :], wgt[:, 0, :], ACT.Exp).then_inc(expd, 1)

                @block.vector
                def _(dve):
                    dve.sem_inc(rest_rdy, 2)
                    dve.sem_inc(lg_rdy, 1)
                    dve.sem_inc(lo_rdy, 1)
                    v = nc.vector

                    def split_rest(i, it):
                        dve.wait_ge(hi_rdy, it * 2 + 2)
                        dve.wait_ge(lo_rdy, it + 1)
                        v.tensor_tensor(rest[:], p_x[i][:, 0:CH], x_hm[:, bass.ds(it * CH, CH)],
                                        ALU.subtract).then_inc(rest_rdy, 1)

                    def split_middle(it):
                        dve.wait_ge(rest_rdy, it + 3)
                        v.tensor_copy(x_hm[C:P, bass.ds(it * CH, CH)], rest[C:P, :]).then_inc(mid_rdy, 1)

                    def split_low(it):
                        at = bass.ds(it * CH, CH)
                        dve.wait_ge(mid_rdy, it + 1)
                        v.tensor_tensor(x_hl[C:P, at], rest[C:P, :], x_hm[C:P, at], ALU.subtract).then_inc(lo_rdy, 1)

                    def take_logits(it):
                        dve.wait_ge(lg_sum, it + 1)
                        v.tensor_tensor(lg[:], p_lg[0:TM, 0:4 * EXP].rearrange("p (t e) -> p t e", e=EXP),
                                        gb[:].unsqueeze(1).to_broadcast([TM, 4, EXP]), ALU.add).then_inc(lg_rdy, 1)

                    def largest(it):
                        dve.wait_ge(lg_rdy, it + 2)
                        dve.sem_inc(carrier, 1)
                        for j in range(4):
                            m = v.max(m8[:, j, :], lg[:, j, :])
                        m.then_inc(tops, 1)

                    def largest_index(it):
                        dve.wait_ge(tops, it * 4 + 1)
                        dve.sem_inc(carrier, 1)
                        for j in range(4):
                            m = v.max_index(i8[:, j, :], m8[:, j, :], lg[:, j, :])
                        m.then_inc(tops, 1)

                    def keep_two(it):
                        v.tensor_copy(top[:, bass.ds(it * 4, 4), :], m8[:, :, 0:2]).then_inc(tops, 1)
                        dve.wait_ge(tops, it * 4 + 2)
                        v.tensor_copy(topi[:, bass.ds(it * 4, 4), :], i8[:, :, 0:2]).then_inc(tops, 1)
                        dve.wait_ge(tops, it * 4 + 4)

                    split_rest(0, 0)
                    split_middle(0)
                    split_low(0)
                    with dve.Fori(0, NTA // 8 - 1) as it2:
                        for i in range(2):
                            it = it2 * 2 + i
                            split_rest(1 - i, it + 1)
                            take_logits(it)
                            split_middle(it + 1)
                            largest(it)
                            split_low(it + 1)
                            largest_index(it)
                            keep_two(it)
                    split_rest(1, CHUNKS - 1)
                    split_middle(CHUNKS - 1)
                    split_low(CHUNKS - 1)
                    for it in (CHUNKS - 2, CHUNKS - 1):
                        take_logits(it)
                        largest(it)
                        largest_index(it)
                        keep_two(it)
                    v.tensor_tensor(wgt[:, 0, :], top[:, :, 1], top[:, :, 0], ALU.subtract).then_inc(diff, 1)
                    dve.wait_ge(expd, 1)
                    step = Steps(dve, gstep)
                    step(v.tensor_scalar(wgt[:, 0, :], wgt[:, 1, :], 1.0, None, ALU.add))
                    step(v.reciprocal(wgt[:, 2, :], wgt[:, 0, :]))
                    step(v.tensor_tensor(wgt[:, 3, :], wgt[:, 1, :], wgt[:, 2, :], ALU.mult))
                    full = [TM, NTA, EXP]
                    for a, buf in ((0, gate), (1, one_hot)):
                        step(v.tensor_tensor(buf[:], eidx[:].unsqueeze(1).to_broadcast(full),
                                             topi[:, :, a:a + 1].to_broadcast(full), ALU.is_equal))
                        step(v.tensor_tensor(buf[:], buf[:], wgt[:, 2 + a, :].unsqueeze(2).to_broadcast(full), ALU.mult))
                    step(v.tensor_tensor(gate[:], gate[:], one_hot[:], ALU.add))
                    split3(step, v, gate[:], [gates[:, :, a * EXP:a * EXP + EXP] for a in range(3)], one_hot[:])

        with ExitStack() as c3:
            def sb3(name, shape, dt):
                return c3.enter_context(nc.sbuf_tensor(name, shape, dt))

            def bank(name):
                return c3.enter_context(nc.psum_tensor(name, [P, 512], F32))

            def sem3(name):
                return c3.enter_context(nc.semaphore(name))

            y_tm = sb3("y_token_major", [TM, NTA, C], F32)
            gst = sb3("gate_chunk", [TM, 4, 3 * EXP], BF16)
            gT = [sb3(f"gates_T{i}", [3 * EXP, CH], BF16) for i in range(2)]
            hid = sb3("hidden_relu", [FF, 2, CH], F32)
            hg = sb3("hidden_gated", [FF, 4, CH], F32)
            zs = sb3("expert_sums", [P, CH], F32)
            sq = [sb3(f"squares{n}", [TM, 4, C], F32) for n in range(2)]
            stat = [sb3(f"stats{n}", [TM, 5, 4], F32) for n in range(2)]
            eps = sb3("eps", [TM, 1], F32)
            p_hid = [bank("p_hid0"), bank("p_hid1")]
            p_gb = [bank("p_gb0"), bank("p_gb1")]
            p_out = bank("p_out")
            p_z = bank("p_z")
            p_gt = c3.enter_context(nc.psum_tensor("p_gt", [P, 1024], BF16))
            staged = sem3("gate_chunk_ready")
            gflip = sem3("gates_flipped")
            g_rdy = sem3("gates_T_ready")
            h_sum = sem3("hid_summed")
            h_rdy = sem3("hid_ready")
            b_sum = sem3("gate_spread")
            hg_rdy = sem3("hid_gated")
            hg_used = sem3("hid_gated_used")
            z_rdy = sem3("expert_out_ready")
            z_sum = sem3("folded")
            y_rdy = sem3("y_ready")
            eps_set = sem3("eps_set")
            centre = [sem3(f"norm{n}_centre_step") for n in range(2)]
            squared = [sem3(f"norm{n}_squared") for n in range(2)]
            summed = [sem3(f"norm{n}_summed") for n in range(2)]
            rooted = [sem3(f"norm{n}_rooted") for n in range(2)]
            scale = [sem3(f"norm{n}_scale_step") for n in range(2)]
            affine = sem3("affine_step")
            out_done = sem3("out_stored")

            def tiles(it):
                return bass.ds(it * 4, 4)

            def spread(column):
                return column.unsqueeze(2).to_broadcast([TM, 4, C])

            with nc.Block() as block:
                @block.gpsimd
                def _(pool):
                    full = [TM, 4, C]

                    def stage_gates(it):
                        pool.wait_ge(gflip, it + 1)
                        nc.gpsimd.tensor_copy(gst[:], gates[:, tiles(it), :]).then_inc(staged, 1)

                    def affine_and_residual(it):
                        y = y_tm[:, tiles(it), :]
                        pool.wait_ge(scale[0], it * 2 + 2)
                        tt = nc.gpsimd.tensor_tensor
                        tt(y, y, gamma[:].unsqueeze(1).to_broadcast(full), ALU.mult).then_inc(affine, 1)
                        pool.wait_ge(affine, it * 3 + 1)
                        pool.sem_inc(carrier, 1)
                        tt(y, y, beta[:].unsqueeze(1).to_broadcast(full), ALU.add).then_inc(affine, 1)
                        pool.wait_ge(affine, it * 3 + 2)
                        tt(y, y, x_tm[:, tiles(it), :], ALU.add).then_inc(affine, 1)

                    stage_gates(0)
                    stage_gates(1)
                    with pool.Fori(2, CHUNKS) as it:
                        stage_gates(it)
                        affine_and_residual(it - 2)
                    affine_and_residual(CHUNKS - 2)
                    affine_and_residual(CHUNKS - 1)

                @block.sync
                def _(sp):
                    for it in range(CHUNKS):
                        sp.wait_ge(scale[1], it * 2 + 2)
                        b, c = it // NCH, it % NCH
                        sp.dma_start(k.out[b, c * CH:c * CH + CH, :].rearrange("(t p) c -> p t c", p=TM),
                                     y_tm[:, it * 4:it * 4 + 4, :]).then_inc(out_done, 16)
                    sp.wait_ge(out_done, 16 * CHUNKS)

                @block.tensor
                def _(pe):
                    pe.sem_inc(gflip, 1)
                    pe.sem_inc(hg_used, 1)
                    pe.sem_inc(z_sum, 1)
                    mm = nc.tensor.matmul

                    def flip_gates(it):
                        pe.wait_ge(g_rdy, it + 1)
                        pe.wait_ge(staged, it + 1)
                        pe.sem_inc(carrier, 1)
                        for j in range(4):
                            m = nc.tensor.transpose(p_gt[0:3 * EXP, j * TM:j * TM + TM], gst[:, j, :],
                                                    k.ident_bf[0:TM, 0:TM])
                        m.then_inc(gflip, 1)

                    def first(it, i, e):
                        at = bass.ds(it * CH, CH)
                        pe.wait_ge(h_rdy, it * EXP + e - (1 if e else 0) + 1)
                        for a, xs in enumerate((x_hm, x_hm, x_hl)):
                            m = mm(p_hid[e % 2][:, 0:CH], w1l[:, a, e, :], xs[:, at], start=(a == 0), stop=(a == 2))
                        m.then_inc(h_sum, 1)
                        if e == 0:
                            pe.wait_ge(g_rdy, it + 2)
                        pe.wait_ge(hg_rdy, it * EXP + e - (1 if e else 0) + 1)
                        mm(p_gb[e % 2][:, 0:CH], sel[:, e, :], gT[i][:], start=True, stop=True).then_inc(b_sum, 1)

                    def biases(it, i):
                        pe.wait_ge(z_rdy, it + 1)
                        pe.sem_inc(carrier, 1)
                        mm(p_out[:, 0:CH], b2l[:, 0:2, :].rearrange("g a c -> g (a c)"), gT[i][:], start=True, stop=False)
                        mm(p_out[0:C, 0:CH], b2l[:, 2, :], gT[i][:], start=False, stop=False)

                    def second(it, e):
                        pe.wait_ge(hg_rdy, it * EXP + e + 3)
                        for o in range(2):
                            mm(p_out[o * C:o * C + C, 0:CH], w2f[:, e + o, :], hg[:, (e + o) % 4, :],
                               start=False, stop=(e >= EXP - 2)).then_inc(hg_used, 1)

                    def fold_halves(it):
                        pe.wait_ge(z_rdy, it + 2)
                        pe.wait_ge(y_rdy, it + 1)
                        for j in range(4):
                            m = mm(p_z[0:TM, j * C:j * C + C], zs[:, j * TM:j * TM + TM], fold[:], start=True, stop=True)
                        m.then_inc(z_sum, 1)

                    def chunk(it, i, has_prev, has_next):
                        for e in range(0, EXP, 2):
                            if e + 2 < EXP:
                                first(it, i, e + 2)
                                first(it, i, e + 3)
                            elif has_next:
                                first(it + 1, 1 - i, 0)
                                first(it + 1, 1 - i, 1)
                            if e == 0:
                                biases(it, i)
                            second(it, e)
                            if e == 2 and has_prev:
                                fold_halves(it - 1)
                            if e == 8 and has_next:
                                flip_gates(it + 1)

                    flip_gates(0)
                    first(0, 0, 0)
                    first(0, 0, 1)
                    chunk(0, 0, False, True)
                    with pe.Fori(0, CHUNKS // 2 - 1) as it2:
                        chunk(it2 * 2 + 1, 1, True, True)
                        chunk(it2 * 2 + 2, 0, True, True)
                    chunk(CHUNKS - 1, 1, True, False)
                    fold_halves(CHUNKS - 1)

                @block.scalar
                def _(act):
                    act.sem_inc(g_rdy, 1)
                    act.sem_inc(h_rdy, 1)
                    act.sem_inc(z_rdy, 1)
                    a = nc.scalar.activation
                    act.wait_ge(eps_set, 1)

                    def take_gates(it, i):
                        act.wait_ge(gflip, it + 2)
                        act.wait_ge(hg_used, (it - 1) * EXP + 1 if not isinstance(it, int) else max(0, it - 1) * EXP + 1)
                        a(gT[i][:], p_gt[0:3 * EXP, 0:CH], ACT.Identity).then_inc(g_rdy, 1)

                    def relu(it, e):
                        act.wait_ge(h_sum, it * EXP + e + 1)
                        act.wait_ge(hg_rdy, it * EXP + e - (1 if e else 0) + 1)
                        a(hid[:, e % 2, :], p_hid[e % 2][:, 0:CH], ACT.Relu, bias=b1t[:, e:e + 1]).then_inc(h_rdy, 1)

                    def take_sums(it):
                        act.wait_ge(hg_used, it * EXP + EXP + 1)
                        act.wait_ge(z_sum, it + 1)
                        a(zs[:], p_out[:, 0:CH], ACT.Identity).then_inc(z_rdy, 1)

                    def square(n, it):
                        act.wait_ge(centre[n], it * 3 + 3)
                        act.sem_inc(carrier, 1)
                        a(sq[n][:], y_tm[:, tiles(it), :], ACT.Square).then_inc(squared[n], 1)

                    def root(n, it):
                        act.wait_ge(summed[n], it + 1)
                        a(stat[n][:, 3, :], stat[n][:, 2, :], ACT.Sqrt, bias=eps[:], scale=1.0 / C).then_inc(rooted[n], 1)

                    def chunk(it, i, prev, prev2, has_next):
                        for e in range(EXP):
                            relu(it, e)
                            if e == 1 and prev:
                                take_sums(it - 1)
                            if e == 4 and prev2:
                                square(1, it - 2)
                            if e == 7 and prev2:
                                root(1, it - 2)
                            if e == 11 and prev:
                                square(0, it - 1)
                            if e == 13 and prev:
                                root(0, it - 1)
                            if e == 11 and has_next:
                                take_gates(it + 1, 1 - i)

                    take_gates(0, 0)
                    chunk(0, 0, False, False, True)
                    chunk(1, 1, True, False, True)
                    with act.Fori(1, CHUNKS // 2 - 1) as it2:
                        chunk(it2 * 2, 0, True, True, True)
                        chunk(it2 * 2 + 1, 1, True, True, True)
                    chunk(CHUNKS - 2, 0, True, True, True)
                    chunk(CHUNKS - 1, 1, True, True, False)
                    take_sums(CHUNKS - 1)
                    square(1, CHUNKS - 2)
                    root(1, CHUNKS - 2)
                    for n in range(2):
                        square(n, CHUNKS - 1)
                        root(n, CHUNKS - 1)

                @block.vector
                def _(dve):
                    dve.sem_inc(hg_rdy, 1)
                    dve.sem_inc(y_rdy, 1)
                    v = nc.vector
                    v.memset(eps[:], EPS).then_inc(eps_set, 1)

                    def gate_hidden(it, e):
                        dve.wait_ge(h_rdy, it * EXP + e + 2)
                        dve.wait_ge(b_sum, it * EXP + e + 1)
                        dve.wait_ge(hg_used, it * EXP + max(0, e - 3) + 1)
                        v.tensor_tensor(hg[:, e % 4, :], p_gb[e % 2][:, 0:CH], hid[:, e % 2, :],
                                        ALU.mult).then_inc(hg_rdy, 1)

                    def add_residual(it):
                        dve.wait_ge(z_sum, it + 2)
                        v.tensor_tensor(y_tm[:, tiles(it), :], x_tm[:, tiles(it), :],
                                        p_z[0:TM, 0:4 * C].rearrange("p (t c) -> p t c", c=C), ALU.add).then_inc(y_rdy, 1)

                    def total(n, it):
                        if n == 0:
                            dve.wait_ge(y_rdy, it + 2)
                        else:
                            dve.wait_ge(affine, it * 3 + 3)
                        dve.sem_inc(carrier, 1)
                        v.tensor_reduce(stat[n][:, 0, :], y_tm[:, tiles(it), :], AX.X, ALU.add).then_inc(centre[n], 1)

                    def mean(n, it):
                        dve.wait_ge(centre[n], it * 3 + 1)
                        v.tensor_scalar(stat[n][:, 1, :], stat[n][:, 0, :], 1.0 / C, None, ALU.mult).then_inc(centre[n], 1)

                    def subtract_mean(n, it):
                        dve.wait_ge(centre[n], it * 3 + 2)
                        y = y_tm[:, tiles(it), :]
                        v.tensor_tensor(y, y, spread(stat[n][:, 1, :]), ALU.subtract).then_inc(centre[n], 1)

                    def total_squares(n, it):
                        dve.wait_ge(squared[n], it + 1)
                        v.tensor_reduce(stat[n][:, 2, :], sq[n][:], AX.X, ALU.add).then_inc(summed[n], 1)

                    def reciprocal(n, it):
                        dve.wait_ge(rooted[n], it + 1)
                        v.reciprocal(stat[n][:, 4, :], stat[n][:, 3, :]).then_inc(scale[n], 1)

                    def multiply(n, it):
                        dve.wait_ge(scale[n], it * 2 + 1)
                        y = y_tm[:, tiles(it), :]
                        v.tensor_tensor(y, y, spread(stat[n][:, 4, :]), ALU.mult).then_inc(scale[n], 1)

                    def chunk(it, prev, prev2):
                        for e in range(EXP):
                            gate_hidden(it, e)
                            if prev2:
                                if e == 0:
                                    total(1, it - 2)
                                if e == 1:
                                    mean(1, it - 2)
                                if e == 2:
                                    subtract_mean(1, it - 2)
                                if e == 5:
                                    total_squares(1, it - 2)
                                if e == 8:
                                    reciprocal(1, it - 2)
                                if e == 9:
                                    multiply(1, it - 2)
                            if prev:
                                if e == 6:
                                    add_residual(it - 1)
                                if e == 7:
                                    total(0, it - 1)
                                if e == 8:
                                    mean(0, it - 1)
                                if e == 10:
                                    subtract_mean(0, it - 1)
                                if e == 12:
                                    total_squares(0, it - 1)
                                if e == 14:
                                    reciprocal(0, it - 1)
                                if e == 15:
                                    multiply(0, it - 1)

                    chunk(0, False, False)
                    chunk(1, True, False)
                    with dve.Fori(2, CHUNKS) as it:
                        chunk(it, True, True)
                    def last_norm(n, it):
                        total(n, it)
                        mean(n, it)
                        subtract_mean(n, it)
                        total_squares(n, it)
                        reciprocal(n, it)
                        multiply(n, it)

                    last_norm(1, CHUNKS - 2)
                    add_residual(CHUNKS - 1)
                    last_norm(0, CHUNKS - 1)
                    last_norm(1, CHUNKS - 1)




def constants():
    p = np.arange(P)
    weight = np.zeros((P, 2), np.float32)
    weight[p, p % 2] = np.exp2(p - 64.0)
    select = np.zeros((3, EXP, EXP, FF), np.float32)
    for e in range(EXP):
        select[:, e, e, :] = 1.0
    bf16 = mybir.dt.np(BF16)
    return {
        "c_ident": np.eye(P, dtype=np.float32),
        "c_index": np.tile(np.arange(P, dtype=np.float32), (P, 1)),
        "c_weight": weight,
        "c_head_sum": np.kron(np.eye(H), np.ones((HD, HD))).astype(np.float32),
        "c_ones": np.ones((3, NP), bf16),
        "c_select": select.reshape(3 * EXP, EXP, FF).astype(bf16),
    }


def build(nc, io, out):
    with ExitStack() as ctx:
        k = Core(nc, io, out, ctx)
        setup_phase(k)
        tok_phase(k)
        with ExitStack() as staging:
            k.stage = Stage(k, staging, "stage", 2)
            maximum_phase(k)
            attention_phase(k)
        project_phase(k)
        moe_phase(k)


def kernel(**inputs):
    import concourse.bacc as bacc
    from concourse.bass_utils import run_bass_kernel_spmd

    nc = bacc.Bacc("TRN2", target_bir_lowering=False, num_devices=1)
    arrays, io = {}, {}
    for name, a in {**inputs, **constants()}.items():
        a = np.ascontiguousarray(a)
        arrays[f"in_{name}"] = a
        io[name] = nc.dram_tensor(f"in_{name}", a.shape, mybir.dt.from_np(a.dtype), kind="ExternalInput").ap()
    out = nc.dram_tensor("out_0", (B, N, C), F32, kind="ExternalOutput").ap()
    build(nc, io, out)
    r = run_bass_kernel_spmd(nc, [arrays], core_ids=[0])
    return r.results[0]["out_0"]
```
